# Optimizing a Trainium2 kernel written in Bass

```python
import numpy as np
import jax
import jax.numpy as jnp

def _softmax(x, axis=-1):
    return jax.nn.softmax(x, axis=axis)

def _gelu(x):
    return jax.nn.gelu(x, approximate=True)

def _silu(x):
    return jax.nn.silu(x)

def _sigmoid(x):
    return jax.nn.sigmoid(x)

def _layernorm(x, axis=-1, eps=1e-05):
    m = jnp.mean(x, axis=axis, keepdims=True)
    v = jnp.var(x, axis=axis, keepdims=True)
    return (x - m) / jnp.sqrt(v + eps)

def _scatter_add(tgt, idx, src, axis=0):
    return tgt.at[idx].add(src)

def _segment_sum(src, seg, n):
    return jax.ops.segment_sum(src, seg, n)
kernel_name = 'mk_gnn_ffn_d1_gnn_r8_e13afb'

def setup_inputs(seed: int=0):
    np.random.seed(seed)
    _w = jnp.asarray

    def _rec_inputs():
        import jax
        import jax.numpy as jnp
        _gk = jax.random.key(seed)
        x = -0.0001126 + 1 * jax.random.normal(jax.random.fold_in(_gk, 1), (3750, 256), jnp.float32)
        _s = jax.random.randint(jax.random.fold_in(_gk, 2), (60000,), 0, 3750, jnp.int32)
        _d = jax.random.randint(jax.random.fold_in(_gk, 3), (60000,), 0, 3750, jnp.int32)
        _loop = jnp.arange(3750, dtype=jnp.int32)
        src = jnp.concatenate([_s, _d, _loop])
        dst = jnp.concatenate([_d, _s, _loop])
        _o = jnp.argsort(dst, stable=True)
        src = src[_o]
        dst = dst[_o]
        edge_type_8 = jax.random.randint(jax.random.fold_in(_gk, 12), (123750,), 0, 8, jnp.int32)
        return (x, src, dst, edge_type_8)
    x, src, dst, edge_type_8 = _rec_inputs()

    def _L0_gnn_setup():
        import jax, jax.numpy as jnp
        import numpy as np
        N_NODES = 3750
        N_EDGES = 60000
        IN_FEAT = 256
        OUT_FEAT = 256
        N_RELS = 8
        N_HEADS = 4
        HEAD_DIM = OUT_FEAT // N_HEADS
        LEAKY_SLOPE = 0.2
        key = jax.random.key(seed)
        ks = jax.random.split(key, 8)
        inputs = jax.random.normal(ks[0], (N_NODES, IN_FEAT), dtype=jnp.float32)
        conv_weights = jax.random.normal(ks[1], (N_RELS, N_HEADS, IN_FEAT, HEAD_DIM), dtype=jnp.float32) * (1.0 / np.sqrt(IN_FEAT))
        attn_l = jax.random.normal(ks[2], (N_RELS, N_HEADS, HEAD_DIM), dtype=jnp.float32) * 0.1
        attn_r = jax.random.normal(ks[3], (N_RELS, N_HEADS, HEAD_DIM), dtype=jnp.float32) * 0.1
        h_bias = jax.random.normal(ks[4], (OUT_FEAT,), dtype=jnp.float32) * 0.02
        edge_src = jax.random.randint(ks[5], (N_EDGES,), 0, N_NODES, dtype=jnp.int32)
        edge_dst = jax.random.randint(ks[6], (N_EDGES,), 0, N_NODES, dtype=jnp.int32)
        edge_type = jax.random.randint(ks[7], (N_EDGES,), 0, N_RELS, dtype=jnp.int32)
        return {'inputs': inputs, 'conv_weights': conv_weights, 'attn_l': attn_l, 'attn_r': attn_r, 'h_bias': h_bias, 'edge_src': edge_src, 'edge_dst': edge_dst, 'edge_type': edge_type}
    _L0_gnn_all = _L0_gnn_setup()
    _L0_gnn_in = {k: v for k, v in _L0_gnn_all.items() if k in ('conv_weights', 'attn_l', 'attn_r', 'h_bias')}
    del _L0_gnn_all

    def _L0_ffn_setup():
        import jax, jax.numpy as jnp
        import numpy as np
        B, T, D, H, E = (16, 512, 256, 512, 8)
        key = jax.random.key(seed)
        ks = jax.random.split(key, 5)
        x = jax.random.normal(ks[0], (B, T, D), dtype=jnp.float32)
        gate_w = jax.random.normal(ks[1], (D, E), dtype=jnp.float32) * 0.02
        gate_b = jnp.zeros((E,), dtype=jnp.float32)
        W1 = jax.random.normal(ks[2], (E, D, H), dtype=jnp.float32) * 0.02
        b1 = jnp.zeros((E, H), dtype=jnp.float32)
        W2 = jax.random.normal(ks[3], (E, H, D), dtype=jnp.float32) * 0.02
        b2 = jnp.zeros((E, D), dtype=jnp.float32)
        return {'x': x, 'gate_w': gate_w, 'gate_b': gate_b, 'W1': W1, 'b1': b1, 'W2': W2, 'b2': b2}
    _L0_ffn_all = _L0_ffn_setup()
    _L0_ffn_in = {k: v for k, v in _L0_ffn_all.items() if k in ('gate_w', 'gate_b', 'W1', 'b1', 'W2', 'b2')}
    del _L0_ffn_all
    return {'x': x, 'src': src, 'dst': dst, 'edge_type_8': edge_type_8, 'L0_gnn_conv_weights': _L0_gnn_in['conv_weights'], 'L0_gnn_attn_l': _L0_gnn_in['attn_l'], 'L0_gnn_attn_r': _L0_gnn_in['attn_r'], 'L0_gnn_h_bias': _L0_gnn_in['h_bias'], 'L0_ffn_gate_w': _L0_ffn_in['gate_w'], 'L0_ffn_gate_b': _L0_ffn_in['gate_b'], 'L0_ffn_W1': _L0_ffn_in['W1'], 'L0_ffn_b1': _L0_ffn_in['b1'], 'L0_ffn_W2': _L0_ffn_in['W2'], 'L0_ffn_b2': _L0_ffn_in['b2']}

def reference(x, src, dst, edge_type_8, L0_gnn_conv_weights, L0_gnn_attn_l, L0_gnn_attn_r, L0_gnn_h_bias, L0_ffn_gate_w, L0_ffn_gate_b, L0_ffn_W1, L0_ffn_b1, L0_ffn_W2, L0_ffn_b2):
    import jax
    import jax.numpy as jnp

    def _L0_gnn_ref(inputs, conv_weights, attn_l, attn_r, h_bias, edge_src, edge_dst, edge_type):
        import jax, jax.numpy as jnp
        import numpy as np
        N_NODES = 3750
        N_EDGES = 60000
        IN_FEAT = 256
        OUT_FEAT = 256
        N_RELS = 8
        N_HEADS = 4
        HEAD_DIM = OUT_FEAT // N_HEADS
        LEAKY_SLOPE = 0.2
        feat_all = jnp.einsum('ni,rhid->rnhd', inputs, conv_weights)
        feat_src_e = feat_all[edge_type, edge_src]
        feat_dst_e = feat_all[edge_type, edge_dst]
        el = jnp.sum(feat_src_e * attn_l[edge_type], axis=-1)
        er = jnp.sum(feat_dst_e * attn_r[edge_type], axis=-1)
        e = jax.nn.leaky_relu(el + er, negative_slope=LEAKY_SLOPE)
        m = jax.ops.segment_max(e, edge_dst, num_segments=N_NODES)
        ex = jnp.exp(e - m[edge_dst])
        denom = jax.ops.segment_sum(ex, edge_dst, num_segments=N_NODES)
        alpha = ex / denom[edge_dst]
        h = jax.ops.segment_sum(alpha[..., None] * feat_src_e, edge_dst, num_segments=N_NODES)
        h = h.reshape(N_NODES, OUT_FEAT) + h_bias
        return h

    def _L0_ffn_ref(x, gate_w, gate_b, W1, b1, W2, b2):
        import jax, jax.numpy as jnp
        import numpy as np
        B, T, D, H, E = (16, 512, 256, 512, 8)
        Bb, Tt, Dd = x.shape
        Ee = gate_w.shape[1]
        xf = x.reshape(-1, Dd)
        N = xf.shape[0]
        logits = xf @ gate_w + gate_b
        probs = jax.nn.softmax(logits, axis=-1)
        top2_vals, top2_idx = jax.lax.top_k(probs, 2)
        cw = jnp.zeros((N, Ee), dtype=xf.dtype).at[jnp.arange(N)[:, None], top2_idx].add(top2_vals)

        def step(acc, params):
            w1, bb1, w2, bb2, we = params
            h = jax.nn.gelu(xf @ w1 + bb1, approximate=False)
            y = h @ w2 + bb2
            return (acc + we[:, None] * y, None)
        out, _ = jax.lax.scan(step, jnp.zeros_like(xf), (W1, b1, W2, b2, cw.T))
        return out.reshape(Bb, Tt, Dd)
    x = x + _L0_gnn_ref(_layernorm(x, axis=-1), L0_gnn_conv_weights, L0_gnn_attn_l, L0_gnn_attn_r, L0_gnn_h_bias, src, dst, edge_type_8)
    x = x + _L0_ffn_ref(_layernorm(x, axis=-1)[None], L0_ffn_gate_w, L0_ffn_gate_b, L0_ffn_W1, L0_ffn_b1, L0_ffn_W2, L0_ffn_b2)[0]
    return x

_drawn_inputs = setup_inputs


def setup_inputs(seed=0):
    import zlib

    import numpy as np

    out = dict(_drawn_inputs(seed))
    spreads = {'L0_ffn_gate_b': (0.0, 0.432), 'L0_ffn_b1': (0.0, 0.8), 'L0_ffn_b2': (0.0, 0.323)}
    factors = {'L0_gnn_h_bias': 2.984, 'L0_ffn_W1': 2.937, 'L0_ffn_W2': 2.762}
    for name, (base, spread) in spreads.items():
        noise = np.random.default_rng([zlib.crc32(name.encode()), seed]).standard_normal(out[name].shape)
        drawn = base * np.exp(spread * noise) if base else spread * noise
        out[name] = jnp.asarray(drawn.astype(out[name].dtype))
    for name, factor in factors.items():
        out[name] = (out[name] * factor).astype(out[name].dtype)
    return out
```

```python
from contextlib import ExitStack

import concourse.bass as bass
from concourse import mybir

ALU = mybir.AluOpType
ACT = mybir.ActivationFunctionType
F32 = mybir.dt.float32
I32 = mybir.dt.int32
U32 = mybir.dt.uint32
AX_X = mybir.AxisListType.X

P = 128
SLOTS = 8
STATIC = 4
CHUNK = 64
RING = 6
BIN = 63
SEARCH = 198
MASKED = -1.0e30
EPS = 1e-5
SLOPE = 0.2


class Steps:

    def __init__(self, eng, sem, base=0):
        self.eng, self.sem, self.base, self.n = eng, sem, base, 0

    def did(self, ins):
        ins.then_inc(self.sem, 1)
        self.n += 1

    def wait(self, back=0):
        if self.n - back > 0 or not isinstance(self.base, int):
            self.eng.wait_ge(self.sem, self.base + (self.n - back))


def bc(ap, axis, n):
    ap = ap.unsqueeze(axis)
    shape = list(ap.shape)
    shape[axis] = n
    return ap.to_broadcast(shape)


def rsqrt_steps(nc, st, y, v, tmp):
    st.did(nc.vector.tensor_scalar(tmp.bitcast(I32), v.bitcast(I32), 1, None, ALU.logical_shift_right))
    st.wait()
    st.did(nc.vector.tensor_scalar(y.bitcast(I32), tmp.bitcast(I32), -1.0, 1597463007.0, ALU.mult, ALU.add))
    st.wait()
    for _ in range(3):
        st.did(nc.vector.tensor_tensor(tmp, y, y, ALU.mult))
        st.wait()
        st.did(nc.vector.tensor_tensor(tmp, tmp, v, ALU.mult))
        st.wait()
        st.did(nc.vector.tensor_scalar(tmp, tmp, -0.5, 1.5, ALU.mult, ALU.add))
        st.wait()
        st.did(nc.vector.tensor_tensor(y, y, tmp, ALU.mult))
        st.wait()


def shift_steps(nc, st, out, block, diff, half, bits, width):
    src, bufs = block, (half, block, out)
    for i, by in enumerate((4, 2, 1)):
        n = width + by - 1
        dst = bufs[i][:, :, 0:n]
        st.did(nc.vector.tensor_tensor(diff[:, :, 0:n], src[:, :, by:by + n], src[:, :, 0:n], ALU.subtract))
        st.wait()
        st.did(nc.vector.tensor_tensor(diff[:, :, 0:n], diff[:, :, 0:n], bc(bits[i], 2, n), ALU.mult))
        st.wait()
        st.did(nc.vector.tensor_tensor(dst, diff[:, :, 0:n], src[:, :, 0:n], ALU.add))
        st.wait()
        src = bufs[i]


def build(nc, x, src, dst, etype, conv, attn_l, attn_r, h_bias, gate_w, gate_b, W1, b1, W2, b2, out):
    N, D = x.shape
    E = src.shape[0]
    R, H, _, HD = conv.shape
    NE, _, HID = W1.shape
    KD, KH = D // P, HID // P
    HC = HD + 1
    AGG = H * HC
    ROW = AGG + H
    TN = 125
    T = N // TN
    J = N // TN
    EJ = E // TN
    W = -(-N // P)
    LAST = N - (W - 1) * P
    NF = E // SEARCH
    BW = CHUNK + SLOTS
    NB = E // SLOTS + 2
    NB += -NB % 16
    GN = NB * SLOTS + BW
    NBINS = BIN + 1
    assert TN * T == N and TN * EJ == E and EJ % SEARCH == 0 and D == H * HD and R * H == 32

    table = nc.dram_tensor("table", (N * R, ROW), F32).ap()
    node_tab = nc.dram_tensor("node_tab", (N, D + R * H), F32).ap()
    first_d = nc.dram_tensor("first_d", (NF,), F32).ap()
    edge_row = nc.dram_tensor("edge_row", (GN,), F32)
    blocks = nc.dram_tensor("blocks", (NB, BW), F32).ap()
    start_d = nc.dram_tensor("start_d", (N + 1,), F32).ap()
    ranked = nc.dram_tensor("ranked", (W * P, 4), I32).ap()
    nb_d = nc.dram_tensor("nb_d", (W,), I32).ap()

    ctx = ExitStack()

    def sem(name):
        return ctx.enter_context(nc.semaphore(name))

    with ctx:
        def sb(name, shape, dt=F32, stack=ctx):
            return stack.enter_context(nc.sbuf_tensor(name, shape, dt))

        ident = sb("ident", [P, P])
        idx_all = sb("idx_all", [P, W, CHUNK], U32)
        typ_all = sb("typ_all", [P, W, CHUNK])
        rank_sb = sb("rank_sb", [P, W, 4], I32)
        nb_row = sb("nb_row", [1, W], I32)
        slot_id = sb("slot_id", [P, CHUNK])

        phase1(nc, sb, sem, locals())
        phase2(nc, sb, sem, locals())


def phase1(nc, sb, sem, env):
    (x, src, dst, etype, conv, attn_l, attn_r, h_bias, table, node_tab, first_d, edge_row, blocks, start_d,
     ranked, nb_d, ident, idx_all, typ_all, rank_sb, nb_row, slot_id) = (env[k] for k in (
         "x", "src", "dst", "etype", "conv", "attn_l", "attn_r", "h_bias", "table", "node_tab", "first_d",
         "edge_row", "blocks", "start_d", "ranked", "nb_d", "ident", "idx_all", "typ_all", "rank_sb", "nb_row",
         "slot_id"))
    N, D, E, R, H, HD, KD, HC, AGG, ROW, TN, T, J, EJ, W, NF, BW, NB, GN, NBINS = (env[k] for k in (
        "N", "D", "E", "R", "H", "HD", "KD", "HC", "AGG", "ROW", "TN", "T", "J", "EJ", "W", "NF", "BW", "NB", "GN",
        "NBINS"))
    RH = R * H
    FEAT = R * D
    BANK = 512
    FB = FEAT // BANK
    RB = BANK // D
    GT = 10
    SPLIT = 16
    PAD = W * P - N

    ctx = ExitStack()
    with ctx:
        def t(name, shape, dt=F32):
            return sb(name, shape, dt, ctx)

        x_all = t("x_all", [TN, T, D])
        xn = [t(f"xn{i}", [TN, D]) for i in range(2)]
        xnT = [t(f"xnT{i}", [P, KD, TN]) for i in range(2)]
        wc = t("wc", [P, KD, FEAT])
        attnb = t("attnb", [P, 2, FEAT])
        wa = t("wa", [P, KD, 2 * RH])
        scratch = t("scratch", [P, FEAT])
        hb = t("hb", [TN, D])
        stage = [t(f"stage{i}", [TN, R, ROW]) for i in range(2)]
        er_all = t("er_all", [TN, T, RH])
        stats = t("stats", [TN, T, 6])
        mv = t("mv", [TN, T, 2])
        var = t("var", [TN, T])
        rstd = t("rstd", [TN, T])
        nmr = t("nmr", [TN, T])
        tmpT = t("tmpT", [TN, T])
        dst_sb = t("dst_sb", [TN, EJ], I32)
        src_sb = t("src_sb", [TN, EJ], I32)
        typ_sb = t("typ_sb", [TN, EJ], I32)
        erow = t("erow", [TN, EJ])
        firsts = t("firsts", [TN, EJ // SEARCH])
        first_b = t("first_b", [TN, NF])
        seek = t("seek", [TN, NF])
        node_i = t("node_i", [TN, J], I32)
        node_f = t("node_f", [TN, J])
        cnt = t("cnt", [TN, J])
        chunk_u = t("chunk_u", [TN, J], U32)
        inner = t("inner", [TN, J])
        start = t("start", [TN, J])
        start_n = t("start_n", [TN, J])
        deg = t("deg", [TN, J])
        edges_end = t("edges_end", [1, 1])
        bin_i = t("bin_i", [TN, NBINS], I32)
        bin_f = t("bin_f", [TN, NBINS])
        slot_i = t("slot_i", [P, CHUNK], I32)
        hot = scratch[0:TN, 0:NBINS * J].rearrange("p (b j) -> p b j", b=NBINS)
        run = t("run", [TN, NBINS, J])
        ones = t("ones", [TN, NBINS * J])
        bin_cnt = t("bin_cnt", [TN, NBINS])
        bin_st = t("bin_st", [TN, NBINS])
        lower = t("lower", [TN, TN])
        rank_f = t("rank_f", [TN, J])
        rank_u = t("rank_u", [TN, J], U32)
        info = t("info", [TN, J, 4], I32)
        zeros = t("zeros", [P, 4], I32)
        blk_u = t("blk_u", [P, W], U32)
        bit_i = t("bit_i", [P, 3, W], I32)
        bit_f = t("bit_f", [P, 3, W])
        wide = t("wide", [P, 3 * W * BW])
        dchunk = wide[0:TN, 0:J * SEARCH].bitcast(I32).rearrange("p (j e) -> p j e", j=J)
        blk, half, diff = (wide[:, i * W * BW:(i + 1) * W * BW].rearrange("p (w k) -> p w k", w=W) for i in range(3))
        zero_f = t("zero_f", [1, GN - E])
        deg_r = t("deg_r", [P, W])
        rank_w = t("rank_w", [W, P, 4], I32)
        mx = t("mx", [W, 1])
        nb_i = t("nb_i", [W, 1], I32)

        feat_ps = [ctx.enter_context(nc.psum_tensor(f"feat_ps{b}", [P, BANK], F32)) for b in range(FB)]
        score_ps = ctx.enter_context(nc.psum_tensor("score_ps", [P, BANK], F32))
        tr_ps = [ctx.enter_context(nc.psum_tensor(f"tr_ps{i}", [P, BANK], F32)) for i in range(2)]
        off_ps = ctx.enter_context(nc.psum_tensor("off_ps", [P, BANK], F32))

        x_in = [sem(f"x_in{g}") for g in range(T // GT)]
        dst_in, et_in, conv_in, attn_in, hb_in = (sem(n) for n in ("dst_in", "et_in", "conv_in", "attn_in", "hb_in"))
        ident0, ident_ok, pool_const, pool_mask = (sem(n) for n in ("ident0", "ident_ok", "pool_const", "pool_mask"))
        firsts_ok, first_out, first_in = sem("firsts_ok"), sem("first_out"), sem("first_in")
        erow_ok, erow_out, blocks_out = sem("erow_ok"), sem("erow_out"), sem("blocks_out")
        norm_ok, xb_ok, node_out = sem("norm_ok"), sem("xb_ok"), sem("node_out")
        ones_ok, wa_ok = sem("ones_ok"), sem("wa_ok")
        chunk_ok, chunk_in = sem("chunk_ok"), [sem(f"chunk_in{g}") for g in range(3)]
        start_ok, start_out, start_in = sem("start_ok"), sem("start_out"), sem("start_in")
        bins_ok, offs_ok, rank_ok = sem("bins_ok"), sem("offs_ok"), sem("rank_ok")
        zero_out, ranked_out, rank_in = sem("zero_out"), sem("ranked_out"), sem("rank_in")
        blk_ok, blk_in, nb_ok, nb_out, nb_in = (sem(n) for n in ("blk_ok", "blk_in", "nb_ok", "nb_out", "nb_in"))
        xn_ok, tr_ok, xnT_ok = sem("xn_ok"), sem("tr_ok"), sem("xnT_ok")
        feat_ok, score_ok = sem("feat_ok"), sem("score_ok")
        feat_free, score_free = [sem(f"feat_free{b}") for b in range(FB)], sem("score_free")
        stage_ok, stored = sem("stage_ok"), [sem(f"stored{i}") for i in range(2)]
        dstep = sem("dstep1")

        table_v = table.rearrange("(t p r) c -> t p (r c)", t=T, p=TN)
        x_v = x.rearrange("(t p) d -> p t d", p=TN)

        block = ctx.enter_context(nc.Block())

        @block.sync
        def _(sp):
            flat = dict(p=TN)
            sp.dma_start(dst_sb[:], dst.rearrange("(p e) -> p e", **flat)).then_inc(dst_in, 16)
            sp.dma_start(x_all[:, 0:GT, :], x_v[:, 0:GT, :]).then_inc(x_in[0], 16)
            sp.dma_start(src_sb[:], src.rearrange("(p e) -> p e", **flat)).then_inc(et_in, 16)
            sp.dma_start(typ_sb[:], etype.rearrange("(p e) -> p e", **flat)).then_inc(et_in, 16)
            for i, a in enumerate((attn_l, attn_r)):
                sp.dma_start(attnb[:, i, :], a.rearrange("r h d -> (r h d)").partition_broadcast(P)).then_inc(attn_in, 16)
            sp.dma_start(hb[:], h_bias.partition_broadcast(TN)).then_inc(hb_in, 16)
            for g in range(1, T // GT):
                sp.dma_start(x_all[:, g * GT:(g + 1) * GT, :], x_v[:, g * GT:(g + 1) * GT, :]).then_inc(x_in[g], 16)
            sp.wait_ge(firsts_ok, 1)
            sp.dma_start(first_d.rearrange("(p c) -> p c", **flat), firsts[:]).then_inc(first_out, 16)
            sp.wait_ge(first_out, 16)
            sp.dma_start(first_b[:], first_d.partition_broadcast(TN)).then_inc(first_in, 16)
            sp.wait_ge(erow_ok, 1)
            sp.wait_ge(pool_const, 3)
            flat_rows = edge_row.ap()
            sp.dma_start(flat_rows[0:E].rearrange("(p e) -> p e", **flat), erow[:]).then_inc(erow_out, 16)
            sp.dma_start(flat_rows[E:GN].rearrange("(p e) -> p e", p=1), zero_f[:]).then_inc(erow_out, 16)
            sp.wait_ge(erow_out, 32)
            sp.dma_start(blocks, bass.AP(edge_row, 0, [[SLOTS, NB], [1, BW]])).then_inc(blocks_out, 16)
            sp.wait_ge(start_ok, 1)
            sp.dma_start(start_d[0:N].rearrange("(p j) -> p j", **flat), start[:]).then_inc(start_out, 16)
            sp.dma_start(start_d[N:N + 1].rearrange("(p j) -> p j", p=1), edges_end[:]).then_inc(start_out, 16)
            sp.wait_ge(start_out, 32)
            sp.dma_start(start_n[:], start_d[1:N + 1].rearrange("(p j) -> p j", **flat)).then_inc(start_in, 16)
            sp.dma_start(ranked[N:W * P, :], zeros[0:PAD, :]).then_inc(zero_out, 16)
            sp.wait_ge(zero_out, 16)
            sp.wait_ge(ranked_out, 16 * J)
            sp.dma_start(rank_sb[:], ranked.rearrange("(w p) c -> p w c", p=P)).then_inc(rank_in, 16)
            sp.dma_start(rank_w[:], ranked.rearrange("(w p) c -> w p c", p=P)).then_inc(rank_in, 16)
            sp.wait_ge(nb_ok, 1)
            sp.dma_start(nb_d.rearrange("(w o) -> w o", o=1), nb_i[:]).then_inc(nb_out, 16)
            sp.wait_ge(nb_out, 16)
            sp.dma_start(nb_row[:], nb_d.rearrange("(o w) -> o w", o=1)).then_inc(nb_in, 16)
            sp.wait_ge(nb_in, 16)
            sp.wait_ge(blocks_out, 16)
            for g in range(T // GT):
                sp.wait_ge(xb_ok, g + 1)
                sp.dma_start(node_tab.rearrange("(t p) d -> p t d", p=TN)[:, g * GT:(g + 1) * GT, 0:D],
                             x_all[:, g * GT:(g + 1) * GT, :]).then_inc(node_out, 16)
            sp.wait_ge(score_free, T)
            sp.dma_start(node_tab.rearrange("(t p) d -> p t d", p=TN)[:, :, D:D + RH], er_all[:]).then_inc(node_out, 16)
            sp.wait_ge(node_out, 16 * (T // GT + 1))
            for i in range(2):
                sp.wait_ge(stored[i], 16 * (T // 2))

        @block.gpsimd
        def _(pool):
            g = nc.gpsimd
            g.memset(zero_f[:], 0.0).then_inc(pool_const, 1)
            g.memset(zeros[:], 0).then_inc(pool_const, 1)
            g.memset(edges_end[:], float(E)).then_inc(pool_const, 1)
            g.memset(ident[:], 0.0).then_inc(ident0, 1)
            g.memset(lower[:], 1.0).then_inc(ident0, 1)
            pool.wait_ge(ident0, 2)
            g.affine_select(out=ident[:], in_=ident[:], compare_op=ALU.not_equal, fill=1.0, base=0,
                            pattern=[[-1, P]], channel_multiplier=1).then_inc(ident_ok, 1)
            g.affine_select(out=lower[:], in_=lower[:], compare_op=ALU.is_ge, fill=0.0, base=-1,
                            pattern=[[1, TN]], channel_multiplier=-1).then_inc(pool_mask, 1)
            g.iota(node_i[:], pattern=[[1, J]], base=0, channel_multiplier=J).then_inc(pool_const, 1)
            g.iota(bin_i[:], pattern=[[1, NBINS]], base=-BIN, channel_multiplier=0).then_inc(pool_const, 1)
            g.iota(slot_i[:], pattern=[[1, CHUNK]], base=0, channel_multiplier=0).then_inc(pool_const, 1)
            pool.wait_ge(chunk_ok, 1)
            for j in range(J):
                g.indirect_dma_start(dchunk[:, j, :], None, dst.rearrange("(c e) -> c e", e=SEARCH),
                                     bass.IndirectOffsetOnAxis(chunk_u[:, j:j + 1], 0)).then_inc(chunk_in[j // 10], 16)
            pool.wait_ge(rank_ok, 1)
            pool.wait_ge(zero_out, 16)
            for j in range(J):
                g.indirect_dma_start(ranked, bass.IndirectOffsetOnAxis(rank_u[:, j:j + 1], 0), info[:, j, :],
                                     None).then_inc(ranked_out, 16)
            pool.wait_ge(blk_ok, 1)
            pool.wait_ge(blocks_out, 16)
            for w in range(W):
                g.indirect_dma_start(blk[:, w, :], None, blocks,
                                     bass.IndirectOffsetOnAxis(blk_u[:, w:w + 1], 0)).then_inc(blk_in, 16)
            pool.wait_ge(blk_in, 16 * W)

        @block.vector
        def _(dve):
            v = nc.vector
            st = Steps(dve, dstep)

            def go(ins):
                st.did(ins)
                st.wait()

            go(v.memset(ones[:], 1.0))
            for i in range(2):
                for h in range(H):
                    v.memset(stage[i][:, :, h * HC + HD:h * HC + HD + 1], 1.0).then_inc(ones_ok, 1)
            dve.wait_ge(dst_in, 16)
            v.tensor_copy(firsts[:], dst_sb[:].rearrange("p (c e) -> p c e", e=SEARCH)[:, :, 0]).then_inc(firsts_ok, 1)
            dve.wait_ge(et_in, 32)
            v.scalar_tensor_tensor(out=erow[:], in0=src_sb[:], scalar=float(R), in1=typ_sb[:], op0=ALU.mult,
                                   op1=ALU.add).then_inc(erow_ok, 1)

            def norms(g):
                dve.wait_ge(x_in[g], 16)
                for i in range(g * GT, (g + 1) * GT):
                    st.did(v.bn_stats(stats[:, i, :], x_all[:, i, :]))
                st.wait()
                for i in range(g * GT, (g + 1) * GT):
                    st.did(v.bn_aggr(mv[:, i, :], stats[:, i, :]))
                st.wait()
                s = slice(g * GT, (g + 1) * GT)
                go(v.tensor_scalar(var[:, s], mv[:, s, 1], EPS, None, ALU.add))
                rsqrt_steps(nc, st, rstd[:, s], var[:, s], tmpT[:, s])
                v.scalar_tensor_tensor(out=nmr[:, s], in0=mv[:, s, 0], scalar=-1.0, in1=rstd[:, s], op0=ALU.mult,
                                       op1=ALU.mult).then_inc(norm_ok, 1)

            norms(0)
            dve.wait_ge(attn_in, 32)
            dve.wait_ge(conv_in, 16 * R * KD)
            for lr in range(2):
                for k in range(KD):
                    go(v.tensor_tensor(scratch[:], wc[:, k, :], attnb[:, lr, :], ALU.mult))
                    go(v.tensor_reduce(wa[:, k, lr * RH:(lr + 1) * RH],
                                       scratch[:].rearrange("p (a d) -> p a d", d=HD), AX_X, ALU.add))
            dve.sem_inc(wa_ok, 1)
            norms(1)
            norms(2)
            dve.wait_ge(pool_const, 6)
            go(v.tensor_copy(node_f[:], node_i[:]))
            go(v.tensor_copy(bin_f[:], bin_i[:]))
            go(v.tensor_copy(slot_id[:], slot_i[:]))
            dve.wait_ge(first_in, 16)
            for j in range(J):
                st.did(v.tensor_scalar(seek[:], first_b[:], node_f[:, j:j + 1], 0.0, ALU.is_lt, ALU.add,
                                       accum_out=cnt[:, j:j + 1]))
                st.wait()
            go(v.tensor_scalar(cnt[:], cnt[:], -1.0, 0.0, ALU.add, ALU.max))
            v.tensor_copy(chunk_u[:], cnt[:]).then_inc(chunk_ok, 1)
            for j in range(J):
                if j % 10 == 0:
                    dve.wait_ge(chunk_in[j // 10], 160)
                st.did(v.tensor_scalar(seek[:, 0:SEARCH], dchunk[:, j, :], node_f[:, j:j + 1], 0.0, ALU.is_lt,
                                       ALU.add, accum_out=inner[:, j:j + 1]))
                st.wait()
            v.scalar_tensor_tensor(out=start[:], in0=cnt[:], scalar=float(SEARCH), in1=inner[:], op0=ALU.mult,
                                   op1=ALU.add).then_inc(start_ok, 1)
            dve.wait_ge(start_in, 16)
            go(v.tensor_tensor(deg[:], start_n[:], start[:], ALU.subtract))
            go(v.tensor_scalar(tmpT[:], deg[:], float(BIN), -1.0, ALU.min, ALU.mult))
            go(v.tensor_tensor(hot, bc(tmpT[:], 1, NBINS), bc(bin_f[:], 2, J), ALU.is_equal))
            go(v.tensor_tensor_scan(out=run[:].rearrange("p b j -> p (b j)"), data0=ones[:],
                                    data1=hot.rearrange("p b j -> p (b j)"), initial=0.0, op0=ALU.mult,
                                    op1=ALU.add))
            go(v.memset(bin_st[:, 0:1], 0.0))
            go(v.tensor_copy(bin_st[:, 1:NBINS], run[:, 0:BIN, J - 1]))
            v.tensor_tensor(bin_cnt[:], run[:, :, J - 1], bin_st[:], ALU.subtract).then_inc(bins_ok, 1)
            dve.wait_ge(offs_ok, 1)
            go(v.scalar_tensor_tensor(out=bin_cnt[:], in0=off_ps[0:TN, 0:NBINS], scalar=-1.0, in1=bin_st[:],
                                      op0=ALU.add, op1=ALU.subtract))
            go(v.tensor_tensor(run[:], run[:], bc(bin_cnt[:], 2, J), ALU.add))
            go(v.tensor_tensor(run[:], run[:], hot, ALU.mult))
            go(v.tensor_reduce(rank_f[:], run[:].rearrange("p b j -> p j b"), AX_X, ALU.add))
            go(v.tensor_copy(info[:, :, 0], node_f[:]))
            go(v.tensor_copy(info[:, :, 1], start[:]))
            go(v.tensor_copy(info[:, :, 2], deg[:]))
            go(v.memset(info[:, :, 3], 0))
            v.tensor_copy(rank_u[:], rank_f[:]).then_inc(rank_ok, 1)
            dve.wait_ge(hb_in, 16)

            def residual(g):
                dve.wait_ge(xn_ok, (g + 1) * GT)
                s = slice(g * GT, (g + 1) * GT)
                v.tensor_tensor(x_all[:, s, :], x_all[:, s, :], bc(hb[:], 1, GT), ALU.add).then_inc(xb_ok, 1)

            residual(0)
            residual(1)
            dve.wait_ge(rank_in, 32)
            v.tensor_scalar(blk_u[:].bitcast(I32), rank_sb[:, :, 1], 3, None, ALU.logical_shift_right).then_inc(blk_ok, 1)
            go(v.tensor_reduce(mx[:], rank_w[:, :, 2], AX_X, ALU.max))
            go(v.tensor_scalar(nb_i[:], mx[:], float(SLOTS - 1 - SLOTS * STATIC), 0.0, ALU.add, ALU.max))
            v.tensor_scalar(nb_i[:], nb_i[:], 3, None, ALU.logical_shift_right).then_inc(nb_ok, 1)
            for i, by in enumerate((4, 2, 1)):
                go(v.tensor_scalar(bit_i[:, i, :], rank_sb[:, :, 1], by, None, ALU.bitwise_and))
                go(v.tensor_scalar(bit_f[:, i, :], bit_i[:, i, :], 1.0 / by, None, ALU.mult))
            go(v.tensor_copy(deg_r[:], rank_sb[:, :, 2]))
            dve.wait_ge(blk_in, 16 * W)
            shift_steps(nc, st, typ_all[:], blk, diff, half, [bit_f[:, i, :] for i in range(3)], CHUNK)
            go(v.tensor_copy(idx_all[:], typ_all[:]))
            low = half[:, :, 0:CHUNK].bitcast(I32)
            go(v.tensor_scalar(low, idx_all[:].bitcast(I32), R - 1, None, ALU.bitwise_and))
            go(v.tensor_tensor(diff[:, :, 0:CHUNK], bc(slot_id[:], 1, W), bc(deg_r[:], 2, CHUNK), ALU.is_ge))
            go(v.scalar_tensor_tensor(out=typ_all[:], in0=diff[:, :, 0:CHUNK], scalar=float(R), in1=low,
                                      op0=ALU.mult, op1=ALU.add))
            go(v.tensor_scalar(typ_all[:], typ_all[:], float(R), None, ALU.min))
            residual(2)

        @block.scalar
        def _(act):
            a = nc.scalar
            for r in range(R):
                for k in range(KD):
                    act.dma_start(wc[:, k, r * D:(r + 1) * D].rearrange("p (h d) -> p h d", h=H),
                                  conv[r, :, k * P:(k + 1) * P, :].rearrange("h p d -> p h d")).then_inc(conv_in, 16)

            def normalize(i, par):
                act.wait_ge(norm_ok, i // GT + 1)
                a.activation(xn[par][:], x_all[:, bass.ds(i, 1), :].rearrange("p o d -> p (o d)"), ACT.Identity,
                             bias=nmr[:, bass.ds(i, 1)], scale=rstd[:, bass.ds(i, 1)]).then_inc(xn_ok, 1)

            def transposed(i, par):
                act.wait_ge(tr_ok, i + 1)
                if not isinstance(i, int) or i >= 2:
                    act.wait_ge(score_ok, i - 1)
                a.copy(xnT[par][:], tr_ps[par][:, 0:KD * TN].rearrange("p (k n) -> p k n", k=KD)).then_inc(xnT_ok, 1)

            def evacuate(i, par, pair, ahead):
                if ahead > 1:
                    normalize(i + 2, par)
                if not isinstance(i, int) or i >= 2:
                    act.wait_ge(stored[par], 16 * pair)
                for b in range(FB):
                    if b == FB // 2 and ahead > 0:
                        transposed(i + 1, 1 - par)
                    act.wait_ge(feat_ok, i * FB + b + 1)
                    a.copy(stage[par][:, b * RB:(b + 1) * RB, 0:AGG].rearrange("p r (h c) -> p r h c", h=H)[:, :, :, 0:HD],
                           feat_ps[b][0:TN, :].rearrange("p (r h d) -> p r h d", r=RB, h=H)).then_inc(feat_free[b], 1)
                act.wait_ge(score_ok, i + 1)
                a.copy(stage[par][:, :, AGG:ROW],
                       score_ps[0:TN, 0:RH].rearrange("p (r h) -> p r h", r=R)).then_inc(stage_ok, 1)
                a.copy(er_all[:, bass.ds(i, 1), :].rearrange("p o c -> p (o c)"),
                       score_ps[0:TN, RH:2 * RH]).then_inc(score_free, 1)
                act.wait_ge(stage_ok, i + 1)
                for b in range(FB):
                    act.wait_ge(feat_free[b], i + 1)
                act.dma_start(table_v[bass.ds(i, 1)].rearrange("o p c -> (o p) c"),
                              stage[par][:].rearrange("p r c -> p (r c)")).then_inc(stored[par], 16)

            normalize(0, 0)
            normalize(1, 1)
            transposed(0, 0)
            act.wait_ge(ones_ok, 2 * H)
            for par in range(2):
                evacuate(par, par, 0, 2)
            with act.Fori(1, T // 2 - 1) as pair:
                for par in range(2):
                    evacuate(pair * 2 + par, par, pair, 2)
            evacuate(T - 2, 0, T // 2 - 1, 1)
            evacuate(T - 1, 1, T // 2 - 1, 0)

        @block.tensor
        def _(pe):
            m = nc.tensor

            def transposes(i, par):
                pe.wait_ge(xn_ok, i + 1)
                if not isinstance(i, int) or i >= 2:
                    pe.wait_ge(xnT_ok, i - 1)
                for k in range(KD):
                    last = m.transpose(tr_ps[par][:, k * TN:(k + 1) * TN], xn[par][:, k * P:(k + 1) * P],
                                       ident[0:TN, 0:TN])
                last.then_inc(tr_ok, 1)

            def products(i, par, ahead=True):
                pe.wait_ge(xnT_ok, i + 1)
                for b in range(FB):
                    if b == FB // 2 and ahead:
                        transposes(i + 1, 1 - par)
                    if not isinstance(i, int) or i >= 1:
                        pe.wait_ge(feat_free[b], i)
                    for k in range(KD):
                        last = m.matmul(feat_ps[b][0:TN, :], xnT[par][:, k, :], wc[:, k, b * BANK:(b + 1) * BANK],
                                        start=(k == 0), stop=(k == KD - 1))
                    last.then_inc(feat_ok, 1)
                if not isinstance(i, int) or i >= 1:
                    pe.wait_ge(score_free, i)
                pe.wait_ge(wa_ok, 1)
                for k in range(KD):
                    last = m.matmul(score_ps[0:TN, 0:2 * RH], xnT[par][:, k, :], wa[:, k, :], start=(k == 0),
                                    stop=(k == KD - 1))
                last.then_inc(score_ok, 1)

            def tiles(lo, hi):
                with pe.Fori(lo, hi) as pair:
                    for par in range(2):
                        products(pair * 2 + par, par)

            pe.wait_ge(ident_ok, 1)
            transposes(0, 0)
            pe.wait_ge(conv_in, 16 * R * KD)
            products(0, 0)
            products(1, 1)
            tiles(1, SPLIT // 2)
            pe.wait_ge(bins_ok, 1)
            pe.wait_ge(pool_mask, 1)
            m.matmul(off_ps[0:TN, 0:NBINS], lower[:], bin_cnt[:], start=True, stop=False)
            m.matmul(off_ps[0:TN, 0:NBINS], ones[:, 0:TN], bin_st[:], start=False, stop=True).then_inc(offs_ok, 1)
            tiles(SPLIT // 2, T // 2 - 1)
            products(T - 2, 0)
            products(T - 1, 1, ahead=False)


def phase2(nc, sb, sem, env):
    (W1, b1, W2, b2, gate_w, gate_b, out, table, node_tab, blocks, ident, idx_all, typ_all, rank_sb, nb_row,
     slot_id) = (env[k] for k in (
         "W1", "b1", "W2", "b2", "gate_w", "gate_b", "out", "table", "node_tab", "blocks", "ident", "idx_all",
         "typ_all", "rank_sb", "nb_row", "slot_id"))
    N, D, E, R, H, HD, HC, AGG, ROW, W, LAST, BW, NE, HID, KD, KH = (env[k] for k in (
        "N", "D", "E", "R", "H", "HD", "HC", "AGG", "ROW", "W", "LAST", "BW", "NE", "HID", "KD", "KH"))
    RH = R * H
    R1 = R + 1
    S1 = SLOTS + 1
    PAIRS = NE // 2
    assert PAIRS == STATIC and W % 2 == 0

    N_FRONT, N_EX, N_ACC, N_BEGIN, N_POST, N_GATE, N_MIX, N_CHUNK = 7, 2, 2, 5, 22, 11, 1 + NE, 25

    rows = sb("rows", [P, RING, SLOTS, ROW])
    prod = sb("prod", [P, SLOTS, AGG])
    w1 = sb("w1", [P, NE, KD, HID])
    w2 = sb("w2", [P, NE, KH, D])
    b1t = sb("b1t", [P, NE, KH])
    b2s = sb("b2s", [NE, D])
    gw = sb("gw", [P, KD, NE])
    gb = sb("gb", [P, NE])
    idx_st = [sb(f"idx_st{i}", [P, CHUNK + 1], U32) for i in range(2)]
    node_row = [sb(f"node_row{i}", [P, D + RH]) for i in range(2)]
    xo = [sb(f"xo{i}", [P, D]) for i in range(2)]
    oid = [sb(f"oid{i}", [P, 1], U32) for i in range(2)]
    typ_cur = sb("typ_cur", [P, CHUNK])
    er9 = sb("er9", [P, H, R1])
    hot9 = sb("hot9", [P, SLOTS, R1])
    er_hot = sb("er_hot", [P, SLOTS, H, R1])
    score = sb("score", [P, SLOTS, H])
    ebuf = sb("ebuf", [P, H, S1])
    m_new = sb("m_new", [P, H])
    diff = sb("e_diff", [P, H, S1])
    th = sb("th", [P, H, S1])
    den = sb("den", [P, H, S1])
    rden = sb("rden", [P, H, S1])
    ex = sb("ex", [P, H, S1])
    acc = sb("acc", [P, H, HC])
    r4 = sb("r4", [P, H])
    valid = sb("valid", [P, 1])
    hn = sb("hn", [P, D])
    st6 = sb("st6", [P, 6])
    mv2 = sb("mv2", [P, 2])
    varp = sb("varp", [P, 1])
    rstd2 = sb("rstd2", [P, 1])
    tmp1 = sb("tmp1", [P, 1])
    z = sb("z", [P, D])
    zT = sb("zT", [P, KD, P])
    hT = [sb(f"hT{i}", [P, KH, P]) for i in range(2)]
    lg = sb("lg", [P, NE])
    mx8 = sb("mx8", [P, NE])
    ix8 = sb("ix8", [P, NE], U32)
    ixf = sb("ixf", [P, 2])
    nm = sb("nm", [P, 1])
    gth = sb("gth", [P, NE])
    gden = sb("gden", [P, NE])
    gp = sb("gp", [P, NE])
    gsum = sb("gsum", [P, 1])
    gmask = sb("gmask", [P, NE])
    cw = sb("cw", [P, NE])
    cwT = sb("cwT", [NE, P])
    coff = sb("coff", [P, 1])
    xst = sb("xst", [P, 1])
    xst_i = sb("xst_i", [P, 1], I32)
    xblk = sb("xblk", [P, 1], U32)
    xbit_i = sb("xbit_i", [P, 3], I32)
    xbit = sb("xbit", [P, 3, 1])
    xraw = sb("xraw", [P, 1, BW])
    xhalf = sb("xhalf", [P, 1, BW])
    xdiff = sb("xdiff", [P, 1, BW])
    xidx_f = sb("xidx_f", [P, 1, CHUNK])
    xidx = sb("xidx", [P, CHUNK], U32)
    xlow = sb("xlow", [P, CHUNK], I32)
    xdeg = sb("xdeg", [P, 1])
    xmask = sb("xmask", [P, CHUNK])

    def bank(name):
        return env["ctx"].enter_context(nc.psum_tensor(name, [P, 512], F32))

    hid_ps = [bank(f"hid_ps{i}") for i in range(2)]
    y_ps = [bank(f"y_ps{i}") for i in range(2)]
    agg_ps, gate_ps, zt_ps = bank("agg_ps"), bank("gate_ps"), bank("zt_ps")
    b2_ps = zt_ps[:, 256:256 + D]
    cwt_ps = gate_ps[0:NE, 128:256]

    w_in, w_in2, const_in = sem("w_in"), sem("w_in2"), sem("const_in")
    const_ok = sem("const_ok")
    idx_staged = sem("idx_staged")
    row_landed = [sem(f"row_landed{i}") for i in range(RING)]
    rows_ready = sem("rows_ready")
    node_landed = [sem(f"node_landed{i}") for i in range(2)]
    diff_ok, th_ok, den_ok = sem("diff_ok"), sem("th_ok"), sem("den_ok")
    weighted = sem("weighted")
    agg_ok = sem("agg_ok")
    z_ok, ztr_ok, zT_ok = sem("z_ok"), sem("ztr_ok"), sem("zT_ok")
    logit_ok, gate_in, gth_ok, gden_ok, cw_ok, cwt_ok, cwT_ok, b2_ok = (sem(n) for n in (
        "logit_ok", "gate_in", "gth_ok", "gden_ok", "cw_ok", "cwt_ok", "cwT_ok", "b2_ok"))
    hid_ok, gelu_ok, w2_ok, y_used = sem("hid_ok"), sem("gelu_ok"), sem("w2_ok"), sem("y_used")
    out_ok, out_done = sem("out_ok"), [sem(f"out_done{i}") for i in range(2)]
    pool_passed, dve_passed = sem("pool_passed"), sem("dve_passed")
    xblk_ok, xblk_in, xidx_ok = sem("xblk_ok"), sem("xblk_in"), sem("xidx_ok")
    (front_step, ex_step, acc_step, begin_step, post_step, gate_step, mix_step, chunk_step, stage_step) = (
        sem(n) for n in ("front_step", "ex_step", "acc_step", "begin_step", "post_step", "gate_step", "mix_step",
                         "chunk_step", "stage_step"))

    def after(eng, s, value):
        if not isinstance(value, int) or value > 0:
            eng.wait_ge(s, value)

    def windows(eng, window):
        for w in range(2):
            window(w, w, 0)
        with eng.Fori(1, W // 2) as j:
            for par in range(2):
                window(j * 2 + par, par, j)

    def alone(eng, passed):
        eng.sem_inc(passed, 1)

    class Batches:

        def __init__(self, eng, name):
            self.eng = eng
            self.total, self.before = eng.alloc_register(f"{name}_total"), eng.alloc_register(f"{name}_before")
            eng.reg_mov(self.total, 0)
            eng.reg_mov(self.before, 0)

        def enter(self, w):
            nb = self.eng.value_load(nb_row[0:1, bass.ds(w, 1)], min_val=0, max_val=E // SLOTS + 1 - STATIC) + STATIC
            if isinstance(w, int) and w == 0:
                return nb, 0, 0
            g = self.eng.snap(self.total, min_val=STATIC)
            return nb, g, (0 if isinstance(w, int) and w == 1 else self.eng.snap(self.before, min_val=STATIC))

        def leave(self, w, nb, g):
            self.eng.reg_mov(self.before, g)
            self.eng.reg_mov(self.total, nb + g)

    def further_batches(eng, nb, batch, chunk):
        def chain(s, c, left):
            if s == SLOTS:
                return
            with eng.If(left > s):
                batch(s, c * SLOTS + s if not isinstance(c, int) else s, c)
                chain(s + 1, c, left)

        chain(STATIC, 0, nb)
        with eng.If(nb > SLOTS):
            with eng.Fori(1, (nb + (SLOTS - 1)) >> 3) as c:
                chunk(c)
                chain(0, c, nb - c * SLOTS)

    block = env["ctx"].enter_context(nc.Block())

    @block.sync
    def _(sp):
        w1_v = W1.rearrange("e (k p) n -> p e k n", p=P)
        w2_v = W2.rearrange("e (k p) n -> p e k n", p=P)
        for e in range(NE):
            sp.dma_start(w1[:, e], w1_v[:, e]).then_inc(w_in, 16)
            sp.dma_start(w2[:, e], w2_v[:, e]).then_inc(w_in2, 16)
        bt = Batches(sp, "sp")
        uses = [sp.alloc_register(f"uses{i}") for i in range(2)]
        for r in uses:
            sp.reg_mov(r, 0)

        def window(w, par, half):
            nb, g, _ = bt.enter(w)
            for s in range(STATIC):
                sp.wait_ge(row_landed[s], (w + 1) * (16 * SLOTS))
                sp.sem_inc(rows_ready, 1)

            def batch(s, i, c):
                u = uses[s % 2]
                sp.reg_add(u, u, 16 * SLOTS)
                sp.wait_ge(row_landed[STATIC + s % 2], sp.snap(u, min_val=16 * SLOTS))
                sp.sem_inc(rows_ready, 1)

            further_batches(sp, nb, batch, lambda c: None)
            bt.leave(w, nb, g)

        windows(sp, window)

    @block.gpsimd
    def _(pool):
        q = nc.gpsimd
        q.memset(er9[:], MASKED).then_inc(const_ok, 1)
        bt = Batches(pool, "pool")
        chunks = pool.alloc_register("pool_chunks")
        pool.reg_mov(chunks, 0)

        def gather(buf, idx, col):
            for k in range(SLOTS):
                q.indirect_dma_start(rows[:, buf, k, :], None, table,
                                     bass.IndirectOffsetOnAxis(idx[:, col + k:col + k + 1], 0)
                                     ).then_inc(row_landed[buf], 16)

        def scatter(v, par, n=P):
            pool.wait_ge(out_ok, v + 1)
            alone(pool, pool_passed)
            q.indirect_dma_start(out, bass.IndirectOffsetOnAxis(oid[par][0:n, :], 0), xo[par][0:n, :],
                                 None).then_inc(out_done[par], 16)

        def window(w, par, half):
            nb, g, before = bt.enter(w)
            pool.wait_ge(idx_staged, w + 1)
            after(pool, z_ok, w - 1)
            alone(pool, pool_passed)
            q.indirect_dma_start(node_row[par][:], None, node_tab,
                                 bass.IndirectOffsetOnAxis(idx_st[par][:, CHUNK:CHUNK + 1], 0)
                                 ).then_inc(node_landed[par], 16)
            for s in range(STATIC):
                if not isinstance(w, int) or w > 0:
                    pool.wait_ge(weighted, before + s + 1)
                    alone(pool, pool_passed)
                gather(s, idx_st[par], s * SLOTS)

            def batch(s, i, c):
                if isinstance(c, int) and s < STATIC + 2:
                    after(pool, weighted, g)
                else:
                    pool.wait_ge(weighted, i + (g - 1))
                alone(pool, pool_passed)
                gather(STATIC + s % 2, idx_st[par] if isinstance(c, int) else xidx, s * SLOTS)

            def chunk(c):
                pool.reg_add(chunks, chunks, 1)
                n = pool.snap(chunks, min_val=1)
                pool.wait_ge(xblk_ok, n)
                alone(pool, pool_passed)
                q.indirect_dma_start(xraw[:, 0, :], None, blocks,
                                     bass.IndirectOffsetOnAxis(xblk[:], 0)).then_inc(xblk_in, 16)
                pool.wait_ge(xidx_ok, n)

            further_batches(pool, nb, batch, chunk)
            if not isinstance(w, int) or w >= 2:
                scatter(w - 2, par)
            bt.leave(w, nb, g)

        windows(pool, window)
        scatter(W - 2, 0)
        scatter(W - 1, 1, LAST)
        for i in range(2):
            pool.wait_ge(out_done[i], 16 * (W // 2))

    @block.vector
    def _(dve):
        v = nc.vector
        bt = Batches(dve, "dve")
        chunks = dve.alloc_register("dve_chunks")
        dve.reg_mov(chunks, 0)

        def stage(w, par):
            v.tensor_copy(idx_st[par][:, 0:CHUNK], idx_all[:, bass.ds(w, 1), :].rearrange("p o k -> p (o k)")
                          ).then_inc(stage_step, 1)
            dve.wait_ge(stage_step, w + 1)
            v.tensor_copy(idx_st[par][:, CHUNK:CHUNK + 1],
                          rank_sb[:, bass.ds(w, 1), 0]).then_inc(idx_staged, 1)

        def begin(w, par, half):
            st = Steps(dve, begin_step, w * N_BEGIN)
            dve.wait_ge(node_landed[par], (half + 1) * 16)
            st.did(v.tensor_copy(er9[:, :, 0:R].rearrange("p h r -> p r h"),
                                 node_row[par][:, D:D + RH].rearrange("p (r h) -> p r h", r=R)))
            st.did(v.memset(ebuf[:, :, SLOTS:S1], MASKED))
            st.did(v.memset(acc[:], 0.0))
            st.did(v.memset(coff[:], 0.0))
            st.did(v.tensor_copy(typ_cur[:], typ_all[:, bass.ds(w, 1), :].rearrange("p o k -> p (o k)")))
            st.wait()
            assert st.n == N_BEGIN

        def front(g, buf, col):
            st = Steps(dve, front_step, g * N_FRONT)
            after(dve, front_step, g * N_FRONT)
            st.did(v.tensor_tensor(hot9[:], bc(typ_cur[:, col], 2, R1),
                                   bc(slot_id[:, 0:R1], 1, SLOTS), ALU.is_equal))
            st.wait()
            st.did(v.tensor_tensor(er_hot[:], bc(er9[:], 1, SLOTS), bc(hot9[:], 2, H), ALU.mult))
            st.wait()
            st.did(v.tensor_reduce(score[:], er_hot[:], AX_X, ALU.add))
            st.wait()
            dve.wait_ge(rows_ready, g + 1)
            st.did(v.tensor_tensor(score[:], score[:], rows[:, buf, :, AGG:ROW], ALU.add))
            st.wait()
            st.did(v.scalar_tensor_tensor(out=ebuf[:, :, 0:SLOTS].rearrange("p h k -> p k h"), in0=score[:],
                                          scalar=SLOPE, in1=score[:], op0=ALU.mult, op1=ALU.max))
            st.wait()
            st.did(v.tensor_reduce(m_new[:], ebuf[:], AX_X, ALU.max))
            st.wait()
            v.tensor_tensor(diff[:], ebuf[:], bc(m_new[:], 2, S1), ALU.subtract).then_inc(diff_ok, 1)
            dve.wait_ge(diff_ok, g + 1)
            st.did(v.tensor_copy(ebuf[:, :, SLOTS], m_new[:]))
            assert st.n == N_FRONT

        def weigh(g, buf):
            st = Steps(dve, ex_step, g * N_EX)
            dve.wait_ge(den_ok, g + 1)
            st.did(v.reciprocal(rden[:], den[:]))
            st.wait()
            st.did(v.tensor_scalar(ex[:], rden[:], 2.0, -1.0, ALU.mult, ALU.add))
            st.wait()
            after(dve, agg_ok, g)
            v.tensor_tensor(prod[:].rearrange("p k (h c) -> p k h c", h=H),
                            rows[:, buf, :, 0:AGG].rearrange("p k (h c) -> p k h c", h=H),
                            bc(ex[:, :, 0:SLOTS].rearrange("p h k -> p k h"), 3, HC), ALU.mult).then_inc(weighted, 1)

        def accumulate(g):
            st = Steps(dve, acc_step, g * N_ACC)
            after(dve, acc_step, g * N_ACC)
            st.did(v.tensor_tensor(acc[:], acc[:], bc(ex[:, :, SLOTS], 2, HC), ALU.mult))
            st.wait()
            dve.wait_ge(agg_ok, g + 1)
            st.did(v.tensor_tensor(acc[:], acc[:], agg_ps[:, 0:AGG].rearrange("p (h c) -> p h c", h=H), ALU.add))
            assert st.n == N_ACC

        def post(w, par, half, g_end):
            st = Steps(dve, post_step, w * N_POST)
            dve.wait_ge(acc_step, g_end * N_ACC)
            st.did(v.reciprocal(r4[:], acc[:, :, HD]))
            st.did(v.tensor_scalar(valid[:], rank_sb[:, bass.ds(w, 1), 2], 0.0, None, ALU.is_gt))
            st.wait()
            st.did(v.tensor_scalar(r4[:], r4[:], valid[:, 0:1], None, ALU.mult))
            st.wait()
            st.did(v.tensor_tensor(hn[:].rearrange("p (h d) -> p h d", h=H), acc[:, :, 0:HD], bc(r4[:], 2, HD),
                                   ALU.mult))
            st.wait()
            after(dve, out_done[par], half * 16)
            st.did(v.tensor_tensor(xo[par][:], hn[:], node_row[par][:, 0:D], ALU.add))
            st.wait()
            st.did(v.bn_stats(st6[:], xo[par][:]))
            st.wait()
            alone(dve, dve_passed)
            st.did(v.bn_aggr(mv2[:], st6[:]))
            st.wait()
            st.did(v.tensor_scalar(varp[:], mv2[:, 1:2], EPS, None, ALU.add))
            st.wait()
            rsqrt_steps(nc, st, rstd2[:], varp[:], tmp1[:])
            assert st.n == N_POST, st.n
            v.tensor_scalar(z[:], xo[par][:], mv2[:, 0:1], rstd2[:, 0:1], ALU.subtract, ALU.mult).then_inc(z_ok, 1)

        def gate_in_steps(u):
            st = Steps(dve, gate_step, u * N_GATE)
            dve.wait_ge(logit_ok, u + 1)
            st.did(v.tensor_tensor(lg[:], gate_ps[:, 0:NE], gb[:], ALU.add))
            st.wait()
            alone(dve, dve_passed)
            st.did(v.max(mx8[:], lg[:]))
            st.wait()
            v.tensor_scalar(nm[:], mx8[:, 0:1], -0.5, None, ALU.mult).then_inc(gate_in, 1)
            alone(dve, dve_passed)
            st.did(v.max_index(ix8[:], mx8[:], lg[:]))
            st.wait()
            st.did(v.tensor_copy(ixf[:], ix8[:, 0:2]))
            return st

        def gate_out_steps(u, st):
            dve.wait_ge(gden_ok, u + 1)
            st.did(v.reciprocal(gp[:], gden[:]))
            st.wait()
            st.did(v.tensor_scalar(gp[:], gp[:], 2.0, -1.0, ALU.mult, ALU.add))
            st.wait()
            st.did(v.tensor_reduce(gsum[:], gp[:], AX_X, ALU.add))
            st.wait()
            st.did(v.reciprocal(gsum[:], gsum[:]))
            st.did(v.tensor_scalar(gmask[:], slot_id[:, 0:NE], ixf[:, 0:1], None, ALU.is_equal))
            st.wait()
            st.did(v.scalar_tensor_tensor(out=gmask[:], in0=slot_id[:, 0:NE], scalar=ixf[:, 1:2], in1=gmask[:],
                                          op0=ALU.is_equal, op1=ALU.add))
            st.wait()
            st.did(v.tensor_scalar(gp[:], gp[:], gsum[:, 0:1], None, ALU.mult))
            st.wait()
            assert st.n == N_GATE, st.n
            v.tensor_tensor(cw[:], gp[:], gmask[:], ALU.mult).then_inc(cw_ok, 1)

        def mix_start(u, par):
            st = Steps(dve, mix_step, u * N_MIX)
            dve.wait_ge(cw_ok, u + 1)
            dve.wait_ge(z_ok, u + 1)
            dve.wait_ge(b2_ok, u + 1)
            st.did(v.tensor_tensor(xo[par][:], xo[par][:], b2_ps, ALU.add))
            return st

        def mix(u, par, p, st):
            dve.wait_ge(w2_ok, u * NE + 2 * p + 2)
            for e in (2 * p, 2 * p + 1):
                st.wait()
                st.did(v.scalar_tensor_tensor(out=xo[par][:], in0=y_ps[p % 2][:, (e % 2) * D:(e % 2 + 1) * D],
                                              scalar=cw[:, e:e + 1], in1=xo[par][:], op0=ALU.mult, op1=ALU.add))
            st.wait()
            dve.sem_inc(y_used, 1)

        def finish(u, par, st):
            assert st.n == N_MIX
            v.tensor_copy(oid[par][:], rank_sb[:, bass.ds(u, 1), 0]).then_inc(out_ok, 1)

        def further_chunk(w):
            n = dve.snap(chunks, min_val=0)
            dve.reg_add(chunks, chunks, 1)
            st = Steps(dve, chunk_step, n * N_CHUNK)

            def go(ins):
                st.did(ins)
                st.wait()

            one = bass.ds(w, 1)
            go(v.tensor_scalar(coff[:], coff[:], float(CHUNK), None, ALU.add))
            go(v.tensor_tensor(xst[:], coff[:], rank_sb[:, one, 1], ALU.add))
            go(v.tensor_scalar(xst_i[:], xst[:], float(E), None, ALU.min))
            go(v.tensor_scalar(xblk[:].bitcast(I32), xst_i[:], 3, None, ALU.logical_shift_right))
            dve.sem_inc(xblk_ok, 1)
            for i, by in enumerate((4, 2, 1)):
                go(v.tensor_scalar(xbit_i[:, i:i + 1], xst_i[:], by, None, ALU.bitwise_and))
            go(v.tensor_copy(xbit[:, :, 0], xbit_i[:]))
            for i, by in enumerate((4, 2)):
                go(v.tensor_scalar(xbit[:, i, :], xbit[:, i, :], 1.0 / by, None, ALU.mult))
            dve.wait_ge(xblk_in, n * 16 + 16)
            shift_steps(nc, st, xidx_f[:], xraw[:], xdiff[:], xhalf[:], [xbit[:, i, :] for i in range(3)], CHUNK)
            go(v.tensor_copy(xidx[:], xidx_f[:, 0, :]))
            go(v.tensor_scalar(xlow[:], xidx[:].bitcast(I32), R - 1, None, ALU.bitwise_and))
            go(v.tensor_tensor(xdeg[:], rank_sb[:, one, 2], coff[:], ALU.subtract))
            go(v.tensor_scalar(xmask[:], slot_id[:], xdeg[:, 0:1], None, ALU.is_ge))
            go(v.scalar_tensor_tensor(out=typ_cur[:], in0=xmask[:], scalar=float(R), in1=xlow[:], op0=ALU.mult,
                                      op1=ALU.add))
            go(v.tensor_scalar(typ_cur[:], typ_cur[:], float(R), None, ALU.min))
            assert st.n == N_CHUNK, st.n
            dve.sem_inc(xidx_ok, 1)

        def window(w, par, half):
            nb, g, _ = bt.enter(w)
            u, upar = w - 1, 1 - par
            ffn = not isinstance(w, int) or w > 0
            begin(w, par, half)
            for s in range(STATIC):
                front(g + s, s, slice(s * SLOTS, (s + 1) * SLOTS))
                if ffn and s == 0:
                    gate = gate_in_steps(u)
                if ffn and s == 1:
                    st = mix_start(u, upar)
                if ffn and s >= 1:
                    mix(u, upar, s - 1, st)
                if s:
                    accumulate(g + (s - 1))
                weigh(g + s, s)
                if ffn and s == 0:
                    gate_out_steps(u, gate)
            with dve.If(nb > STATIC):
                with dve.Fori(STATIC - 1, nb - 1) as last:
                    i = dve.snap(last + 1, min_val=STATIC)
                    with dve.If(6 < (SLOTS - 1) - (i & (SLOTS - 1))):
                        further_chunk(w)
                    buf = STATIC + (i & 1)
                    front(g + i, buf, bass.ds((i & (SLOTS - 1)) * SLOTS, SLOTS))
                    accumulate(g + last)
                    weigh(g + i, buf)
            if ffn:
                mix(u, upar, PAIRS - 1, st)
                finish(u, upar, st)
            accumulate(g + nb - 1)
            post(w, par, half, g + nb)
            if not isinstance(w, int):
                with dve.If(w < W - 2):
                    stage(nc.s_assert_within(w + 2, 2, W - 1, skip_runtime_bounds_check_because="the If bounds it"),
                          par)
            else:
                stage(w + 2, par)
            bt.leave(w, nb, g)

        stage(0, 0)
        stage(1, 1)
        dve.wait_ge(const_ok, 1)
        dve.wait_ge(const_in, 64)
        windows(dve, window)
        u = W - 1
        gate_out_steps(u, gate_in_steps(u))
        st = mix_start(u, 1)
        for p in range(PAIRS):
            mix(u, 1, p, st)
        finish(u, 1, st)

    @block.scalar
    def _(act):
        a = nc.scalar
        act.dma_start(gw[:], gate_w.rearrange("(k p) e -> p k e", p=P)).then_inc(const_in, 16)
        act.dma_start(gb[:], gate_b.partition_broadcast(P)).then_inc(const_in, 16)
        act.dma_start(b2s[:], b2).then_inc(const_in, 16)
        act.dma_start(b1t[:], b1.rearrange("e (m p) -> p e m", p=P), allow_slow_non_contiguous=True).then_inc(const_in, 16)
        act.wait_ge(const_in, 64)
        bt = Batches(act, "act")

        def den_of(g):
            act.wait_ge(diff_ok, g + 1)
            a.activation(th[:], diff[:], ACT.Tanh, scale=0.5).then_inc(th_ok, 1)
            act.wait_ge(th_ok, g + 1)
            a.activation(den[:], th[:], ACT.Copy, bias=1.0, scale=-1.0).then_inc(den_ok, 1)

        def z_in(u):
            act.wait_ge(ztr_ok, u + 1)
            a.copy(zT[:], zt_ps[:, 0:D].rearrange("p (k n) -> p k n", k=KD)).then_inc(zT_ok, 1)

        def gate_den(u):
            act.wait_ge(gate_in, u + 1)
            a.activation(gth[:], lg[:], ACT.Tanh, bias=nm[:, 0:1], scale=0.5).then_inc(gth_ok, 1)
            act.wait_ge(gth_ok, u + 1)
            a.activation(gden[:], gth[:], ACT.Copy, bias=1.0, scale=-1.0).then_inc(gden_ok, 1)

        def gelus(u, p):
            for e in (2 * p, 2 * p + 1):
                act.wait_ge(hid_ok, u * NE + e + 1)
                after(act, w2_ok, u * NE + e - 1)
                for m in range(KH):
                    last = a.activation(hT[e % 2][:, m, :], hid_ps[e % 2][:, m * P:(m + 1) * P], ACT.Gelu,
                                        bias=b1t[:, e, m:m + 1])
                    if m < KH - 1:
                        last.then_inc(gelu_ok, 1)
                last.then_inc(gelu_ok, 1)

        def cwt_in(u):
            act.wait_ge(cwt_ok, u + 1)
            a.copy(cwT[:], cwt_ps).then_inc(cwT_ok, 1)

        def window(w, par, half):
            nb, g, _ = bt.enter(w)
            ffn = not isinstance(w, int) or w > 0
            u = w - 1
            if ffn:
                z_in(u)
            for s in range(STATIC):
                den_of(g + s)
                if ffn and s == 0:
                    gate_den(u)
                if ffn:
                    gelus(u, s)
                if ffn and s == 0:
                    cwt_in(u)
            with act.If(nb > STATIC):
                with act.Fori(STATIC, nb) as i:
                    den_of(g + i)
            bt.leave(w, nb, g)

        windows(act, window)
        u = W - 1
        z_in(u)
        gate_den(u)
        for p in range(PAIRS):
            gelus(u, p)
            if p == 0:
                cwt_in(u)

    @block.tensor
    def _(pe):
        t = nc.tensor
        bt = Batches(pe, "pe")

        def z_turn(u):
            pe.wait_ge(z_ok, u + 1)
            for k in range(KD):
                last = t.transpose(zt_ps[:, k * P:(k + 1) * P], z[:, k * P:(k + 1) * P], ident[:])
            last.then_inc(ztr_ok, 1)
            pe.wait_ge(zT_ok, u + 1)
            for k in range(KD):
                last = t.matmul(gate_ps[:, 0:NE], zT[:, k, :], gw[:, k, :], start=(k == 0), stop=(k == KD - 1))
            last.then_inc(logit_ok, 1)

        def experts(u, p):
            for e in (2 * p, 2 * p + 1):
                after(pe, gelu_ok, (u * NE + e - 1) * KH)
                for m in range(KH):
                    for k in range(KD):
                        last = t.matmul(hid_ps[e % 2][:, m * P:(m + 1) * P], w1[:, e, k, m * P:(m + 1) * P],
                                        zT[:, k, :], start=(k == 0), stop=(k == KD - 1))
                last.then_inc(hid_ok, 1)
            after(pe, y_used, u * PAIRS + p - 1)
            for e in (2 * p, 2 * p + 1):
                pe.wait_ge(gelu_ok, (u * NE + e + 1) * KH)
                for k in range(KH):
                    last = t.matmul(y_ps[p % 2][:, (e % 2) * D:(e % 2 + 1) * D], hT[e % 2][:, k, :], w2[:, e, k, :],
                                    start=(k == 0), stop=(k == KH - 1))
                last.then_inc(w2_ok, 1)

        def cw_turn(u):
            pe.wait_ge(cw_ok, u + 1)
            t.transpose(cwt_ps, cw[:], ident[:]).then_inc(cwt_ok, 1)

        def b2_term(u):
            pe.wait_ge(cwT_ok, u + 1)
            t.matmul(b2_ps, cwT[:], b2s[:], start=True, stop=True).then_inc(b2_ok, 1)

        def sums(g):
            pe.wait_ge(weighted, g + 1)
            after(pe, acc_step, g * N_ACC)
            for k in range(SLOTS):
                last = t.matmul(agg_ps[:, 0:AGG], ident[:], prod[:, k, :], start=(k == 0), stop=(k == SLOTS - 1))
            last.then_inc(agg_ok, 1)

        def window(w, par, half):
            nb, g, _ = bt.enter(w)
            ffn = not isinstance(w, int) or w > 0
            u = w - 1
            if ffn:
                z_turn(u)
            for s in range(STATIC):
                if ffn and s == 1:
                    b2_term(u)
                if ffn:
                    experts(u, s)
                if ffn and s == 0:
                    cw_turn(u)
                sums(g + s)
            with pe.If(nb > STATIC):
                with pe.Fori(STATIC, nb) as i:
                    sums(g + i)
            bt.leave(w, nb, g)

        pe.wait_ge(const_in, 64)
        pe.wait_ge(w_in, 16 * NE)
        pe.wait_ge(w_in2, 16 * NE)
        windows(pe, window)
        u = W - 1
        z_turn(u)
        for p in range(PAIRS):
            if p == 1:
                b2_term(u)
            experts(u, p)
            if p == 0:
                cw_turn(u)


_INS = ['x', 'src', 'dst', 'edge_type_8', 'L0_gnn_conv_weights', 'L0_gnn_attn_l', 'L0_gnn_attn_r', 'L0_gnn_h_bias',
        'L0_ffn_gate_w', 'L0_ffn_gate_b', 'L0_ffn_W1', 'L0_ffn_b1', 'L0_ffn_W2', 'L0_ffn_b2']


def kernel(**inputs):
    import numpy as _np
    import concourse.bacc as _bacc
    from concourse import mybir as _mybir
    from concourse.bass_utils import run_bass_kernel_spmd as _run

    nc = _bacc.Bacc("TRN2", target_bir_lowering=False, num_devices=1)
    arrays, args = {}, []
    for name in _INS:
        a = _np.ascontiguousarray(inputs[name])
        arrays[f"in_{name}_dram"] = a
        args.append(nc.dram_tensor(f"in_{name}_dram", a.shape, _mybir.dt.from_np(a.dtype), kind="ExternalInput").ap())
    args.append(nc.dram_tensor("out_dram", (3750, 256), _mybir.dt.float32, kind="ExternalOutput").ap())
    build(nc, *args)
    r = _run(nc, [arrays], core_ids=[0])
    return r.results[0]["out_dram"]
```

```python
from contextlib import ExitStack

import concourse.bass as bass
from concourse import mybir

ALU = mybir.AluOpType
ACT = mybir.ActivationFunctionType
F32 = mybir.dt.float32
I32 = mybir.dt.int32
U32 = mybir.dt.uint32
AX_X = mybir.AxisListType.X

P = 128
SLOTS = 8
STATIC = 4
CHUNK = 64
RING = 6
BIN = 63
SEARCH = 198
MASKED = -1.0e30
EPS = 1e-5
SLOPE = 0.2


class Steps:

    def __init__(self, eng, sem, base=0):
        self.eng, self.sem, self.base, self.n = eng, sem, base, 0

    def did(self, ins):
        ins.then_inc(self.sem, 1)
        self.n += 1

    def wait(self, back=0):
        if self.n - back > 0 or not isinstance(self.base, int):
            self.eng.wait_ge(self.sem, self.base + (self.n - back))


def bc(ap, axis, n):
    ap = ap.unsqueeze(axis)
    shape = list(ap.shape)
    shape[axis] = n
    return ap.to_broadcast(shape)


def rsqrt_steps(nc, st, y, v, tmp):
    st.did(nc.vector.tensor_scalar(tmp.bitcast(I32), v.bitcast(I32), 1, None, ALU.logical_shift_right))
    st.wait()
    st.did(nc.vector.tensor_scalar(y.bitcast(I32), tmp.bitcast(I32), -1.0, 1597463007.0, ALU.mult, ALU.add))
    st.wait()
    for _ in range(3):
        st.did(nc.vector.tensor_tensor(tmp, y, y, ALU.mult))
        st.wait()
        st.did(nc.vector.tensor_tensor(tmp, tmp, v, ALU.mult))
        st.wait()
        st.did(nc.vector.tensor_scalar(tmp, tmp, -0.5, 1.5, ALU.mult, ALU.add))
        st.wait()
        st.did(nc.vector.tensor_tensor(y, y, tmp, ALU.mult))
        st.wait()


def shift_steps(nc, st, out, block, diff, half, bits, width):
    src, bufs = block, (half, block, out)
    for i, by in enumerate((4, 2, 1)):
        n = width + by - 1
        dst = bufs[i][:, :, 0:n]
        st.did(nc.vector.tensor_tensor(diff[:, :, 0:n], src[:, :, by:by + n], src[:, :, 0:n], ALU.subtract))
        st.wait()
        st.did(nc.vector.tensor_tensor(diff[:, :, 0:n], diff[:, :, 0:n], bc(bits[i], 2, n), ALU.mult))
        st.wait()
        st.did(nc.vector.tensor_tensor(dst, diff[:, :, 0:n], src[:, :, 0:n], ALU.add))
        st.wait()
        src = bufs[i]


def build(nc, x, src, dst, etype, conv, attn_l, attn_r, h_bias, gate_w, gate_b, W1, b1, W2, b2, out):
    N, D = x.shape
    E = src.shape[0]
    R, H, _, HD = conv.shape
    NE, _, HID = W1.shape
    KD, KH = D // P, HID // P
    HC = HD + 1
    AGG = H * HC
    ROW = AGG + H
    TN = 125
    T = N // TN
    J = N // TN
    EJ = E // TN
    W = -(-N // P)
    LAST = N - (W - 1) * P
    NF = E // SEARCH
    BW = CHUNK + SLOTS
    NB = E // SLOTS + 2
    NB += -NB % 16
    GN = NB * SLOTS + BW
    NBINS = BIN + 1
    assert TN * T == N and TN * EJ == E and EJ % SEARCH == 0 and D == H * HD and R * H == 32

    table = nc.dram_tensor("table", (N * R, ROW), F32).ap()
    node_tab = nc.dram_tensor("node_tab", (N, D + R * H), F32).ap()
    first_d = nc.dram_tensor("first_d", (NF,), F32).ap()
    edge_row = nc.dram_tensor("edge_row", (GN,), F32)
    blocks = nc.dram_tensor("blocks", (NB, BW), F32).ap()
    start_d = nc.dram_tensor("start_d", (N + 1,), F32).ap()
    ranked = nc.dram_tensor("ranked", (W * P, 4), I32).ap()
    nb_d = nc.dram_tensor("nb_d", (W, 2), I32).ap()

    ctx = ExitStack()

    def sem(name):
        return ctx.enter_context(nc.semaphore(name))

    with ctx:
        def sb(name, shape, dt=F32, stack=ctx):
            return stack.enter_context(nc.sbuf_tensor(name, shape, dt))

        ident = sb("ident", [P, P])
        idx_all = sb("idx_all", [P, W, CHUNK], U32)
        typ_all = sb("typ_all", [P, W, CHUNK])
        rank_sb = sb("rank_sb", [P, W, 4], I32)
        nb_row = sb("nb_row", [1, 2 * W], I32)
        slot_id = sb("slot_id", [P, CHUNK])

        phase1(nc, sb, sem, locals())
        phase2(nc, sb, sem, locals())


def phase1(nc, sb, sem, env):
    (x, src, dst, etype, conv, attn_l, attn_r, h_bias, table, node_tab, first_d, edge_row, blocks, start_d,
     ranked, nb_d, ident, idx_all, typ_all, rank_sb, nb_row, slot_id) = (env[k] for k in (
         "x", "src", "dst", "etype", "conv", "attn_l", "attn_r", "h_bias", "table", "node_tab", "first_d",
         "edge_row", "blocks", "start_d", "ranked", "nb_d", "ident", "idx_all", "typ_all", "rank_sb", "nb_row",
         "slot_id"))
    N, D, E, R, H, HD, KD, HC, AGG, ROW, TN, T, J, EJ, W, NF, BW, NB, GN, NBINS = (env[k] for k in (
        "N", "D", "E", "R", "H", "HD", "KD", "HC", "AGG", "ROW", "TN", "T", "J", "EJ", "W", "NF", "BW", "NB", "GN",
        "NBINS"))
    RH = R * H
    FEAT = R * D
    BANK = 512
    FB = FEAT // BANK
    RB = BANK // D
    GT = 10
    SPLIT = 8
    PAD = W * P - N

    ctx = ExitStack()
    with ctx:
        def t(name, shape, dt=F32):
            return sb(name, shape, dt, ctx)

        x_all = t("x_all", [TN, T, D])
        xn = [t(f"xn{i}", [TN, D]) for i in range(2)]
        xnT = [t(f"xnT{i}", [P, KD, TN]) for i in range(2)]
        wc = t("wc", [P, KD, FEAT])
        attnb = t("attnb", [P, 2, FEAT])
        wa = t("wa", [P, KD, 2 * RH])
        scratch = t("scratch", [P, FEAT])
        hb = t("hb", [TN, D])
        stage = [t(f"stage{i}", [TN, R, ROW]) for i in range(2)]
        er_all = t("er_all", [TN, T, RH])
        stats = t("stats", [TN, T, 6])
        mv = t("mv", [TN, T, 2])
        var = t("var", [TN, T])
        rstd = t("rstd", [TN, T])
        nmr = t("nmr", [TN, T])
        tmpT = t("tmpT", [TN, T])
        dst_sb = t("dst_sb", [TN, EJ], I32)
        src_sb = t("src_sb", [TN, EJ], I32)
        typ_sb = t("typ_sb", [TN, EJ], I32)
        erow = t("erow", [TN, EJ])
        firsts = t("firsts", [TN, EJ // SEARCH])
        first_b = t("first_b", [TN, NF])
        seek = t("seek", [TN, NF])
        node_i = t("node_i", [TN, J], I32)
        node_f = t("node_f", [TN, J])
        cnt = t("cnt", [TN, J])
        chunk_u = t("chunk_u", [TN, J], U32)
        inner = t("inner", [TN, J])
        start = t("start", [TN, J])
        start_n = t("start_n", [TN, J])
        deg = t("deg", [TN, J])
        edges_end = t("edges_end", [1, 1])
        bin_i = t("bin_i", [TN, NBINS], I32)
        bin_f = t("bin_f", [TN, NBINS])
        slot_i = t("slot_i", [P, CHUNK], I32)
        hot = scratch[0:TN, 0:NBINS * J].rearrange("p (b j) -> p b j", b=NBINS)
        run = t("run", [TN, NBINS, J])
        ones = t("ones", [TN, NBINS * J])
        bin_cnt = t("bin_cnt", [TN, NBINS])
        bin_st = t("bin_st", [TN, NBINS])
        lower = t("lower", [TN, TN])
        rank_f = t("rank_f", [TN, J])
        rank_u = t("rank_u", [TN, J], U32)
        info = t("info", [TN, J, 4], I32)
        zeros = t("zeros", [P, 4], I32)
        blk_u = t("blk_u", [P, W], U32)
        bit_i = t("bit_i", [P, 3, W], I32)
        bit_f = t("bit_f", [P, 3, W])
        wide = t("wide", [P, 3 * W * BW])
        dchunk = wide[0:TN, 0:J * SEARCH].bitcast(I32).rearrange("p (j e) -> p j e", j=J)
        blk, half, diff = (wide[:, i * W * BW:(i + 1) * W * BW].rearrange("p (w k) -> p w k", w=W) for i in range(3))
        zero_f = t("zero_f", [1, GN - E])
        deg_r = t("deg_r", [P, W])
        rank_w = t("rank_w", [W, P, 4], I32)
        mx = t("mx", [W, 1])
        nb_i = t("nb_i", [W, 2], I32)

        feat_ps = [ctx.enter_context(nc.psum_tensor(f"feat_ps{b}", [P, BANK], F32)) for b in range(FB)]
        score_ps = ctx.enter_context(nc.psum_tensor("score_ps", [P, BANK], F32))
        tr_ps = [ctx.enter_context(nc.psum_tensor(f"tr_ps{i}", [P, BANK], F32)) for i in range(2)]
        off_ps = ctx.enter_context(nc.psum_tensor("off_ps", [P, BANK], F32))

        x_in = [sem(f"x_in{g}") for g in range(T // GT)]
        dst_in, et_in, conv_in, attn_in, hb_in = (sem(n) for n in ("dst_in", "et_in", "conv_in", "attn_in", "hb_in"))
        ident0, ident_ok, pool_const, pool_mask = (sem(n) for n in ("ident0", "ident_ok", "pool_const", "pool_mask"))
        firsts_ok, first_out, first_in = sem("firsts_ok"), sem("first_out"), sem("first_in")
        erow_ok, erow_out, blocks_out = sem("erow_ok"), sem("erow_out"), sem("blocks_out")
        norm_ok, xb_ok, node_out = sem("norm_ok"), sem("xb_ok"), sem("node_out")
        ones_ok, wa_ok = sem("ones_ok"), sem("wa_ok")
        chunk_ok, chunk_in = sem("chunk_ok"), [sem(f"chunk_in{g}") for g in range(3)]
        start_ok, start_out, start_in = sem("start_ok"), sem("start_out"), sem("start_in")
        bins_ok, offs_ok, rank_ok = sem("bins_ok"), sem("offs_ok"), sem("rank_ok")
        zero_out, ranked_out, rank_in = sem("zero_out"), sem("ranked_out"), sem("rank_in")
        blk_ok, blk_in, nb_ok, nb_out, nb_in = (sem(n) for n in ("blk_ok", "blk_in", "nb_ok", "nb_out", "nb_in"))
        xn_ok, tr_ok, xnT_ok = sem("xn_ok"), sem("tr_ok"), sem("xnT_ok")
        feat_ok, score_ok = sem("feat_ok"), sem("score_ok")
        feat_free, score_free = [sem(f"feat_free{b}") for b in range(FB)], sem("score_free")
        stage_ok, stored = sem("stage_ok"), [sem(f"stored{i}") for i in range(2)]
        dstep = sem("dstep1")

        table_v = table.rearrange("(t p r) c -> t p (r c)", t=T, p=TN)
        x_v = x.rearrange("(t p) d -> p t d", p=TN)

        block = ctx.enter_context(nc.Block())

        @block.sync
        def _(sp):
            flat = dict(p=TN)
            sp.dma_start(dst_sb[:], dst.rearrange("(p e) -> p e", **flat)).then_inc(dst_in, 16)
            sp.dma_start(x_all[:, 0:GT, :], x_v[:, 0:GT, :]).then_inc(x_in[0], 16)
            sp.dma_start(src_sb[:], src.rearrange("(p e) -> p e", **flat)).then_inc(et_in, 16)
            sp.dma_start(typ_sb[:], etype.rearrange("(p e) -> p e", **flat)).then_inc(et_in, 16)
            for i, a in enumerate((attn_l, attn_r)):
                sp.dma_start(attnb[:, i, :], a.rearrange("r h d -> (r h d)").partition_broadcast(P)).then_inc(attn_in, 16)
            sp.dma_start(hb[:], h_bias.partition_broadcast(TN)).then_inc(hb_in, 16)
            for g in range(1, T // GT):
                sp.dma_start(x_all[:, g * GT:(g + 1) * GT, :], x_v[:, g * GT:(g + 1) * GT, :]).then_inc(x_in[g], 16)
            sp.wait_ge(firsts_ok, 1)
            sp.dma_start(first_d.rearrange("(p c) -> p c", **flat), firsts[:]).then_inc(first_out, 16)
            sp.wait_ge(first_out, 16)
            sp.dma_start(first_b[:], first_d.partition_broadcast(TN)).then_inc(first_in, 16)
            sp.wait_ge(erow_ok, 1)
            sp.wait_ge(pool_const, 3)
            flat_rows = edge_row.ap()
            sp.dma_start(flat_rows[0:E].rearrange("(p e) -> p e", **flat), erow[:]).then_inc(erow_out, 16)
            sp.dma_start(flat_rows[E:GN].rearrange("(p e) -> p e", p=1), zero_f[:]).then_inc(erow_out, 16)
            sp.wait_ge(erow_out, 32)
            sp.dma_start(blocks, bass.AP(edge_row, 0, [[SLOTS, NB], [1, BW]])).then_inc(blocks_out, 16)
            sp.wait_ge(start_ok, 1)
            sp.dma_start(start_d[0:N].rearrange("(p j) -> p j", **flat), start[:]).then_inc(start_out, 16)
            sp.dma_start(start_d[N:N + 1].rearrange("(p j) -> p j", p=1), edges_end[:]).then_inc(start_out, 16)
            sp.wait_ge(start_out, 32)
            sp.dma_start(start_n[:], start_d[1:N + 1].rearrange("(p j) -> p j", **flat)).then_inc(start_in, 16)
            sp.dma_start(ranked[N:W * P, :], zeros[0:PAD, :]).then_inc(zero_out, 16)
            sp.wait_ge(zero_out, 16)
            sp.wait_ge(ranked_out, 16 * J)
            sp.dma_start(rank_sb[:], ranked.rearrange("(w p) c -> p w c", p=P)).then_inc(rank_in, 16)
            sp.dma_start(rank_w[:], ranked.rearrange("(w p) c -> w p c", p=P)).then_inc(rank_in, 16)
            sp.wait_ge(nb_ok, 1)
            sp.dma_start(nb_d, nb_i[:]).then_inc(nb_out, 16)
            sp.wait_ge(nb_out, 16)
            sp.dma_start(nb_row[:], nb_d.rearrange("(o w) c -> o (w c)", o=1)).then_inc(nb_in, 16)
            sp.wait_ge(nb_in, 16)
            sp.wait_ge(blocks_out, 16)
            for g in range(T // GT):
                sp.wait_ge(xb_ok, g + 1)
                sp.dma_start(node_tab.rearrange("(t p) d -> p t d", p=TN)[:, g * GT:(g + 1) * GT, 0:D],
                             x_all[:, g * GT:(g + 1) * GT, :]).then_inc(node_out, 16)
            sp.wait_ge(score_free, T)
            sp.dma_start(node_tab.rearrange("(t p) d -> p t d", p=TN)[:, :, D:D + RH], er_all[:]).then_inc(node_out, 16)
            sp.wait_ge(node_out, 16 * (T // GT + 1))
            for i in range(2):
                sp.wait_ge(stored[i], 16 * (T // 2))

        @block.gpsimd
        def _(pool):
            g = nc.gpsimd
            g.memset(zero_f[:], 0.0).then_inc(pool_const, 1)
            g.memset(zeros[:], 0).then_inc(pool_const, 1)
            g.memset(edges_end[:], float(E)).then_inc(pool_const, 1)
            g.memset(ident[:], 0.0).then_inc(ident0, 1)
            g.memset(lower[:], 1.0).then_inc(ident0, 1)
            pool.wait_ge(ident0, 2)
            g.affine_select(out=ident[:], in_=ident[:], compare_op=ALU.not_equal, fill=1.0, base=0,
                            pattern=[[-1, P]], channel_multiplier=1).then_inc(ident_ok, 1)
            g.affine_select(out=lower[:], in_=lower[:], compare_op=ALU.is_ge, fill=0.0, base=-1,
                            pattern=[[1, TN]], channel_multiplier=-1).then_inc(pool_mask, 1)
            g.iota(node_i[:], pattern=[[1, J]], base=0, channel_multiplier=J).then_inc(pool_const, 1)
            g.iota(bin_i[:], pattern=[[1, NBINS]], base=-BIN, channel_multiplier=0).then_inc(pool_const, 1)
            g.iota(slot_i[:], pattern=[[1, CHUNK]], base=0, channel_multiplier=0).then_inc(pool_const, 1)
            pool.wait_ge(chunk_ok, 1)
            for j in range(J):
                g.indirect_dma_start(dchunk[:, j, :], None, dst.rearrange("(c e) -> c e", e=SEARCH),
                                     bass.IndirectOffsetOnAxis(chunk_u[:, j:j + 1], 0)).then_inc(chunk_in[j // 10], 16)
            pool.wait_ge(rank_ok, 1)
            pool.wait_ge(zero_out, 16)
            for j in range(J):
                g.indirect_dma_start(ranked, bass.IndirectOffsetOnAxis(rank_u[:, j:j + 1], 0), info[:, j, :],
                                     None).then_inc(ranked_out, 16)
            pool.wait_ge(blk_ok, 1)
            pool.wait_ge(blocks_out, 16)
            for w in range(W):
                g.indirect_dma_start(blk[:, w, :], None, blocks,
                                     bass.IndirectOffsetOnAxis(blk_u[:, w:w + 1], 0)).then_inc(blk_in, 16)
            pool.wait_ge(blk_in, 16 * W)

        @block.vector
        def _(dve):
            v = nc.vector
            st = Steps(dve, dstep)

            def go(ins):
                st.did(ins)
                st.wait()

            go(v.memset(ones[:], 1.0))
            for i in range(2):
                for h in range(H):
                    v.memset(stage[i][:, :, h * HC + HD:h * HC + HD + 1], 1.0).then_inc(ones_ok, 1)
            dve.wait_ge(dst_in, 16)
            v.tensor_copy(firsts[:], dst_sb[:].rearrange("p (c e) -> p c e", e=SEARCH)[:, :, 0]).then_inc(firsts_ok, 1)

            def norms(g):
                dve.wait_ge(x_in[g], 16)
                for i in range(g * GT, (g + 1) * GT):
                    st.did(v.bn_stats(stats[:, i, :], x_all[:, i, :]))
                st.wait()
                for i in range(g * GT, (g + 1) * GT):
                    st.did(v.bn_aggr(mv[:, i, :], stats[:, i, :]))
                st.wait()
                s = slice(g * GT, (g + 1) * GT)
                go(v.tensor_scalar(var[:, s], mv[:, s, 1], EPS, None, ALU.add))
                rsqrt_steps(nc, st, rstd[:, s], var[:, s], tmpT[:, s])
                v.scalar_tensor_tensor(out=nmr[:, s], in0=mv[:, s, 0], scalar=-1.0, in1=rstd[:, s], op0=ALU.mult,
                                       op1=ALU.mult).then_inc(norm_ok, 1)

            norms(0)
            dve.wait_ge(pool_const, 6)
            go(v.tensor_copy(node_f[:], node_i[:]))
            go(v.tensor_copy(bin_f[:], bin_i[:]))
            go(v.tensor_copy(slot_id[:], slot_i[:]))
            dve.wait_ge(first_in, 16)
            for j in range(J):
                st.did(v.tensor_scalar(seek[:], first_b[:], node_f[:, j:j + 1], 0.0, ALU.is_lt, ALU.add,
                                       accum_out=cnt[:, j:j + 1]))
                st.wait()
            go(v.tensor_scalar(cnt[:], cnt[:], -1.0, 0.0, ALU.add, ALU.max))
            v.tensor_copy(chunk_u[:], cnt[:]).then_inc(chunk_ok, 1)
            dve.wait_ge(et_in, 32)
            v.scalar_tensor_tensor(out=erow[:], in0=src_sb[:], scalar=float(R), in1=typ_sb[:], op0=ALU.mult,
                                   op1=ALU.add).then_inc(erow_ok, 1)
            dve.wait_ge(attn_in, 32)
            dve.wait_ge(conv_in, 16 * R * KD)
            for lr in range(2):
                for k in range(KD):
                    go(v.tensor_tensor(scratch[:], wc[:, k, :], attnb[:, lr, :], ALU.mult))
                    go(v.tensor_reduce(wa[:, k, lr * RH:(lr + 1) * RH],
                                       scratch[:].rearrange("p (a d) -> p a d", d=HD), AX_X, ALU.add))
            dve.sem_inc(wa_ok, 1)
            norms(1)
            norms(2)
            for j in range(J):
                if j % 10 == 0:
                    dve.wait_ge(chunk_in[j // 10], 160)
                st.did(v.tensor_scalar(seek[:, 0:SEARCH], dchunk[:, j, :], node_f[:, j:j + 1], 0.0, ALU.is_lt,
                                       ALU.add, accum_out=inner[:, j:j + 1]))
                st.wait()
            v.scalar_tensor_tensor(out=start[:], in0=cnt[:], scalar=float(SEARCH), in1=inner[:], op0=ALU.mult,
                                   op1=ALU.add).then_inc(start_ok, 1)
            dve.wait_ge(start_in, 16)
            go(v.tensor_tensor(deg[:], start_n[:], start[:], ALU.subtract))
            go(v.tensor_scalar(tmpT[:], deg[:], float(BIN), -1.0, ALU.min, ALU.mult))
            go(v.tensor_tensor(hot, bc(tmpT[:], 1, NBINS), bc(bin_f[:], 2, J), ALU.is_equal))
            go(v.tensor_tensor_scan(out=run[:].rearrange("p b j -> p (b j)"), data0=ones[:],
                                    data1=hot.rearrange("p b j -> p (b j)"), initial=0.0, op0=ALU.mult,
                                    op1=ALU.add))
            go(v.memset(bin_st[:, 0:1], 0.0))
            go(v.tensor_copy(bin_st[:, 1:NBINS], run[:, 0:BIN, J - 1]))
            v.tensor_tensor(bin_cnt[:], run[:, :, J - 1], bin_st[:], ALU.subtract).then_inc(bins_ok, 1)
            dve.wait_ge(offs_ok, 1)
            go(v.scalar_tensor_tensor(out=bin_cnt[:], in0=off_ps[0:TN, 0:NBINS], scalar=-1.0, in1=bin_st[:],
                                      op0=ALU.add, op1=ALU.subtract))
            go(v.tensor_tensor(run[:], run[:], bc(bin_cnt[:], 2, J), ALU.add))
            go(v.tensor_tensor(run[:], run[:], hot, ALU.mult))
            go(v.tensor_reduce(rank_f[:], run[:].rearrange("p b j -> p j b"), AX_X, ALU.add))
            go(v.tensor_copy(info[:, :, 0], node_f[:]))
            go(v.tensor_copy(info[:, :, 1], start[:]))
            go(v.tensor_copy(info[:, :, 2], deg[:]))
            go(v.memset(info[:, :, 3], 0))
            v.tensor_copy(rank_u[:], rank_f[:]).then_inc(rank_ok, 1)
            dve.wait_ge(hb_in, 16)

            def residual(g):
                dve.wait_ge(xn_ok, (g + 1) * GT)
                s = slice(g * GT, (g + 1) * GT)
                v.tensor_tensor(x_all[:, s, :], x_all[:, s, :], bc(hb[:], 1, GT), ALU.add).then_inc(xb_ok, 1)

            residual(0)
            residual(1)
            dve.wait_ge(rank_in, 32)
            v.tensor_scalar(blk_u[:].bitcast(I32), rank_sb[:, :, 1], 3, None, ALU.logical_shift_right).then_inc(blk_ok, 1)
            go(v.tensor_reduce(mx[:], rank_w[:, :, 2], AX_X, ALU.max))
            go(v.tensor_copy(nb_i[:, 1:2], mx[:]))
            go(v.tensor_scalar(nb_i[:, 0:1], mx[:], float(SLOTS - 1 - SLOTS * STATIC), 0.0, ALU.add, ALU.max))
            v.tensor_scalar(nb_i[:, 0:1], nb_i[:, 0:1], 3, None, ALU.logical_shift_right).then_inc(nb_ok, 1)
            for i, by in enumerate((4, 2, 1)):
                go(v.tensor_scalar(bit_i[:, i, :], rank_sb[:, :, 1], by, None, ALU.bitwise_and))
                go(v.tensor_scalar(bit_f[:, i, :], bit_i[:, i, :], 1.0 / by, None, ALU.mult))
            go(v.tensor_copy(deg_r[:], rank_sb[:, :, 2]))
            dve.wait_ge(blk_in, 16 * W)
            shift_steps(nc, st, typ_all[:], blk, diff, half, [bit_f[:, i, :] for i in range(3)], CHUNK)
            go(v.tensor_copy(idx_all[:], typ_all[:]))
            low = half[:, :, 0:CHUNK].bitcast(I32)
            go(v.tensor_scalar(low, idx_all[:].bitcast(I32), R - 1, None, ALU.bitwise_and))
            go(v.tensor_tensor(diff[:, :, 0:CHUNK], bc(slot_id[:], 1, W), bc(deg_r[:], 2, CHUNK), ALU.is_ge))
            go(v.scalar_tensor_tensor(out=typ_all[:], in0=diff[:, :, 0:CHUNK], scalar=float(R), in1=low,
                                      op0=ALU.mult, op1=ALU.add))
            go(v.tensor_scalar(typ_all[:], typ_all[:], float(R), None, ALU.min))
            residual(2)

        @block.scalar
        def _(act):
            a = nc.scalar
            for r in range(R):
                for k in range(KD):
                    act.dma_start(wc[:, k, r * D:(r + 1) * D].rearrange("p (h d) -> p h d", h=H),
                                  conv[r, :, k * P:(k + 1) * P, :].rearrange("h p d -> p h d")).then_inc(conv_in, 16)

            def normalize(i, par):
                act.wait_ge(norm_ok, i // GT + 1)
                a.activation(xn[par][:], x_all[:, bass.ds(i, 1), :].rearrange("p o d -> p (o d)"), ACT.Identity,
                             bias=nmr[:, bass.ds(i, 1)], scale=rstd[:, bass.ds(i, 1)]).then_inc(xn_ok, 1)

            def transposed(i, par):
                act.wait_ge(tr_ok, i + 1)
                if not isinstance(i, int) or i >= 2:
                    act.wait_ge(score_ok, i - 1)
                a.copy(xnT[par][:], tr_ps[par][:, 0:KD * TN].rearrange("p (k n) -> p k n", k=KD)).then_inc(xnT_ok, 1)

            def evacuate(i, par, pair, ahead):
                if ahead > 1:
                    normalize(i + 2, par)
                if not isinstance(i, int) or i >= 2:
                    act.wait_ge(stored[par], 16 * pair)
                for b in range(FB):
                    if b == FB // 2 and ahead > 0:
                        transposed(i + 1, 1 - par)
                    act.wait_ge(feat_ok, i * FB + b + 1)
                    a.copy(stage[par][:, b * RB:(b + 1) * RB, 0:AGG].rearrange("p r (h c) -> p r h c", h=H)[:, :, :, 0:HD],
                           feat_ps[b][0:TN, :].rearrange("p (r h d) -> p r h d", r=RB, h=H)).then_inc(feat_free[b], 1)
                act.wait_ge(score_ok, i + 1)
                a.copy(stage[par][:, :, AGG:ROW],
                       score_ps[0:TN, 0:RH].rearrange("p (r h) -> p r h", r=R)).then_inc(stage_ok, 1)
                a.copy(er_all[:, bass.ds(i, 1), :].rearrange("p o c -> p (o c)"),
                       score_ps[0:TN, RH:2 * RH]).then_inc(score_free, 1)
                act.wait_ge(stage_ok, i + 1)
                for b in range(FB):
                    act.wait_ge(feat_free[b], i + 1)
                act.dma_start(table_v[bass.ds(i, 1)].rearrange("o p c -> (o p) c"),
                              stage[par][:].rearrange("p r c -> p (r c)")).then_inc(stored[par], 16)

            normalize(0, 0)
            normalize(1, 1)
            transposed(0, 0)
            act.wait_ge(ones_ok, 2 * H)
            for par in range(2):
                evacuate(par, par, 0, 2)
            with act.Fori(1, T // 2 - 1) as pair:
                for par in range(2):
                    evacuate(pair * 2 + par, par, pair, 2)
            evacuate(T - 2, 0, T // 2 - 1, 1)
            evacuate(T - 1, 1, T // 2 - 1, 0)

        @block.tensor
        def _(pe):
            m = nc.tensor

            def transposes(i, par):
                pe.wait_ge(xn_ok, i + 1)
                if not isinstance(i, int) or i >= 2:
                    pe.wait_ge(xnT_ok, i - 1)
                for k in range(KD):
                    last = m.transpose(tr_ps[par][:, k * TN:(k + 1) * TN], xn[par][:, k * P:(k + 1) * P],
                                       ident[0:TN, 0:TN])
                last.then_inc(tr_ok, 1)

            def products(i, par, ahead=True):
                pe.wait_ge(xnT_ok, i + 1)
                for b in range(FB):
                    if b == FB // 2 and ahead:
                        transposes(i + 1, 1 - par)
                    if not isinstance(i, int) or i >= 1:
                        pe.wait_ge(feat_free[b], i)
                    for k in range(KD):
                        last = m.matmul(feat_ps[b][0:TN, :], xnT[par][:, k, :], wc[:, k, b * BANK:(b + 1) * BANK],
                                        start=(k == 0), stop=(k == KD - 1))
                    last.then_inc(feat_ok, 1)

            def node_scores(i, par):
                if not isinstance(i, int) or i >= 1:
                    pe.wait_ge(score_free, i)
                pe.wait_ge(wa_ok, 1)
                for k in range(KD):
                    last = m.matmul(score_ps[0:TN, 0:2 * RH], xnT[par][:, k, :], wa[:, k, :], start=(k == 0),
                                    stop=(k == KD - 1))
                last.then_inc(score_ok, 1)

            def tiles(lo, hi):
                with pe.Fori(lo, hi) as pair:
                    for par in range(2):
                        products(pair * 2 + par, par)
                        node_scores(pair * 2 + par, par)

            pe.wait_ge(ident_ok, 1)
            transposes(0, 0)
            pe.wait_ge(conv_in, 16 * R * KD)
            products(0, 0)
            products(1, 1, ahead=False)
            node_scores(0, 0)
            transposes(2, 0)
            node_scores(1, 1)
            tiles(1, SPLIT // 2)
            pe.wait_ge(bins_ok, 1)
            pe.wait_ge(pool_mask, 1)
            m.matmul(off_ps[0:TN, 0:NBINS], lower[:], bin_cnt[:], start=True, stop=False)
            m.matmul(off_ps[0:TN, 0:NBINS], ones[:, 0:TN], bin_st[:], start=False, stop=True).then_inc(offs_ok, 1)
            tiles(SPLIT // 2, T // 2 - 1)
            products(T - 2, 0)
            node_scores(T - 2, 0)
            products(T - 1, 1, ahead=False)
            node_scores(T - 1, 1)


def phase2(nc, sb, sem, env):
    (W1, b1, W2, b2, gate_w, gate_b, out, table, node_tab, blocks, ident, idx_all, typ_all, rank_sb, nb_row,
     slot_id) = (env[k] for k in (
         "W1", "b1", "W2", "b2", "gate_w", "gate_b", "out", "table", "node_tab", "blocks", "ident", "idx_all",
         "typ_all", "rank_sb", "nb_row", "slot_id"))
    N, D, E, R, H, HD, HC, AGG, ROW, W, LAST, BW, NE, HID, KD, KH = (env[k] for k in (
        "N", "D", "E", "R", "H", "HD", "HC", "AGG", "ROW", "W", "LAST", "BW", "NE", "HID", "KD", "KH"))
    RH = R * H
    R1 = R + 1
    HALF = SLOTS // 2
    NS = STATIC * SLOTS
    S1 = SLOTS + 1
    PAIRS = NE // 2
    assert PAIRS == STATIC and W % 2 == 0

    N_FRONT, N_EX, N_BEGIN, N_POST, N_GATE, N_MIX = 6, 6, 5, 21, 11, 1 + NE
    N_XFRONT, N_XEX, N_XACC, N_CHUNK = 7, 4, 1, 25

    rows = [sb(f"rows{i}", [P, NS, ROW]) for i in range(2)]
    xrows = sb("xrows", [P, 2, SLOTS, ROW])
    xprod = sb("xprod", [P, HALF, AGG])
    w1 = sb("w1", [P, NE, KD, HID])
    w2 = sb("w2", [P, NE, KH, D])
    b1t = sb("b1t", [P, NE, KH])
    b2s = sb("b2s", [NE, D])
    gw = sb("gw", [P, KD, NE])
    gb = sb("gb", [P, NE])
    idx_st = [sb(f"idx_st{i}", [P, NS + 1], U32) for i in range(2)]
    idx_x = [sb(f"idx_x{i}", [P, CHUNK - NS], U32) for i in range(2)]
    xres = [sb(f"xres{i}", [P, D]) for i in range(2)]
    node_row = [sb(f"node_row{i}", [P, D + RH]) for i in range(2)]
    xo = [sb(f"xo{i}", [P, D]) for i in range(2)]
    oid = [sb(f"oid{i}", [P, 1], U32) for i in range(2)]
    typ_cur = [sb(f"typ_cur{i}", [P, CHUNK]) for i in range(2)]
    er9 = [sb(f"er9{i}", [P, H, R1]) for i in range(2)]
    hot9 = sb("hot9", [P, NS, R1])
    er_hot = sb("er_hot", [P, NS, H, R1])
    score = sb("score", [P, NS, H])
    ebuf, diff, th, den, rden, ex = (sb(n, [P, H, NS]) for n in ("ebuf", "e_diff", "th", "den", "rden", "ex"))
    xebuf, xdiff, xth, xden, xrden, xex = (sb(n, [P, H, S1]) for n in ("xebuf", "xdiff", "xth", "xden", "xrden",
                                                                       "xex"))
    m_win = [sb(f"m_win{i}", [P, H]) for i in range(2)]
    m_new = sb("m_new", [P, H])
    acc = sb("acc", [P, H, HC])
    r4 = sb("r4", [P, H])
    valid = [sb(f"valid{i}", [P, 1]) for i in range(2)]
    hn = sb("hn", [P, D])
    st6 = sb("st6", [P, 6])
    mv2 = sb("mv2", [P, 2])
    varp = sb("varp", [P, 1])
    rstd2 = sb("rstd2", [P, 1])
    tmp1 = sb("tmp1", [P, 1])
    z = sb("z", [P, D])
    zT = sb("zT", [P, KD, P])
    hT = [sb(f"hT{i}", [P, KH, P]) for i in range(2)]
    lg = sb("lg", [P, NE])
    mx8 = sb("mx8", [P, NE])
    ix8 = sb("ix8", [P, NE], U32)
    ixf = sb("ixf", [P, 2])
    nm = sb("nm", [P, 1])
    gth = sb("gth", [P, NE])
    gden = sb("gden", [P, NE])
    gp = sb("gp", [P, NE])
    gsum = sb("gsum", [P, 1])
    gmask = sb("gmask", [P, NE])
    cw = sb("cw", [P, NE])
    cwT = sb("cwT", [NE, P])
    coff = [sb(f"coff{i}", [P, 1]) for i in range(2)]
    xst = sb("xst", [P, 1])
    xst_i = sb("xst_i", [P, 1], I32)
    xblk = sb("xblk", [P, 1], U32)
    xbit_i = sb("xbit_i", [P, 3], I32)
    xbit = sb("xbit", [P, 3, 1])
    xraw = sb("xraw", [P, 1, BW])
    xhalf = sb("xhalf", [P, 1, BW])
    xby = sb("xby", [P, 1, BW])
    xidx_f = sb("xidx_f", [P, 1, CHUNK])
    xidx = sb("xidx", [P, CHUNK], U32)
    xlow = sb("xlow", [P, CHUNK], I32)
    xdeg = sb("xdeg", [P, 1])
    xmask = sb("xmask", [P, CHUNK])

    def bank(name):
        return env["ctx"].enter_context(nc.psum_tensor(name, [P, 512], F32))

    hid_ps = [bank(f"hid_ps{i}") for i in range(2)]
    y_ps = [bank(f"y_ps{i}") for i in range(2)]
    agg_ps, gate_ps, zt_ps = bank("agg_ps"), bank("gate_ps"), bank("zt_ps")
    b2_ps = zt_ps[:, 256:256 + D]
    cwt_ps = gate_ps[0:NE, 128:256]

    w_in, w_in2, const_in = sem("w_in"), sem("w_in2"), sem("const_in")
    const_ok = sem("const_ok")
    idx_staged = sem("idx_staged")
    xidx_staged = sem("xidx_staged")
    row_landed = [[sem(f"row_landed{i}_{k}") for k in range(STATIC)] for i in range(2)]
    xrow_landed = [sem(f"xrow_landed{i}") for i in range(2)]
    last_ready = sem("last_ready")
    xrows_ready = sem("xrows_ready")
    cleared = sem("cleared")
    node_landed = [sem(f"node_landed{i}") for i in range(2)]
    diff_ok, th_ok, den_ok = sem("diff_ok"), sem("th_ok"), sem("den_ok")
    xdiff_ok, xth_ok, xden_ok = sem("xdiff_ok"), sem("xth_ok"), sem("xden_ok")
    folded = sem("folded")
    agg_ok = sem("agg_ok")
    acc_ok = sem("acc_ok")
    xfolded, xagg_ok = sem("xfolded"), sem("xagg_ok")
    z_ok, ztr_ok, zT_ok = sem("z_ok"), sem("ztr_ok"), sem("zT_ok")
    logit_ok, gate_in, gth_ok, gden_ok, cw_ok, cwt_ok, cwT_ok, b2_ok = (sem(n) for n in (
        "logit_ok", "gate_in", "gth_ok", "gden_ok", "cw_ok", "cwt_ok", "cwT_ok", "b2_ok"))
    hid_ok, gelu_ok, w2_ok, y_used = sem("hid_ok"), sem("gelu_ok"), sem("w2_ok"), sem("y_used")
    out_ok, out_done = sem("out_ok"), [sem(f"out_done{i}") for i in range(2)]
    pool_passed, dve_passed = sem("pool_passed"), sem("dve_passed")
    clear_step, take_step = sem("clear_step"), sem("take_step")
    xblk_ok, xblk_in, xidx_ok = sem("xblk_ok"), sem("xblk_in"), sem("xidx_ok")
    (front_step, ex_step, begin_step, post_step, gate_step, mix_step, chunk_step, stage_step) = (
        sem(n) for n in ("front_step", "ex_step", "begin_step", "post_step", "gate_step", "mix_step",
                         "chunk_step", "stage_step"))
    xfront_step, xex_step, xacc_step = sem("xfront_step"), sem("xex_step"), sem("xacc_step")

    def after(eng, s, value):
        if not isinstance(value, int) or value > 0:
            eng.wait_ge(s, value)

    def windows(eng, window):
        for w in range(2):
            window(w, w, 0)
        with eng.Fori(1, W // 2) as j:
            for par in range(2):
                window(j * 2 + par, par, j)

    def within(w):
        return nc.s_assert_within(w, 2, W - 1, skip_runtime_bounds_check_because="the If around it bounds it")

    def next_window(eng, act_on, w, par, half):
        if isinstance(w, int) or par == 0:
            act_on(w + 1, 1 - par, half + par)
        else:
            with eng.If(w < W - 1):
                act_on(within(w + 1), 1 - par, half + par)

    def alone(eng, passed):
        eng.sem_inc(passed, 1)

    class Batches:

        def __init__(self, eng, name):
            self.eng = eng
            self.total = eng.alloc_register(f"{name}_total")
            eng.reg_mov(self.total, 0)

        def enter(self, w):
            more = self.eng.value_load(nb_row[0:1, bass.ds(w * 2, 1)], min_val=0, max_val=E // SLOTS + 1 - STATIC)
            return more + STATIC, (0 if isinstance(w, int) and w == 0 else self.eng.snap(self.total, min_val=0))

        def leave(self, w, nb, g):
            self.eng.reg_mov(self.total, (nb - STATIC) + g)

    def further_batches(eng, nb, batch, chunk):
        def chain(s, c, left):
            if s == SLOTS:
                return
            with eng.If(left > s):
                batch(s, c * SLOTS + s if not isinstance(c, int) else s, c)
                chain(s + 1, c, left)

        chain(STATIC, 0, nb)
        with eng.If(nb > SLOTS):
            with eng.Fori(1, (nb + (SLOTS - 1)) >> 3) as c:
                chunk(c)
                chain(0, c, nb - c * SLOTS)

    block = env["ctx"].enter_context(nc.Block())

    @block.sync
    def _(sp):
        w1_v = W1.rearrange("e (k p) n -> p e k n", p=P)
        w2_v = W2.rearrange("e (k p) n -> p e k n", p=P)
        for e in range(NE):
            sp.dma_start(w1[:, e], w1_v[:, e]).then_inc(w_in, 16)
            sp.dma_start(w2[:, e], w2_v[:, e]).then_inc(w_in2, 16)
        bt = Batches(sp, "sp")
        uses = [sp.alloc_register(f"uses{i}") for i in range(2)]
        last_uses = [sp.alloc_register(f"last_uses{i}") for i in range(2)]
        for r in uses + last_uses:
            sp.reg_mov(r, 0)

        def relay(use, landed, halved, ready):
            sp.reg_add(use, use, 16 * HALF)
            with sp.If(halved):
                sp.reg_add(use, use, 16 * HALF)
            sp.wait_ge(landed, sp.snap(use, min_val=16 * HALF))
            sp.sem_inc(ready, 1)

        def last_static(w, par, half):
            degree = sp.value_load(nb_row[0:1, bass.ds(w * 2 + 1, 1)], min_val=0, max_val=E)
            relay(last_uses[par], row_landed[par][STATIC - 1], degree > NS - HALF, last_ready)

        def window(w, par, half):
            nb, g = bt.enter(w)

            next_window(sp, last_static, w, par, half)
            degree = sp.value_load(nb_row[0:1, bass.ds(w * 2 + 1, 1)], min_val=0, max_val=E)

            def batch(s, i, c):
                relay(uses[s % 2], xrow_landed[s % 2], degree > i * SLOTS + HALF, xrows_ready)

            further_batches(sp, nb, batch, lambda c: None)
            bt.leave(w, nb, g)

        last_static(0, 0, 0)
        windows(sp, window)

    @block.gpsimd
    def _(pool):
        q = nc.gpsimd
        for i in range(2):
            q.memset(er9[i][:], MASKED).then_inc(const_ok, 1)
        bt = Batches(pool, "pool")
        chunks = pool.alloc_register("pool_chunks")
        pool.reg_mov(chunks, 0)

        def gather(buf, landed, idx, col, slots):
            for k in slots:
                q.indirect_dma_start(buf[:, k, :], None, table,
                                     bass.IndirectOffsetOnAxis(idx[:, col + k:col + k + 1], 0)
                                     ).then_inc(landed, 16)

        def scatter(v, par, n=P):
            pool.wait_ge(out_ok, v + 1)
            alone(pool, pool_passed)
            q.indirect_dma_start(out, bass.IndirectOffsetOnAxis(oid[par][0:n, :], 0), xo[par][0:n, :],
                                 None).then_inc(out_done[par], 16)

        def static_rows(w, par, half):
            degree = pool.value_load(nb_row[0:1, bass.ds(w * 2 + 1, 1)], min_val=0, max_val=E)
            pool.wait_ge(idx_staged, w + 1)
            after(pool, begin_step, (w - 1) * N_BEGIN)
            alone(pool, pool_passed)
            q.indirect_dma_start(node_row[par][:], None, node_tab,
                                 bass.IndirectOffsetOnAxis(idx_st[par][:, NS:NS + 1], 0)
                                 ).then_inc(node_landed[par], 16)
            for s in range(STATIC):
                if s % 2 == 0 and (not isinstance(w, int) or w >= 2):
                    pool.wait_ge(agg_ok, (w - 2) * 2 + (1 + s // 2))
                    alone(pool, pool_passed)
                if isinstance(w, int) and s == STATIC - 1:
                    pool.wait_ge(cleared, 1)
                lo = s * SLOTS
                buf, landed = rows[par][:, lo:lo + SLOTS, :], row_landed[par][s]
                if s < STATIC - 1:
                    gather(buf, landed, idx_st[par], lo, range(SLOTS))
                else:
                    gather(buf, landed, idx_st[par], lo, range(HALF))
                    with pool.If(degree > lo + HALF):
                        gather(buf, landed, idx_st[par], lo, range(HALF, SLOTS))

        def window(w, par, half):
            next_window(pool, static_rows, w, par, half)
            if not isinstance(w, int) or w >= 2:
                scatter(w - 2, par)
            nb, g = bt.enter(w)
            degree = pool.value_load(nb_row[0:1, bass.ds(w * 2 + 1, 1)], min_val=0, max_val=E)
            pool.wait_ge(xidx_staged, w + 1)
            alone(pool, pool_passed)

            def batch(s, i, c):
                k = i - STATIC
                pool.wait_ge(xfolded, g + (max(k, 1) + 1 if isinstance(k, int) else k + 1))
                alone(pool, pool_passed)
                idx, lo = (idx_x[par], (s - STATIC) * SLOTS) if isinstance(c, int) else (xidx, s * SLOTS)
                buf, landed = xrows[:, s % 2], xrow_landed[s % 2]
                gather(buf, landed, idx, lo, range(HALF))
                with pool.If(degree > i * SLOTS + HALF):
                    gather(buf, landed, idx, lo, range(HALF, SLOTS))

            def chunk(c):
                pool.reg_add(chunks, chunks, 1)
                n = pool.snap(chunks, min_val=1)
                pool.wait_ge(xblk_ok, n)
                alone(pool, pool_passed)
                q.indirect_dma_start(xraw[:, 0, :], None, blocks,
                                     bass.IndirectOffsetOnAxis(xblk[:], 0)).then_inc(xblk_in, 16)
                pool.wait_ge(xidx_ok, n)

            further_batches(pool, nb, batch, chunk)
            bt.leave(w, nb, g)

        static_rows(0, 0, 0)
        windows(pool, window)
        scatter(W - 2, 0)
        scatter(W - 1, 1, LAST)
        for i in range(2):
            pool.wait_ge(out_done[i], 16 * (W // 2))

    @block.vector
    def _(dve):
        v = nc.vector
        bt = Batches(dve, "dve")
        chunks = dve.alloc_register("dve_chunks")
        dve.reg_mov(chunks, 0)

        def stage(w, par):
            v.tensor_copy(idx_st[par][:, 0:NS], idx_all[:, bass.ds(w, 1), 0:NS].rearrange("p o k -> p (o k)")
                          ).then_inc(stage_step, 1)
            dve.wait_ge(stage_step, w + 1)
            v.tensor_copy(idx_st[par][:, NS:NS + 1],
                          rank_sb[:, bass.ds(w, 1), 0]).then_inc(idx_staged, 1)

        def xstage(w, par):
            v.tensor_copy(idx_x[par][:], idx_all[:, bass.ds(w, 1), NS:CHUNK].rearrange("p o k -> p (o k)")
                          ).then_inc(xidx_staged, 1)

        def begin(w, par, half):
            st = Steps(dve, begin_step, w * N_BEGIN)
            dve.wait_ge(node_landed[par], (half + 1) * 16)
            st.did(v.tensor_copy(er9[par][:, :, 0:R].rearrange("p h r -> p r h"),
                                 node_row[par][:, D:D + RH].rearrange("p (r h) -> p r h", r=R)))
            st.did(v.tensor_copy(xres[par][:], node_row[par][:, 0:D]))
            st.did(v.memset(coff[par][:], 0.0))
            st.did(v.tensor_copy(typ_cur[par][:], typ_all[:, bass.ds(w, 1), :].rearrange("p o k -> p (o k)")))
            st.did(v.tensor_scalar(valid[par][:], rank_sb[:, bass.ds(w, 1), 2], 0.0, None, ALU.is_gt))
            st.wait()
            assert st.n == N_BEGIN

        def scores(st, par, n, col, el, landed, out_e):
            hot, eh, sc = hot9[:, 0:n], er_hot[:, 0:n], score[:, 0:n]
            st.did(v.tensor_tensor(hot, bc(typ_cur[par][:, col], 2, R1), bc(slot_id[:, 0:R1], 1, n), ALU.is_equal))
            st.wait()
            st.did(v.tensor_tensor(eh, bc(er9[par][:], 1, n), bc(hot, 2, H), ALU.mult))
            st.wait()
            st.did(v.tensor_reduce(sc, eh, AX_X, ALU.add))
            st.wait()
            landed()
            st.did(v.tensor_tensor(sc, sc, el, ALU.add))
            st.wait()
            st.did(v.scalar_tensor_tensor(out=out_e.rearrange("p h k -> p k h"), in0=sc, scalar=SLOPE, in1=sc,
                                          op0=ALU.mult, op1=ALU.max))
            st.wait()

        def front(w, par, half):
            st = Steps(dve, front_step, w * N_FRONT)

            def landed():
                for s in range(STATIC - 1):
                    dve.wait_ge(row_landed[par][s], (half + 1) * (16 * SLOTS))
                dve.wait_ge(last_ready, w + 1)

            scores(st, par, NS, slice(0, NS), rows[par][:, :, AGG:ROW], landed, ebuf[:])
            st.did(v.tensor_reduce(m_win[par][:], ebuf[:], AX_X, ALU.max))
            st.wait()
            v.tensor_tensor(diff[:], ebuf[:], bc(m_win[par][:], 2, NS), ALU.subtract).then_inc(diff_ok, 1)
            dve.wait_ge(diff_ok, w + 1)
            alone(dve, dve_passed)
            assert st.n == N_FRONT

        def exps(w):
            st = Steps(dve, ex_step, w * N_EX)
            dve.wait_ge(den_ok, w + 1)
            st.did(v.reciprocal(rden[:], den[:]))
            st.wait()
            st.did(v.tensor_scalar(ex[:], rden[:], 2.0, -1.0, ALU.mult, ALU.add))
            st.wait()
            return st

        def weigh(w, par, s, st):
            lo = s * SLOTS
            r = rows[par][:, lo:lo + SLOTS, 0:AGG].rearrange("p k (h c) -> p k h c", h=H)
            st.did(v.tensor_tensor(r, r, bc(ex[:, :, lo:lo + SLOTS].rearrange("p h k -> p k h"), 3, HC), ALU.mult))
            if s % 2:
                st.wait()
                a, b = (rows[par][:, i:i + SLOTS, 0:AGG] for i in (lo - SLOTS, lo))
                v.tensor_tensor(a, a, b, ALU.add).then_inc(folded, 1)
            if s == STATIC - 1:
                assert st.n == N_EX

        def take(w, par, g):
            dve.wait_ge(xfront_step, g * N_XFRONT + 1)
            v.tensor_copy(xebuf[:, :, SLOTS], m_win[par][:]).then_inc(take_step, 1)
            dve.wait_ge(take_step, w + 1)
            dve.wait_ge(agg_ok, w * 2 + 2)
            v.tensor_copy(acc[:], agg_ps[:, 0:AGG].rearrange("p (h c) -> p h c", h=H)).then_inc(acc_ok, 1)
            dve.wait_ge(acc_ok, w + 1)
            alone(dve, dve_passed)

        def further(j, par, buf, col):
            st = Steps(dve, xfront_step, j * N_XFRONT + 1)
            st.wait()
            scores(st, par, SLOTS, col, xrows[:, buf, :, AGG:ROW], lambda: dve.wait_ge(xrows_ready, j + 1),
                   xebuf[:, :, 0:SLOTS])
            st.did(v.tensor_reduce(m_new[:], xebuf[:], AX_X, ALU.max))
            st.wait()
            v.tensor_tensor(xdiff[:], xebuf[:], bc(m_new[:], 2, S1), ALU.subtract).then_inc(xdiff_ok, 1)
            dve.wait_ge(xdiff_ok, j + 1)
            st.did(v.tensor_copy(xebuf[:, :, SLOTS], m_new[:]))
            assert st.n == N_XFRONT
            st = Steps(dve, xex_step, j * N_XEX + 1)
            dve.wait_ge(xden_ok, j + 1)
            st.did(v.reciprocal(xrden[:], xden[:]))
            st.wait()
            st.did(v.tensor_scalar(xex[:], xrden[:], 2.0, -1.0, ALU.mult, ALU.add))
            st.wait()
            r = xrows[:, buf, :, 0:AGG].rearrange("p k (h c) -> p k h c", h=H)
            st.did(v.tensor_tensor(r, r, bc(xex[:, :, 0:SLOTS].rearrange("p h k -> p k h"), 3, HC), ALU.mult))
            st.wait()
            v.tensor_tensor(xprod[:], xrows[:, buf, 0:HALF, 0:AGG], xrows[:, buf, HALF:SLOTS, 0:AGG], ALU.add
                            ).then_inc(xfolded, 1)
            st.did(v.tensor_tensor(acc[:], acc[:], bc(xex[:, :, SLOTS], 2, HC), ALU.mult))
            st.wait()
            assert st.n == N_XEX
            dve.wait_ge(xagg_ok, j + 1)
            v.tensor_tensor(acc[:], acc[:], agg_ps[:, 0:AGG].rearrange("p (h c) -> p h c", h=H), ALU.add
                            ).then_inc(xacc_step, N_XACC)
            dve.wait_ge(xacc_step, j + 2)
            alone(dve, dve_passed)

        def post(w, par, half):
            st = Steps(dve, post_step, w * N_POST)
            st.did(v.reciprocal(r4[:], acc[:, :, HD]))
            st.wait()
            st.did(v.tensor_scalar(r4[:], r4[:], valid[par][:, 0:1], None, ALU.mult))
            st.wait()
            st.did(v.tensor_tensor(hn[:].rearrange("p (h d) -> p h d", h=H), acc[:, :, 0:HD], bc(r4[:], 2, HD),
                                   ALU.mult))
            st.wait()
            after(dve, out_done[par], half * 16)
            st.did(v.tensor_tensor(xo[par][:], hn[:], xres[par][:], ALU.add))
            st.wait()
            st.did(v.bn_stats(st6[:], xo[par][:]))
            st.wait()
            alone(dve, dve_passed)
            st.did(v.bn_aggr(mv2[:], st6[:]))
            st.wait()
            st.did(v.tensor_scalar(varp[:], mv2[:, 1:2], EPS, None, ALU.add))
            st.wait()
            rsqrt_steps(nc, st, rstd2[:], varp[:], tmp1[:])
            assert st.n == N_POST, st.n
            v.tensor_scalar(z[:], xo[par][:], mv2[:, 0:1], rstd2[:, 0:1], ALU.subtract, ALU.mult).then_inc(z_ok, 1)

        def gate_in_steps(u):
            st = Steps(dve, gate_step, u * N_GATE)
            dve.wait_ge(logit_ok, u + 1)
            st.did(v.tensor_tensor(lg[:], gate_ps[:, 0:NE], gb[:], ALU.add))
            st.wait()
            alone(dve, dve_passed)
            st.did(v.max(mx8[:], lg[:]))
            st.wait()
            v.tensor_scalar(nm[:], mx8[:, 0:1], -0.5, None, ALU.mult).then_inc(gate_in, 1)
            alone(dve, dve_passed)
            st.did(v.max_index(ix8[:], mx8[:], lg[:]))
            st.wait()
            st.did(v.tensor_copy(ixf[:], ix8[:, 0:2]))
            return st

        def gate_out_steps(u, st):
            dve.wait_ge(gden_ok, u + 1)
            st.did(v.reciprocal(gp[:], gden[:]))
            st.wait()
            st.did(v.tensor_scalar(gp[:], gp[:], 2.0, -1.0, ALU.mult, ALU.add))
            st.wait()
            st.did(v.tensor_reduce(gsum[:], gp[:], AX_X, ALU.add))
            st.wait()
            st.did(v.reciprocal(gsum[:], gsum[:]))
            st.did(v.tensor_scalar(gmask[:], slot_id[:, 0:NE], ixf[:, 0:1], None, ALU.is_equal))
            st.wait()
            st.did(v.scalar_tensor_tensor(out=gmask[:], in0=slot_id[:, 0:NE], scalar=ixf[:, 1:2], in1=gmask[:],
                                          op0=ALU.is_equal, op1=ALU.add))
            st.wait()
            st.did(v.tensor_scalar(gp[:], gp[:], gsum[:, 0:1], None, ALU.mult))
            st.wait()
            assert st.n == N_GATE, st.n
            v.tensor_tensor(cw[:], gp[:], gmask[:], ALU.mult).then_inc(cw_ok, 1)

        def mix_start(u, par):
            st = Steps(dve, mix_step, u * N_MIX)
            dve.wait_ge(cw_ok, u + 1)
            dve.wait_ge(z_ok, u + 1)
            dve.wait_ge(b2_ok, u + 1)
            st.did(v.tensor_tensor(xo[par][:], xo[par][:], b2_ps, ALU.add))
            return st

        def mix(u, par, p, st):
            dve.wait_ge(w2_ok, u * NE + 2 * p + 2)
            for e in (2 * p, 2 * p + 1):
                st.wait()
                st.did(v.scalar_tensor_tensor(out=xo[par][:], in0=y_ps[p % 2][:, (e % 2) * D:(e % 2 + 1) * D],
                                              scalar=cw[:, e:e + 1], in1=xo[par][:], op0=ALU.mult, op1=ALU.add))
            st.wait()
            dve.sem_inc(y_used, 1)

        def finish(u, par, st):
            assert st.n == N_MIX
            v.tensor_copy(oid[par][:], rank_sb[:, bass.ds(u, 1), 0]).then_inc(out_ok, 1)

        def further_chunk(w, par):
            n = dve.snap(chunks, min_val=0)
            dve.reg_add(chunks, chunks, 1)
            st = Steps(dve, chunk_step, n * N_CHUNK)

            def go(ins):
                st.did(ins)
                st.wait()

            one = bass.ds(w, 1)
            go(v.tensor_scalar(coff[par][:], coff[par][:], float(CHUNK), None, ALU.add))
            go(v.tensor_tensor(xst[:], coff[par][:], rank_sb[:, one, 1], ALU.add))
            go(v.tensor_scalar(xst_i[:], xst[:], float(E), None, ALU.min))
            go(v.tensor_scalar(xblk[:].bitcast(I32), xst_i[:], 3, None, ALU.logical_shift_right))
            dve.sem_inc(xblk_ok, 1)
            for i, by in enumerate((4, 2, 1)):
                go(v.tensor_scalar(xbit_i[:, i:i + 1], xst_i[:], by, None, ALU.bitwise_and))
            go(v.tensor_copy(xbit[:, :, 0], xbit_i[:]))
            for i, by in enumerate((4, 2)):
                go(v.tensor_scalar(xbit[:, i, :], xbit[:, i, :], 1.0 / by, None, ALU.mult))
            dve.wait_ge(xblk_in, n * 16 + 16)
            shift_steps(nc, st, xidx_f[:], xraw[:], xby[:], xhalf[:], [xbit[:, i, :] for i in range(3)], CHUNK)
            go(v.tensor_copy(xidx[:], xidx_f[:, 0, :]))
            go(v.tensor_scalar(xlow[:], xidx[:].bitcast(I32), R - 1, None, ALU.bitwise_and))
            go(v.tensor_tensor(xdeg[:], rank_sb[:, one, 2], coff[par][:], ALU.subtract))
            go(v.tensor_scalar(xmask[:], slot_id[:], xdeg[:, 0:1], None, ALU.is_ge))
            go(v.scalar_tensor_tensor(out=typ_cur[par][:], in0=xmask[:], scalar=float(R), in1=xlow[:], op0=ALU.mult,
                                      op1=ALU.add))
            go(v.tensor_scalar(typ_cur[par][:], typ_cur[par][:], float(R), None, ALU.min))
            assert st.n == N_CHUNK, st.n
            dve.sem_inc(xidx_ok, 1)

        def window(w, par, half):
            nb, g = bt.enter(w)
            u, upar = w - 1, 1 - par
            ffn = not isinstance(w, int) or w > 0
            if ffn:
                gate = gate_in_steps(u)
            st = exps(w)
            if ffn:
                gate_out_steps(u, gate)
            weigh(w, par, 0, st)
            weigh(w, par, 1, st)
            weigh(w, par, 2, st)
            weigh(w, par, 3, st)
            if ffn:
                xo_st = mix_start(u, upar)
                mix(u, upar, 0, xo_st)
                mix(u, upar, 1, xo_st)
            next_window(dve, prepare, w, par, half)
            if isinstance(w, int):
                stage(w + 3, 1 - par)
            else:
                with dve.If(w < W - 3):
                    stage(within(w + 3), 1 - par)
            take(w, par, g)
            with dve.If(nb > STATIC):
                with dve.Fori(STATIC, nb) as i:
                    with dve.If(6 < (SLOTS - 1) - (i & (SLOTS - 1))):
                        further_chunk(w, par)
                    further(i - STATIC + g, par, i & 1, bass.ds((i & (SLOTS - 1)) * SLOTS, SLOTS))
            post(w, par, half)
            if ffn:
                mix(u, upar, 2, xo_st)
                mix(u, upar, 3, xo_st)
                finish(u, upar, xo_st)
            if isinstance(w, int):
                xstage(w + 2, par)
            else:
                with dve.If(w < W - 2):
                    xstage(within(w + 2), par)
            bt.leave(w, nb, g)

        def prepare(w, par, half):
            begin(w, par, half)
            front(w, par, half)

        for s in (xfront_step, xex_step, xacc_step):
            dve.sem_inc(s, 1)
        dve.sem_inc(xfolded, 2)
        stage(0, 0)
        stage(1, 1)
        xstage(0, 0)
        xstage(1, 1)
        v.memset(rows[0][:, NS - HALF:NS, :], 0.0).then_inc(clear_step, 1)
        v.memset(rows[1][:, NS - HALF:NS, :], 0.0).then_inc(clear_step, 1)
        v.memset(xrows[:, :, HALF:SLOTS, :], 0.0).then_inc(clear_step, 1)
        dve.wait_ge(clear_step, 3)
        dve.sem_inc(cleared, 1)
        dve.wait_ge(const_ok, 2)
        dve.wait_ge(const_in, 64)
        prepare(0, 0, 0)
        stage(2, 0)
        windows(dve, window)
        u = W - 1
        gate_out_steps(u, gate_in_steps(u))
        st = mix_start(u, 1)
        for p in range(PAIRS):
            mix(u, 1, p, st)
        finish(u, 1, st)

    @block.scalar
    def _(act):
        a = nc.scalar
        act.dma_start(gw[:], gate_w.rearrange("(k p) e -> p k e", p=P)).then_inc(const_in, 16)
        act.dma_start(gb[:], gate_b.partition_broadcast(P)).then_inc(const_in, 16)
        act.dma_start(b2s[:], b2).then_inc(const_in, 16)
        act.dma_start(b1t[:], b1.rearrange("e (m p) -> p e m", p=P), allow_slow_non_contiguous=True).then_inc(const_in, 16)
        act.wait_ge(const_in, 64)
        bt = Batches(act, "act")

        def den_of(n, d, d_ok, t, t_ok, out, out_ok):
            act.wait_ge(d_ok, n + 1)
            a.activation(t[:], d[:], ACT.Tanh, scale=0.5).then_inc(t_ok, 1)
            act.wait_ge(t_ok, n + 1)
            a.activation(out[:], t[:], ACT.Copy, bias=1.0, scale=-1.0).then_inc(out_ok, 1)

        def den_of_window(w, par, half):
            den_of(w, diff, diff_ok, th, th_ok, den, den_ok)

        def z_in(u):
            act.wait_ge(ztr_ok, u + 1)
            a.copy(zT[:], zt_ps[:, 0:D].rearrange("p (k n) -> p k n", k=KD)).then_inc(zT_ok, 1)

        def gate_den(u):
            act.wait_ge(gate_in, u + 1)
            a.activation(gth[:], lg[:], ACT.Tanh, bias=nm[:, 0:1], scale=0.5).then_inc(gth_ok, 1)
            act.wait_ge(gth_ok, u + 1)
            a.activation(gden[:], gth[:], ACT.Copy, bias=1.0, scale=-1.0).then_inc(gden_ok, 1)

        def gelu(u, e):
            act.wait_ge(hid_ok, u * NE + e + 1)
            after(act, w2_ok, u * NE + e - 1)
            for m in range(KH):
                a.activation(hT[e % 2][:, m, :], hid_ps[e % 2][:, m * P:(m + 1) * P], ACT.Gelu,
                             bias=b1t[:, e, m:m + 1]).then_inc(gelu_ok, 1)

        def cwt_in(u):
            act.wait_ge(cwt_ok, u + 1)
            a.copy(cwT[:], cwt_ps).then_inc(cwT_ok, 1)

        def window(w, par, half):
            nb, g = bt.enter(w)
            ffn = not isinstance(w, int) or w > 0
            u = w - 1
            if ffn:
                z_in(u)
                gelu(u, 0)
                gate_den(u)
                for e in range(1, 4):
                    gelu(u, e)
                cwt_in(u)
                for e in range(4, 6):
                    gelu(u, e)
            next_window(act, den_of_window, w, par, half)
            with act.If(nb > STATIC):
                with act.Fori(STATIC, nb) as i:
                    den_of(i - STATIC + g, xdiff, xdiff_ok, xth, xth_ok, xden, xden_ok)
            if ffn:
                for e in range(6, NE):
                    gelu(u, e)
            bt.leave(w, nb, g)

        den_of_window(0, 0, 0)
        windows(act, window)
        u = W - 1
        z_in(u)
        gelu(u, 0)
        gate_den(u)
        for e in range(1, NE):
            gelu(u, e)
            if e == 3:
                cwt_in(u)

    @block.tensor
    def _(pe):
        t = nc.tensor
        bt = Batches(pe, "pe")

        def z_turn(u):
            pe.wait_ge(z_ok, u + 1)
            for k in range(KD):
                last = t.transpose(zt_ps[:, k * P:(k + 1) * P], z[:, k * P:(k + 1) * P], ident[:])
            last.then_inc(ztr_ok, 1)
            pe.wait_ge(zT_ok, u + 1)
            for k in range(KD):
                last = t.matmul(gate_ps[:, 0:NE], zT[:, k, :], gw[:, k, :], start=(k == 0), stop=(k == KD - 1))
            last.then_inc(logit_ok, 1)

        def hidden(u, p):
            for e in (2 * p, 2 * p + 1):
                after(pe, gelu_ok, (u * NE + e - 1) * KH)
                for m in range(KH):
                    for k in range(KD):
                        last = t.matmul(hid_ps[e % 2][:, m * P:(m + 1) * P], w1[:, e, k, m * P:(m + 1) * P],
                                        zT[:, k, :], start=(k == 0), stop=(k == KD - 1))
                last.then_inc(hid_ok, 1)

        def second(u, p):
            after(pe, y_used, u * PAIRS + p - 1)
            for e in (2 * p, 2 * p + 1):
                pe.wait_ge(gelu_ok, (u * NE + e + 1) * KH)
                for k in range(KH):
                    last = t.matmul(y_ps[p % 2][:, (e % 2) * D:(e % 2 + 1) * D], hT[e % 2][:, k, :], w2[:, e, k, :],
                                    start=(k == 0), stop=(k == KH - 1))
                last.then_inc(w2_ok, 1)

        def cw_turn(u):
            pe.wait_ge(cw_ok, u + 1)
            t.transpose(cwt_ps, cw[:], ident[:]).then_inc(cwt_ok, 1)

        def b2_term(u):
            pe.wait_ge(cwT_ok, u + 1)
            t.matmul(b2_ps, cwT[:], b2s[:], start=True, stop=True).then_inc(b2_ok, 1)

        def sums(w, par, half):
            pe.wait_ge(folded, w * 2 + (half + 1))
            for k in range(SLOTS):
                last = t.matmul(agg_ps[:, 0:AGG], ident[:], rows[par][:, 2 * half * SLOTS + k, 0:AGG],
                                start=(half == 0 and k == 0), stop=(half == 1 and k == SLOTS - 1))
            last.then_inc(agg_ok, 1)

        def further_sums(j, w):
            pe.wait_ge(xfolded, j + 3)
            pe.wait_ge(acc_ok, w + 1)
            pe.wait_ge(xacc_step, j + 1)
            for k in range(HALF):
                last = t.matmul(agg_ps[:, 0:AGG], ident[:], xprod[:, k, :], start=(k == 0), stop=(k == HALF - 1))
            last.then_inc(xagg_ok, 1)

        def window(w, par, half):
            nb, g = bt.enter(w)
            ffn = not isinstance(w, int) or w > 0
            u = w - 1
            if ffn:
                z_turn(u)
                hidden(u, 0)
                second(u, 0)
                hidden(u, 1)
                cw_turn(u)
                second(u, 1)
                b2_term(u)
            sums(w, par, 0)
            sums(w, par, 1)
            if ffn:
                hidden(u, 2)
                second(u, 2)
            with pe.If(nb > STATIC):
                with pe.Fori(STATIC, nb) as i:
                    further_sums(i - STATIC + g, w)
            if ffn:
                hidden(u, 3)
                second(u, 3)
            bt.leave(w, nb, g)

        pe.wait_ge(const_in, 64)
        pe.wait_ge(w_in, 16 * NE)
        pe.wait_ge(w_in2, 16 * NE)
        windows(pe, window)
        u = W - 1
        z_turn(u)
        for p in range(PAIRS):
            hidden(u, p)
            if p == 1:
                cw_turn(u)
            second(u, p)
            if p == 1:
                b2_term(u)


_INS = ['x', 'src', 'dst', 'edge_type_8', 'L0_gnn_conv_weights', 'L0_gnn_attn_l', 'L0_gnn_attn_r', 'L0_gnn_h_bias',
        'L0_ffn_gate_w', 'L0_ffn_gate_b', 'L0_ffn_W1', 'L0_ffn_b1', 'L0_ffn_W2', 'L0_ffn_b2']


def kernel(**inputs):
    import numpy as _np
    import concourse.bacc as _bacc
    from concourse import mybir as _mybir
    from concourse.bass_utils import run_bass_kernel_spmd as _run

    nc = _bacc.Bacc("TRN2", target_bir_lowering=False, num_devices=1)
    arrays, args = {}, []
    for name in _INS:
        a = _np.ascontiguousarray(inputs[name])
        arrays[f"in_{name}_dram"] = a
        args.append(nc.dram_tensor(f"in_{name}_dram", a.shape, _mybir.dt.from_np(a.dtype), kind="ExternalInput").ap())
    args.append(nc.dram_tensor("out_dram", (3750, 256), _mybir.dt.float32, kind="ExternalOutput").ap())
    build(nc, *args)
    r = _run(nc, [arrays], core_ids=[0])
    return r.results[0]["out_dram"]
```

```python
from contextlib import ExitStack

import concourse.bass as bass
from concourse import mybir

ALU = mybir.AluOpType
ACT = mybir.ActivationFunctionType
F32 = mybir.dt.float32
I32 = mybir.dt.int32
U32 = mybir.dt.uint32
BF16 = mybir.dt.bfloat16
AX_X = mybir.AxisListType.X

P = 128
SLOTS = 8
STATIC = 5
PAIRED = 4
CHUNK = 64
BIN = 63
SEARCH = 198
MASKED = -1.0e30
EPS = 1e-5
SLOPE = 0.2


class Steps:

    def __init__(self, eng, sem, base=0):
        self.eng, self.sem, self.base, self.n = eng, sem, base, 0

    def did(self, ins):
        ins.then_inc(self.sem, 1)
        self.n += 1

    def wait(self, back=0):
        if self.n - back > 0 or not isinstance(self.base, int):
            self.eng.wait_ge(self.sem, self.base + (self.n - back))


def bc(ap, axis, n):
    ap = ap.unsqueeze(axis)
    shape = list(ap.shape)
    shape[axis] = n
    return ap.to_broadcast(shape)


def rsqrt_steps(nc, st, y, v, tmp):
    st.did(nc.vector.tensor_scalar(tmp.bitcast(I32), v.bitcast(I32), 1, None, ALU.logical_shift_right))
    st.wait()
    st.did(nc.vector.tensor_scalar(y.bitcast(I32), tmp.bitcast(I32), -1.0, 1597463007.0, ALU.mult, ALU.add))
    st.wait()
    for _ in range(3):
        st.did(nc.vector.tensor_tensor(tmp, y, y, ALU.mult))
        st.wait()
        st.did(nc.vector.tensor_tensor(tmp, tmp, v, ALU.mult))
        st.wait()
        st.did(nc.vector.tensor_scalar(tmp, tmp, -0.5, 1.5, ALU.mult, ALU.add))
        st.wait()
        st.did(nc.vector.tensor_tensor(y, y, tmp, ALU.mult))
        st.wait()


def rsqrt_column_steps(nc, st, y, v, h, t):
    st.did(nc.vector.tensor_scalar(h.bitcast(I32), v.bitcast(I32), 1, None, ALU.logical_shift_right))
    st.wait()
    st.did(nc.vector.tensor_scalar(y.bitcast(I32), h.bitcast(I32), -1.0, 1597463007.0, ALU.mult, ALU.add))
    st.wait()
    for _ in range(2):
        st.did(nc.vector.tensor_scalar(h, y, y, v, ALU.mult, ALU.mult))
        st.wait()
        st.did(nc.vector.tensor_scalar(t, h, 0.375, -1.25, ALU.mult, ALU.add))
        st.wait()
        st.did(nc.vector.tensor_scalar(t, t, h, 1.875, ALU.mult, ALU.add))
        st.wait()
        st.did(nc.vector.tensor_scalar(y, y, t, None, ALU.mult))
        st.wait()


def shift_steps(nc, st, out, block, diff, half, bits, width):
    src, bufs = block, (half, block, out)
    for i, by in enumerate((4, 2, 1)):
        n = width + by - 1
        dst = bufs[i][:, :, 0:n]
        st.did(nc.vector.tensor_tensor(diff[:, :, 0:n], src[:, :, by:by + n], src[:, :, 0:n], ALU.subtract))
        st.wait()
        st.did(nc.vector.tensor_tensor(diff[:, :, 0:n], diff[:, :, 0:n], bc(bits[i], 2, n), ALU.mult))
        st.wait()
        st.did(nc.vector.tensor_tensor(dst, diff[:, :, 0:n], src[:, :, 0:n], ALU.add))
        st.wait()
        src = bufs[i]


def build(nc, x, src, dst, etype, conv, attn_l, attn_r, h_bias, gate_w, gate_b, W1, b1, W2, b2, out):
    N, D = x.shape
    E = src.shape[0]
    R, H, _, HD = conv.shape
    NE, _, HID = W1.shape
    KD, KH = D // P, HID // P
    HC = HD + 1
    AGG = H * HC
    ROW = AGG + H
    TN = 125
    T = N // TN
    J = N // TN
    EJ = E // TN
    W = -(-N // P)
    LAST = N - (W - 1) * P
    NF = E // SEARCH
    BW = CHUNK + SLOTS
    NB = E // SLOTS + 2
    NB += -NB % 16
    GN = NB * SLOTS + BW
    NBINS = BIN + 1
    assert TN * T == N and TN * EJ == E and EJ % SEARCH == 0 and D == H * HD and R * H == 32

    table = nc.dram_tensor("table", (N * R, ROW), F32).ap()
    node_tab = nc.dram_tensor("node_tab", (N, D + R * H), F32).ap()
    first_d = nc.dram_tensor("first_d", (NF,), F32).ap()
    edge_row = nc.dram_tensor("edge_row", (GN,), F32)
    blocks = nc.dram_tensor("blocks", (NB, BW), F32).ap()
    start_d = nc.dram_tensor("start_d", (N + 1,), F32).ap()
    ranked = nc.dram_tensor("ranked", (W * P, 4), I32).ap()
    nb_d = nc.dram_tensor("nb_d", (W, 2), I32).ap()

    ctx = ExitStack()

    def sem(name):
        return ctx.enter_context(nc.semaphore(name))

    with ctx:
        def sb(name, shape, dt=F32, stack=ctx):
            return stack.enter_context(nc.sbuf_tensor(name, shape, dt))

        ident = sb("ident", [P, P])
        idx_all = sb("idx_all", [P, W, CHUNK], U32)
        typ_all = sb("typ_all", [P, W, CHUNK], BF16)
        rank_sb = sb("rank_sb", [P, W, 4], I32)
        nb_row = sb("nb_row", [1, 2 * W], I32)
        slot_id = sb("slot_id", [P, CHUNK])

        phase1(nc, sb, sem, locals())
        phase2(nc, sb, sem, locals())


def phase1(nc, sb, sem, env):
    (x, src, dst, etype, conv, attn_l, attn_r, h_bias, table, node_tab, first_d, edge_row, blocks, start_d,
     ranked, nb_d, ident, idx_all, typ_all, rank_sb, nb_row, slot_id) = (env[k] for k in (
         "x", "src", "dst", "etype", "conv", "attn_l", "attn_r", "h_bias", "table", "node_tab", "first_d",
         "edge_row", "blocks", "start_d", "ranked", "nb_d", "ident", "idx_all", "typ_all", "rank_sb", "nb_row",
         "slot_id"))
    N, D, E, R, H, HD, KD, HC, AGG, ROW, TN, T, J, EJ, W, NF, BW, NB, GN, NBINS = (env[k] for k in (
        "N", "D", "E", "R", "H", "HD", "KD", "HC", "AGG", "ROW", "TN", "T", "J", "EJ", "W", "NF", "BW", "NB", "GN",
        "NBINS"))
    RH = R * H
    FEAT = R * D
    BANK = 512
    FB = FEAT // BANK
    RB = BANK // D
    GT = 10
    SPLIT = 8
    PAD = W * P - N
    JD = 16

    ctx = ExitStack()
    with ctx:
        def t(name, shape, dt=F32):
            return sb(name, shape, dt, ctx)

        x_all = t("x_all", [TN, T, D])
        xn = [t(f"xn{i}", [TN, D]) for i in range(2)]
        xnT = [t(f"xnT{i}", [P, KD, TN]) for i in range(2)]
        wc = t("wc", [P, KD, FEAT])
        attnb = t("attnb", [P, 2, FEAT])
        wa = t("wa", [P, KD, 2 * RH])
        scratch = t("scratch", [P, FEAT])
        hb = t("hb", [TN, D])
        stage = [t(f"stage{i}", [TN, R, ROW]) for i in range(2)]
        er_all = t("er_all", [TN, T, RH])
        stats = t("stats", [TN, T, 6])
        mv = t("mv", [TN, T, 2])
        var = t("var", [TN, T])
        rstd = t("rstd", [TN, T])
        nmr = t("nmr", [TN, T])
        tmpT = t("tmpT", [TN, T])
        dst_sb = t("dst_sb", [TN, EJ], I32)
        src_sb = t("src_sb", [TN, EJ], I32)
        typ_sb = t("typ_sb", [TN, EJ], I32)
        erow = t("erow", [TN, EJ])
        firsts = t("firsts", [TN, EJ // SEARCH])
        first_b = t("first_b", [TN, NF])
        seek = t("seek", [TN, NF])
        node_i = t("node_i", [TN, J], I32)
        node_f = t("node_f", [TN, J])
        cnt = t("cnt", [TN, J])
        chunk_u = t("chunk_u", [TN, J], U32)
        inner = t("inner", [TN, J])
        start = t("start", [TN, J])
        start_n = t("start_n", [TN, J])
        deg = t("deg", [TN, J])
        edges_end = t("edges_end", [1, 1])
        bin_i = t("bin_i", [TN, NBINS], I32)
        bin_f = t("bin_f", [TN, NBINS])
        slot_i = t("slot_i", [P, CHUNK], I32)
        hot = scratch[0:TN, 0:NBINS * J].rearrange("p (b j) -> p b j", b=NBINS)
        run = t("run", [TN, NBINS, J])
        ones = t("ones", [TN, NBINS * J])
        bin_cnt = t("bin_cnt", [TN, NBINS])
        bin_st = t("bin_st", [TN, NBINS])
        lower = t("lower", [TN, TN])
        rank_f = t("rank_f", [TN, J])
        rank_u = t("rank_u", [TN, J], U32)
        info = t("info", [TN, J, 4], I32)
        zeros = t("zeros", [P, 4], I32)
        blk_u = t("blk_u", [P, W], U32)
        bit_i = t("bit_i", [P, 3, W], I32)
        bit_f = t("bit_f", [P, 3, W])
        wide = t("wide", [P, 3 * W * BW])
        dchunk = wide[0:TN, 0:J * SEARCH].bitcast(I32).rearrange("p (j e) -> p j e", j=J)
        blk, half, diff = (wide[:, i * W * BW:(i + 1) * W * BW].rearrange("p (w k) -> p w k", w=W) for i in range(3))
        seek_a = t("seek_a", [TN, NF])
        signs = t("signs", [TN, J - JD])
        node_h = t("node_h", [TN, J])
        zero_f = t("zero_f", [1, GN - E])
        deg_r = t("deg_r", [P, W])
        rank_w = t("rank_w", [W, P, 4], I32)
        mx = t("mx", [W, 1])
        nb_i = t("nb_i", [W, 2], I32)

        feat_ps = [ctx.enter_context(nc.psum_tensor(f"feat_ps{b}", [P, BANK], F32)) for b in range(FB)]
        score_ps = ctx.enter_context(nc.psum_tensor("score_ps", [P, BANK], F32))
        tr_ps = [ctx.enter_context(nc.psum_tensor(f"tr_ps{i}", [P, BANK], F32)) for i in range(2)]
        off_ps = ctx.enter_context(nc.psum_tensor("off_ps", [P, BANK], F32))

        x_in = [sem(f"x_in{g}") for g in range(T // GT)]
        dst_in, et_in, conv_in, attn_in, hb_in = (sem(n) for n in ("dst_in", "et_in", "conv_in", "attn_in", "hb_in"))
        ident0, ident_ok, pool_const, pool_mask = (sem(n) for n in ("ident0", "ident_ok", "pool_const", "pool_mask"))
        firsts_ok, first_out, first_in = sem("firsts_ok"), sem("first_out"), sem("first_in")
        erow_ok, erow_out, blocks_out = sem("erow_ok"), sem("erow_out"), sem("blocks_out")
        norm_ok, xb_ok, node_out = sem("norm_ok"), sem("xb_ok"), sem("node_out")
        ones_ok, wa_ok = sem("ones_ok"), sem("wa_ok")
        chunk_ok, chunk_in = sem("chunk_ok"), [sem(f"chunk_in{g}") for g in range(3)]
        start_ok, start_out, start_in = sem("start_ok"), sem("start_out"), sem("start_in")
        bins_ok, offs_ok, rank_ok = sem("bins_ok"), sem("offs_ok"), sem("rank_ok")
        zero_out, ranked_out, rank_in = sem("zero_out"), sem("ranked_out"), sem("rank_in")
        blk_ok, blk_in, nb_ok, nb_out, nb_in = (sem(n) for n in ("blk_ok", "blk_in", "nb_ok", "nb_out", "nb_in"))
        xn_ok, tr_ok, xnT_ok = sem("xn_ok"), sem("tr_ok"), sem("xnT_ok")
        feat_ok, score_ok = sem("feat_ok"), sem("score_ok")
        feat_free, score_free = [sem(f"feat_free{b}") for b in range(FB)], sem("score_free")
        sought, node_ok = sem("sought"), sem("node_ok")
        stage_ok, stored = sem("stage_ok"), [sem(f"stored{i}") for i in range(2)]
        dstep = sem("dstep1")

        table_v = table.rearrange("(t p r) c -> t p (r c)", t=T, p=TN)
        x_v = x.rearrange("(t p) d -> p t d", p=TN)

        block = ctx.enter_context(nc.Block())

        @block.sync
        def _(sp):
            flat = dict(p=TN)
            sp.dma_start(dst_sb[:], dst.rearrange("(p e) -> p e", **flat)).then_inc(dst_in, 16)
            sp.dma_start(x_all[:, 0:GT, :], x_v[:, 0:GT, :]).then_inc(x_in[0], 16)
            sp.wait_ge(firsts_ok, 1)
            sp.dma_start(first_d.rearrange("(p c) -> p c", **flat), firsts[:]).then_inc(first_out, 16)
            sp.wait_ge(first_out, 16)
            sp.dma_start(first_b[:], first_d.partition_broadcast(TN)).then_inc(first_in, 16)
            sp.dma_start(src_sb[:], src.rearrange("(p e) -> p e", **flat)).then_inc(et_in, 16)
            sp.dma_start(typ_sb[:], etype.rearrange("(p e) -> p e", **flat)).then_inc(et_in, 16)
            for i, a in enumerate((attn_l, attn_r)):
                sp.dma_start(attnb[:, i, :], a.rearrange("r h d -> (r h d)").partition_broadcast(P)).then_inc(attn_in, 16)
            sp.dma_start(hb[:], h_bias.partition_broadcast(TN)).then_inc(hb_in, 16)
            for g in range(1, T // GT):
                sp.dma_start(x_all[:, g * GT:(g + 1) * GT, :], x_v[:, g * GT:(g + 1) * GT, :]).then_inc(x_in[g], 16)
            sp.wait_ge(erow_ok, 1)
            sp.wait_ge(pool_const, 3)
            flat_rows = edge_row.ap()
            sp.dma_start(flat_rows[0:E].rearrange("(p e) -> p e", **flat), erow[:]).then_inc(erow_out, 16)
            sp.dma_start(flat_rows[E:GN].rearrange("(p e) -> p e", p=1), zero_f[:]).then_inc(erow_out, 16)
            sp.wait_ge(erow_out, 32)
            sp.dma_start(blocks, bass.AP(edge_row, 0, [[SLOTS, NB], [1, BW]])).then_inc(blocks_out, 16)
            sp.wait_ge(start_ok, 1)
            sp.dma_start(start_d[0:N].rearrange("(p j) -> p j", **flat), start[:]).then_inc(start_out, 16)
            sp.dma_start(start_d[N:N + 1].rearrange("(p j) -> p j", p=1), edges_end[:]).then_inc(start_out, 16)
            sp.wait_ge(start_out, 32)
            sp.dma_start(start_n[:], start_d[1:N + 1].rearrange("(p j) -> p j", **flat)).then_inc(start_in, 16)
            sp.dma_start(ranked[N:W * P, :], zeros[0:PAD, :]).then_inc(zero_out, 16)
            sp.wait_ge(zero_out, 16)
            sp.wait_ge(ranked_out, 16 * J)
            sp.dma_start(rank_sb[:], ranked.rearrange("(w p) c -> p w c", p=P)).then_inc(rank_in, 16)
            sp.dma_start(rank_w[:], ranked.rearrange("(w p) c -> w p c", p=P)).then_inc(rank_in, 16)
            sp.wait_ge(nb_ok, 1)
            sp.dma_start(nb_d, nb_i[:]).then_inc(nb_out, 16)
            sp.wait_ge(nb_out, 16)
            sp.dma_start(nb_row[:], nb_d.rearrange("(o w) c -> o (w c)", o=1)).then_inc(nb_in, 16)
            sp.wait_ge(nb_in, 16)
            sp.wait_ge(blocks_out, 16)
            for g in range(T // GT):
                sp.wait_ge(xb_ok, g + 1)
                sp.dma_start(node_tab.rearrange("(t p) d -> p t d", p=TN)[:, g * GT:(g + 1) * GT, 0:D],
                             x_all[:, g * GT:(g + 1) * GT, :]).then_inc(node_out, 16)
            sp.wait_ge(score_free, T)
            sp.dma_start(node_tab.rearrange("(t p) d -> p t d", p=TN)[:, :, D:D + RH], er_all[:]).then_inc(node_out, 16)
            sp.wait_ge(node_out, 16 * (T // GT + 1))
            for i in range(2):
                sp.wait_ge(stored[i], 16 * (T // 2))

        @block.gpsimd
        def _(pool):
            g = nc.gpsimd
            g.memset(zero_f[:], 0.0).then_inc(pool_const, 1)
            g.memset(zeros[:], 0).then_inc(pool_const, 1)
            g.memset(edges_end[:], float(E)).then_inc(pool_const, 1)
            g.memset(ident[:], 0.0).then_inc(ident0, 1)
            g.memset(lower[:], 1.0).then_inc(ident0, 1)
            pool.wait_ge(ident0, 2)
            g.affine_select(out=ident[:], in_=ident[:], compare_op=ALU.not_equal, fill=1.0, base=0,
                            pattern=[[-1, P]], channel_multiplier=1).then_inc(ident_ok, 1)
            g.affine_select(out=lower[:], in_=lower[:], compare_op=ALU.is_ge, fill=0.0, base=-1,
                            pattern=[[1, TN]], channel_multiplier=-1).then_inc(pool_mask, 1)
            g.iota(node_i[:], pattern=[[1, J]], base=0, channel_multiplier=J).then_inc(pool_const, 1)
            g.iota(bin_i[:], pattern=[[1, NBINS]], base=0, channel_multiplier=0).then_inc(pool_const, 1)
            g.iota(slot_i[:], pattern=[[1, CHUNK]], base=0, channel_multiplier=0).then_inc(pool_const, 1)
            pool.wait_ge(chunk_ok, 1)
            for j in range(J):
                g.indirect_dma_start(dchunk[:, j, :], None, dst.rearrange("(c e) -> c e", e=SEARCH),
                                     bass.IndirectOffsetOnAxis(chunk_u[:, j:j + 1], 0)).then_inc(chunk_in[j // 10], 16)
            pool.wait_ge(rank_ok, 1)
            pool.wait_ge(zero_out, 16)
            for j in range(J):
                g.indirect_dma_start(ranked, bass.IndirectOffsetOnAxis(rank_u[:, j:j + 1], 0), info[:, j, :],
                                     None).then_inc(ranked_out, 16)
            pool.wait_ge(blk_ok, 1)
            pool.wait_ge(blocks_out, 16)
            for w in range(W):
                g.indirect_dma_start(blk[:, w, :], None, blocks,
                                     bass.IndirectOffsetOnAxis(blk_u[:, w:w + 1], 0)).then_inc(blk_in, 16)
            pool.wait_ge(blk_in, 16 * W)

        @block.vector
        def _(dve):
            v = nc.vector
            st = Steps(dve, dstep)

            def go(ins):
                st.did(ins)
                st.wait()

            go(v.memset(ones[:], 1.0))
            for i in range(2):
                for h in range(H):
                    v.memset(stage[i][:, :, h * HC + HD:h * HC + HD + 1], 1.0).then_inc(ones_ok, 1)
            dve.wait_ge(dst_in, 16)
            v.tensor_copy(firsts[:], dst_sb[:].rearrange("p (c e) -> p c e", e=SEARCH)[:, :, 0]).then_inc(firsts_ok, 1)

            def norms(g):
                dve.wait_ge(x_in[g], 16)
                for i in range(g * GT, (g + 1) * GT):
                    st.did(v.bn_stats(stats[:, i, :], x_all[:, i, :]))
                st.wait()
                for i in range(g * GT, (g + 1) * GT):
                    st.did(v.bn_aggr(mv[:, i, :], stats[:, i, :]))
                st.wait()
                s = slice(g * GT, (g + 1) * GT)
                go(v.tensor_scalar(var[:, s], mv[:, s, 1], EPS, None, ALU.add))
                rsqrt_steps(nc, st, rstd[:, s], var[:, s], tmpT[:, s])
                v.scalar_tensor_tensor(out=nmr[:, s], in0=mv[:, s, 0], scalar=-1.0, in1=rstd[:, s], op0=ALU.mult,
                                       op1=ALU.mult).then_inc(norm_ok, 1)

            norms(0)
            dve.wait_ge(pool_const, 6)
            go(v.tensor_copy(node_f[:], node_i[:]))
            v.tensor_scalar(node_h[:], node_f[:], -0.5, None, ALU.add).then_inc(node_ok, 1)
            go(v.tensor_copy(bin_f[:], bin_i[:]))
            go(v.tensor_copy(slot_id[:], slot_i[:]))
            dve.wait_ge(first_in, 16)
            for j in range(JD):
                st.did(v.tensor_scalar(seek[:], first_b[:], node_f[:, j:j + 1], 0.0, ALU.is_lt, ALU.add,
                                       accum_out=cnt[:, j:j + 1]))
                st.wait()
            dve.wait_ge(sought, J - JD)
            go(v.tensor_scalar(cnt[:, JD:J], signs[:], 0.5, NF / 2, ALU.mult, ALU.add))
            go(v.tensor_scalar(cnt[:], cnt[:], -1.0, 0.0, ALU.add, ALU.max))
            v.tensor_copy(chunk_u[:], cnt[:]).then_inc(chunk_ok, 1)
            dve.wait_ge(et_in, 32)
            v.scalar_tensor_tensor(out=erow[:], in0=src_sb[:], scalar=float(R), in1=typ_sb[:], op0=ALU.mult,
                                   op1=ALU.add).then_inc(erow_ok, 1)
            dve.wait_ge(attn_in, 32)
            dve.wait_ge(conv_in, 16 * R * KD)
            for lr in range(2):
                for k in range(KD):
                    go(v.tensor_tensor(scratch[:], wc[:, k, :], attnb[:, lr, :], ALU.mult))
                    go(v.tensor_reduce(wa[:, k, lr * RH:(lr + 1) * RH],
                                       scratch[:].rearrange("p (a d) -> p a d", d=HD), AX_X, ALU.add))
            dve.sem_inc(wa_ok, 1)
            norms(1)
            norms(2)
            for j in range(J):
                if j % 10 == 0:
                    dve.wait_ge(chunk_in[j // 10], 160)
                st.did(v.tensor_scalar(seek[:, 0:SEARCH], dchunk[:, j, :], node_f[:, j:j + 1], 0.0, ALU.is_lt,
                                       ALU.add, accum_out=inner[:, j:j + 1]))
                st.wait()
            v.scalar_tensor_tensor(out=start[:], in0=cnt[:], scalar=float(SEARCH), in1=inner[:], op0=ALU.mult,
                                   op1=ALU.add).then_inc(start_ok, 1)
            dve.wait_ge(start_in, 16)
            go(v.tensor_tensor(deg[:], start_n[:], start[:], ALU.subtract))
            go(v.tensor_scalar(tmpT[:], deg[:], float(BIN), None, ALU.min))
            go(v.tensor_tensor(hot, bc(tmpT[:], 1, NBINS), bc(bin_f[:], 2, J), ALU.is_equal))
            go(v.tensor_tensor_scan(out=run[:].rearrange("p b j -> p (b j)"), data0=ones[:],
                                    data1=hot.rearrange("p b j -> p (b j)"), initial=0.0, op0=ALU.mult,
                                    op1=ALU.add))
            go(v.memset(bin_st[:, 0:1], 0.0))
            go(v.tensor_copy(bin_st[:, 1:NBINS], run[:, 0:BIN, J - 1]))
            v.tensor_tensor(bin_cnt[:], run[:, :, J - 1], bin_st[:], ALU.subtract).then_inc(bins_ok, 1)
            dve.wait_ge(offs_ok, 1)
            go(v.scalar_tensor_tensor(out=bin_cnt[:], in0=off_ps[0:TN, 0:NBINS], scalar=-1.0, in1=bin_st[:],
                                      op0=ALU.add, op1=ALU.subtract))
            go(v.tensor_tensor(run[:], run[:], bc(bin_cnt[:], 2, J), ALU.add))
            go(v.tensor_tensor(run[:], run[:], hot, ALU.mult))
            go(v.tensor_reduce(rank_f[:], run[:].rearrange("p b j -> p j b"), AX_X, ALU.add))
            go(v.tensor_copy(info[:, :, 0], node_f[:]))
            go(v.tensor_copy(info[:, :, 1], start[:]))
            go(v.tensor_copy(info[:, :, 2], deg[:]))
            go(v.memset(info[:, :, 3], 0))
            v.tensor_copy(rank_u[:], rank_f[:]).then_inc(rank_ok, 1)
            dve.wait_ge(hb_in, 16)

            def residual(g):
                dve.wait_ge(xn_ok, (g + 1) * GT)
                s = slice(g * GT, (g + 1) * GT)
                v.tensor_tensor(x_all[:, s, :], x_all[:, s, :], bc(hb[:], 1, GT), ALU.add).then_inc(xb_ok, 1)

            residual(0)
            residual(1)
            dve.wait_ge(rank_in, 32)
            v.tensor_scalar(blk_u[:].bitcast(I32), rank_sb[:, :, 1], 3, None, ALU.logical_shift_right).then_inc(blk_ok, 1)
            go(v.tensor_reduce(mx[:], rank_w[:, :, 2], AX_X, ALU.max))
            go(v.tensor_copy(nb_i[:, 1:2], mx[:]))
            go(v.tensor_scalar(nb_i[:, 0:1], mx[:], float(SLOTS - 1 - SLOTS * STATIC), 0.0, ALU.add, ALU.max))
            v.tensor_scalar(nb_i[:, 0:1], nb_i[:, 0:1], 3, None, ALU.logical_shift_right).then_inc(nb_ok, 1)
            for i, by in enumerate((4, 2, 1)):
                go(v.tensor_scalar(bit_i[:, i, :], rank_sb[:, :, 1], by, None, ALU.bitwise_and))
                go(v.tensor_scalar(bit_f[:, i, :], bit_i[:, i, :], 1.0 / by, None, ALU.mult))
            go(v.tensor_copy(deg_r[:], rank_sb[:, :, 2]))
            dve.wait_ge(blk_in, 16 * W)
            rows_f = half[:, :, 0:CHUNK]
            shift_steps(nc, st, rows_f, blk, diff, half, [bit_f[:, i, :] for i in range(3)], CHUNK)
            go(v.tensor_copy(idx_all[:], rows_f))
            low = blk[:, :, 0:CHUNK].bitcast(I32)
            go(v.tensor_scalar(low, idx_all[:].bitcast(I32), R - 1, None, ALU.bitwise_and))
            go(v.tensor_tensor(diff[:, :, 0:CHUNK], bc(slot_id[:], 1, W), bc(deg_r[:], 2, CHUNK), ALU.is_ge))
            go(v.scalar_tensor_tensor(out=rows_f, in0=diff[:, :, 0:CHUNK], scalar=float(R), in1=low,
                                      op0=ALU.mult, op1=ALU.add))
            go(v.tensor_scalar(typ_all[:], rows_f, float(R), None, ALU.min))
            residual(2)

        @block.scalar
        def _(act):
            a = nc.scalar
            for r in range(R):
                for k in range(KD):
                    act.dma_start(wc[:, k, r * D:(r + 1) * D].rearrange("p (h d) -> p h d", h=H),
                                  conv[r, :, k * P:(k + 1) * P, :].rearrange("h p d -> p h d")).then_inc(conv_in, 16)

            def normalize(i, par):
                act.wait_ge(norm_ok, i // GT + 1)
                a.activation(xn[par][:], x_all[:, bass.ds(i, 1), :].rearrange("p o d -> p (o d)"), ACT.Identity,
                             bias=nmr[:, bass.ds(i, 1)], scale=rstd[:, bass.ds(i, 1)]).then_inc(xn_ok, 1)

            def transposed(i, par):
                act.wait_ge(tr_ok, i + 1)
                if not isinstance(i, int) or i >= 2:
                    act.wait_ge(score_ok, i - 1)
                a.copy(xnT[par][:], tr_ps[par][:, 0:KD * TN].rearrange("p (k n) -> p k n", k=KD)).then_inc(xnT_ok, 1)

            def evacuate(i, par, pair, ahead):
                if ahead > 1:
                    normalize(i + 2, par)
                if not isinstance(i, int) or i >= 2:
                    act.wait_ge(stored[par], 16 * pair)
                for b in range(FB):
                    if b == FB // 2 and ahead > 0:
                        transposed(i + 1, 1 - par)
                    act.wait_ge(feat_ok, i * FB + b + 1)
                    a.copy(stage[par][:, b * RB:(b + 1) * RB, 0:AGG].rearrange("p r (h c) -> p r h c", h=H)[:, :, :, 0:HD],
                           feat_ps[b][0:TN, :].rearrange("p (r h d) -> p r h d", r=RB, h=H)).then_inc(feat_free[b], 1)
                act.wait_ge(score_ok, i + 1)
                a.copy(stage[par][:, :, AGG:ROW],
                       score_ps[0:TN, 0:RH].rearrange("p (r h) -> p r h", r=R)).then_inc(stage_ok, 1)
                a.copy(er_all[:, bass.ds(i, 1), :].rearrange("p o c -> p (o c)"),
                       score_ps[0:TN, RH:2 * RH]).then_inc(score_free, 1)
                act.wait_ge(stage_ok, i + 1)
                for b in range(FB):
                    act.wait_ge(feat_free[b], i + 1)
                act.dma_start(table_v[bass.ds(i, 1)].rearrange("o p c -> (o p) c"),
                              stage[par][:].rearrange("p r c -> p (r c)")).then_inc(stored[par], 16)

            normalize(0, 0)
            normalize(1, 1)
            transposed(0, 0)
            act.wait_ge(node_ok, 1)
            act.wait_ge(first_in, 16)
            for j in range(JD, J):
                if j > JD:
                    act.wait_ge(sought, j - JD)
                a.activation(seek_a[:], first_b[:], ACT.Sign, bias=node_h[:, j:j + 1], scale=-1.0,
                             accum_out=signs[:, j - JD:j - JD + 1]).then_inc(sought, 1)
            act.wait_ge(ones_ok, 2 * H)
            for par in range(2):
                evacuate(par, par, 0, 2)
            with act.Fori(1, T // 2 - 1) as pair:
                for par in range(2):
                    evacuate(pair * 2 + par, par, pair, 2)
            evacuate(T - 2, 0, T // 2 - 1, 1)
            evacuate(T - 1, 1, T // 2 - 1, 0)

        @block.tensor
        def _(pe):
            m = nc.tensor

            def transposes(i, par):
                pe.wait_ge(xn_ok, i + 1)
                if not isinstance(i, int) or i >= 2:
                    pe.wait_ge(xnT_ok, i - 1)
                for k in range(KD):
                    last = m.transpose(tr_ps[par][:, k * TN:(k + 1) * TN], xn[par][:, k * P:(k + 1) * P],
                                       ident[0:TN, 0:TN])
                last.then_inc(tr_ok, 1)

            def products(i, par, ahead=True):
                pe.wait_ge(xnT_ok, i + 1)
                for b in range(FB):
                    if b == FB // 2 and ahead:
                        transposes(i + 1, 1 - par)
                    if not isinstance(i, int) or i >= 1:
                        pe.wait_ge(feat_free[b], i)
                    for k in range(KD):
                        last = m.matmul(feat_ps[b][0:TN, :], xnT[par][:, k, :], wc[:, k, b * BANK:(b + 1) * BANK],
                                        start=(k == 0), stop=(k == KD - 1))
                    last.then_inc(feat_ok, 1)

            def node_scores(i, par):
                if not isinstance(i, int) or i >= 1:
                    pe.wait_ge(score_free, i)
                pe.wait_ge(wa_ok, 1)
                for k in range(KD):
                    last = m.matmul(score_ps[0:TN, 0:2 * RH], xnT[par][:, k, :], wa[:, k, :], start=(k == 0),
                                    stop=(k == KD - 1))
                last.then_inc(score_ok, 1)

            def tiles(lo, hi):
                with pe.Fori(lo, hi) as pair:
                    for par in range(2):
                        products(pair * 2 + par, par)
                        node_scores(pair * 2 + par, par)

            pe.wait_ge(ident_ok, 1)
            transposes(0, 0)
            pe.wait_ge(conv_in, 16 * R * KD)
            products(0, 0)
            products(1, 1, ahead=False)
            node_scores(0, 0)
            transposes(2, 0)
            node_scores(1, 1)
            tiles(1, SPLIT // 2)
            pe.wait_ge(bins_ok, 1)
            pe.wait_ge(pool_mask, 1)
            m.matmul(off_ps[0:TN, 0:NBINS], lower[:], bin_cnt[:], start=True, stop=False)
            m.matmul(off_ps[0:TN, 0:NBINS], ones[:, 0:TN], bin_st[:], start=False, stop=True).then_inc(offs_ok, 1)
            tiles(SPLIT // 2, T // 2 - 1)
            products(T - 2, 0)
            node_scores(T - 2, 0)
            products(T - 1, 1, ahead=False)
            node_scores(T - 1, 1)


def phase2(nc, sb, sem, env):
    (W1, b1, W2, b2, gate_w, gate_b, out, table, node_tab, blocks, ident, idx_all, typ_all, rank_sb, nb_row,
     slot_id) = (env[k] for k in (
         "W1", "b1", "W2", "b2", "gate_w", "gate_b", "out", "table", "node_tab", "blocks", "ident", "idx_all",
         "typ_all", "rank_sb", "nb_row", "slot_id"))
    N, D, E, R, H, HD, HC, AGG, ROW, W, LAST, BW, NE, HID, KD, KH = (env[k] for k in (
        "N", "D", "E", "R", "H", "HD", "HC", "AGG", "ROW", "W", "LAST", "BW", "NE", "HID", "KD", "KH"))
    RH = R * H
    R1 = R + 1
    HALF = SLOTS // 2
    STEP = 2
    NS = STATIC * SLOTS
    BY_ACT = 7
    S1 = SLOTS + 1
    PAIRS = NE // 2
    assert PAIRED == 4 and STATIC == 5 and W % 2 == 0

    N_FRONT, N_EX, N_BEGIN, N_POST, N_GATE, N_MIX = 6, 6, 5, 16, 11, 1 + NE
    N_XFRONT, N_XEX, N_CHUNK = 7, 7, 25

    rows = [sb(f"rows{i}", [P, NS, ROW]) for i in range(2)]
    xrows = sb("xrows", [P, SLOTS, ROW])
    w1 = sb("w1", [P, NE, KD, HID])
    w2 = sb("w2", [P, NE, KH, D])
    b1t = sb("b1t", [P, NE, KH])
    b2s = sb("b2s", [NE, D])
    gw = sb("gw", [P, KD, NE])
    gb = sb("gb", [P, NE])
    idx_st = [sb(f"idx_st{i}", [P, NS + 1], U32) for i in range(2)]
    idx_x = [sb(f"idx_x{i}", [P, CHUNK - NS], U32) for i in range(2)]
    xres = [sb(f"xres{i}", [P, D]) for i in range(2)]
    node_row = [sb(f"node_row{i}", [P, D + RH]) for i in range(2)]
    xo = [sb(f"xo{i}", [P, D]) for i in range(2)]
    oid = [sb(f"oid{i}", [P, 1], U32) for i in range(2)]
    typ_cur = [sb(f"typ_cur{i}", [P, CHUNK]) for i in range(2)]
    er9 = [sb(f"er9{i}", [P, H, R1]) for i in range(2)]
    hot9 = sb("hot9", [P, NS, R1])
    er_hot = sb("er_hot", [P, NS, H, R1])
    score = sb("score", [P, NS, H])
    ebuf, diff, th, den, rden, ex = (sb(n, [P, H, NS]) for n in ("ebuf", "e_diff", "th", "den", "rden", "ex"))
    xebuf, xdiff, xth, xden, xrden, xex = (sb(n, [P, H, S1]) for n in ("xebuf", "xdiff", "xth", "xden", "xrden",
                                                                       "xex"))
    m_win = [sb(f"m_win{i}", [P, H]) for i in range(2)]
    m_new = sb("m_new", [P, H])
    acc = sb("acc", [P, H, HC])
    r4 = sb("r4", [P, H])
    valid = [sb(f"valid{i}", [P, 1]) for i in range(2)]
    hn = sb("hn", [P, D])
    st6 = sb("st6", [P, 6])
    mv2 = sb("mv2", [P, 2])
    varp = sb("varp", [P, 1])
    rstd2 = sb("rstd2", [P, 1])
    hcol = sb("hcol", [P, 1])
    tmp1 = sb("tmp1", [P, 1])
    z = sb("z", [P, D])
    zT = sb("zT", [P, KD, P])
    hT = [sb(f"hT{i}", [P, KH, P]) for i in range(2)]
    lg = sb("lg", [P, NE])
    mx8 = sb("mx8", [P, NE])
    ix8 = sb("ix8", [P, NE], U32)
    ixf = sb("ixf", [P, 2])
    nm = sb("nm", [P, 1])
    gth = sb("gth", [P, NE])
    gden = sb("gden", [P, NE])
    gp = sb("gp", [P, NE])
    gsum = sb("gsum", [P, 1])
    gmask = sb("gmask", [P, NE])
    cw = sb("cw", [P, NE])
    cwT = sb("cwT", [NE, P])
    coff = [sb(f"coff{i}", [P, 1]) for i in range(2)]
    xst = sb("xst", [P, 1])
    xst_i = sb("xst_i", [P, 1], I32)
    xblk = sb("xblk", [P, 1], U32)
    xbit_i = sb("xbit_i", [P, 3], I32)
    xbit = sb("xbit", [P, 3, 1])
    xraw = sb("xraw", [P, 1, BW])
    xhalf = sb("xhalf", [P, 1, BW])
    xby = sb("xby", [P, 1, BW])
    xidx_f = sb("xidx_f", [P, 1, CHUNK])
    xidx = sb("xidx", [P, CHUNK], U32)
    xlow = sb("xlow", [P, CHUNK], I32)
    xdeg = sb("xdeg", [P, 1])
    xmask = sb("xmask", [P, CHUNK])

    def bank(name):
        return env["ctx"].enter_context(nc.psum_tensor(name, [P, 512], F32))

    hid_ps = [bank(f"hid_ps{i}") for i in range(2)]
    y_ps = [bank(f"y_ps{i}") for i in range(2)]
    agg_ps, gate_ps, zt_ps = bank("agg_ps"), bank("gate_ps"), bank("zt_ps")
    b2_ps = zt_ps[:, 256:256 + D]
    cwt_ps = gate_ps[0:NE, 128:256]

    w_in, w_in2, const_in = sem("w_in"), sem("w_in2"), sem("const_in")
    const_ok = sem("const_ok")
    idx_staged = sem("idx_staged")
    xidx_staged = sem("xidx_staged")
    row_landed = [[sem(f"row_landed{i}_{k}") for k in range(PAIRED)] for i in range(2)]
    xrow_landed = sem("xrow_landed")
    last_ready = sem("last_ready")
    xrows_ready = sem("xrows_ready")
    cleared = sem("cleared")
    node_landed = [sem(f"node_landed{i}") for i in range(2)]
    diff_ok, th_ok, den_ok = sem("diff_ok"), sem("th_ok"), sem("den_ok")
    xdiff_ok, xth_ok, xden_ok = sem("xdiff_ok"), sem("xth_ok"), sem("xden_ok")
    act_weighed = sem("act_weighed")
    folded = sem("folded")
    agg_ok = sem("agg_ok")
    acc_ok = sem("acc_ok")
    xfolded = sem("xfolded")
    z_ok, ztr_ok, zT_ok = sem("z_ok"), sem("ztr_ok"), sem("zT_ok")
    logit_ok, gate_in, gth_ok, gden_ok, cw_ok, cwt_ok, cwT_ok, b2_ok = (sem(n) for n in (
        "logit_ok", "gate_in", "gth_ok", "gden_ok", "cw_ok", "cwt_ok", "cwT_ok", "b2_ok"))
    hid_ok, gelu_ok, w2_ok = sem("hid_ok"), sem("gelu_ok"), sem("w2_ok")
    out_ok, out_done = sem("out_ok"), [sem(f"out_done{i}") for i in range(2)]
    pool_passed, dve_passed = sem("pool_passed"), sem("dve_passed")
    clear_step = sem("clear_step")
    xblk_ok, xblk_in, xidx_ok = sem("xblk_ok"), sem("xblk_in"), sem("xidx_ok")
    (front_step, ex_step, begin_step, post_step, gate_step, mix_step, chunk_step, stage_step) = (
        sem(n) for n in ("front_step", "ex_step", "begin_step", "post_step", "gate_step", "mix_step",
                         "chunk_step", "stage_step"))
    xfront_step, xex_step = sem("xfront_step"), sem("xex_step")

    def after(eng, s, value):
        if not isinstance(value, int) or value > 0:
            eng.wait_ge(s, value)

    def windows(eng, window):
        for w in range(2):
            window(w, w, 0)
        with eng.Fori(1, W // 2) as j:
            for par in range(2):
                window(j * 2 + par, par, j)

    def within(w):
        return nc.s_assert_within(w, 2, W - 1, skip_runtime_bounds_check_because="the If around it bounds it")

    def next_window(eng, act_on, w, par, half):
        if isinstance(w, int) or par == 0:
            act_on(w + 1, 1 - par, half + par)
        else:
            with eng.If(w < W - 1):
                act_on(within(w + 1), 1 - par, half + par)

    def alone(eng, passed):
        eng.sem_inc(passed, 1)

    class Batches:

        def __init__(self, eng, name):
            self.eng = eng
            self.total = eng.alloc_register(f"{name}_total")
            eng.reg_mov(self.total, 0)

        def enter(self, w):
            more = self.eng.value_load(nb_row[0:1, bass.ds(w * 2, 1)], min_val=0, max_val=E // SLOTS + 1 - STATIC)
            return more + STATIC, (0 if isinstance(w, int) and w == 0 else self.eng.snap(self.total, min_val=0))

        def leave(self, w, nb, g):
            self.eng.reg_mov(self.total, (nb - STATIC) + g)

    def further_batches(eng, nb, batch, chunk):
        def chain(s, c, left):
            if s == SLOTS:
                return
            with eng.If(left > s):
                batch(s, c * SLOTS + s if not isinstance(c, int) else s, c)
                chain(s + 1, c, left)

        chain(STATIC, 0, nb)
        with eng.If(nb > SLOTS):
            with eng.Fori(1, (nb + (SLOTS - 1)) >> 3) as c:
                chunk(c)
                chain(0, c, nb - c * SLOTS)

    block = env["ctx"].enter_context(nc.Block())

    @block.sync
    def _(sp):
        w1_v = W1.rearrange("e (k p) n -> p e k n", p=P)
        w2_v = W2.rearrange("e (k p) n -> p e k n", p=P)
        for e in range(NE):
            sp.dma_start(w1[:, e], w1_v[:, e]).then_inc(w_in, 16)
            sp.dma_start(w2[:, e], w2_v[:, e]).then_inc(w_in2, 16)
        bt = Batches(sp, "sp")
        xuses = sp.alloc_register("xuses")
        uses = [sp.alloc_register(f"uses{i}") for i in range(2)]
        for reg in [xuses] + uses:
            sp.reg_mov(reg, 0)

        def relay(use, landed, degree, limits, slots, ready):
            sp.reg_add(use, use, 16 * HALF)
            for limit in limits:
                with sp.If(degree > limit):
                    sp.reg_add(use, use, 16 * slots)
            sp.wait_ge(landed, sp.snap(use, min_val=16 * HALF))
            sp.sem_inc(ready, 1)

        def degree_of(w):
            return sp.value_load(nb_row[0:1, bass.ds(w * 2 + 1, 1)], min_val=0, max_val=E)

        def last_static(w, par, half):
            relay(uses[par], row_landed[par][PAIRED - 1], degree_of(w), range(NS - 3 * HALF, NS, STEP), STEP,
                  last_ready)

        def window(w, par, half):
            nb, g = bt.enter(w)

            next_window(sp, last_static, w, par, half)
            degree = degree_of(w)

            def batch(s, i, c):
                relay(xuses, xrow_landed, degree, [i * SLOTS + HALF], HALF, xrows_ready)

            further_batches(sp, nb, batch, lambda c: None)
            bt.leave(w, nb, g)

        last_static(0, 0, 0)
        windows(sp, window)

    @block.gpsimd
    def _(pool):
        q = nc.gpsimd
        for i in range(2):
            q.memset(er9[i][:], MASKED).then_inc(const_ok, 1)
        bt = Batches(pool, "pool")
        chunks = pool.alloc_register("pool_chunks")
        pool.reg_mov(chunks, 0)

        def gather(buf, landed, idx, slots, col=0):
            for k in slots:
                q.indirect_dma_start(buf[:, k, :], None, table,
                                     bass.IndirectOffsetOnAxis(idx[:, col + k:col + k + 1], 0)
                                     ).then_inc(landed, 16)

        def scatter(v, par, n=P):
            pool.wait_ge(out_ok, v + 1)
            alone(pool, pool_passed)
            q.indirect_dma_start(out, bass.IndirectOffsetOnAxis(oid[par][0:n, :], 0), xo[par][0:n, :],
                                 None).then_inc(out_done[par], 16)

        def static_rows(w, par, half):
            degree = pool.value_load(nb_row[0:1, bass.ds(w * 2 + 1, 1)], min_val=0, max_val=E)
            pool.wait_ge(idx_staged, w + 1)
            after(pool, begin_step, (w - 1) * N_BEGIN)
            alone(pool, pool_passed)
            q.indirect_dma_start(node_row[par][:], None, node_tab,
                                 bass.IndirectOffsetOnAxis(idx_st[par][:, NS:NS + 1], 0)
                                 ).then_inc(node_landed[par], 16)
            for n, s in enumerate((1, 3, 2, 0)):
                if not isinstance(w, int) or w >= 2:
                    if s:
                        pool.wait_ge(folded, (w - 2) * 3 + (n + 1))
                    else:
                        pool.wait_ge(agg_ok, w - 1)
                    alone(pool, pool_passed)
                lo = s * SLOTS
                gather(rows[par], row_landed[par][s], idx_st[par], range(lo, lo + (HALF if s == 3 else SLOTS)))
            if isinstance(w, int):
                pool.wait_ge(cleared, 1)

            def more(lo):
                if lo < NS:
                    with pool.If(degree > lo):
                        gather(rows[par], row_landed[par][PAIRED - 1], idx_st[par], range(lo, lo + STEP))
                        more(lo + STEP)

            more(NS - 3 * HALF)

        def window(w, par, half):
            next_window(pool, static_rows, w, par, half)
            if not isinstance(w, int) or w >= 2:
                scatter(w - 2, par)
            nb, g = bt.enter(w)
            degree = pool.value_load(nb_row[0:1, bass.ds(w * 2 + 1, 1)], min_val=0, max_val=E)
            pool.wait_ge(xidx_staged, w + 1)
            alone(pool, pool_passed)

            def batch(s, i, c):
                pool.wait_ge(xfolded, g + (i - STATIC + 1))
                alone(pool, pool_passed)
                idx, lo = (idx_x[par], (s - STATIC) * SLOTS) if isinstance(c, int) else (xidx, s * SLOTS)
                gather(xrows, xrow_landed, idx, range(HALF), lo)
                with pool.If(degree > i * SLOTS + HALF):
                    gather(xrows, xrow_landed, idx, range(HALF, SLOTS), lo)

            def chunk(c):
                pool.reg_add(chunks, chunks, 1)
                n = pool.snap(chunks, min_val=1)
                pool.wait_ge(xblk_ok, n)
                alone(pool, pool_passed)
                q.indirect_dma_start(xraw[:, 0, :], None, blocks,
                                     bass.IndirectOffsetOnAxis(xblk[:], 0)).then_inc(xblk_in, 16)
                pool.wait_ge(xidx_ok, n)

            further_batches(pool, nb, batch, chunk)
            bt.leave(w, nb, g)

        static_rows(0, 0, 0)
        windows(pool, window)
        scatter(W - 2, 0)
        scatter(W - 1, 1, LAST)
        for i in range(2):
            pool.wait_ge(out_done[i], 16 * (W // 2))

    @block.vector
    def _(dve):
        v = nc.vector
        bt = Batches(dve, "dve")
        chunks = dve.alloc_register("dve_chunks")
        dve.reg_mov(chunks, 0)

        def begin(w, par, half):
            st = Steps(dve, begin_step, w * N_BEGIN)
            dve.wait_ge(node_landed[par], (half + 1) * 16)
            st.did(v.tensor_copy(er9[par][:, :, 0:R].rearrange("p h r -> p r h"),
                                 node_row[par][:, D:D + RH].rearrange("p (r h) -> p r h", r=R)))
            st.did(v.tensor_copy(xres[par][:], node_row[par][:, 0:D]))
            st.did(v.memset(coff[par][:], 0.0))
            st.did(v.tensor_copy(typ_cur[par][:], typ_all[:, bass.ds(w, 1), :].rearrange("p o k -> p (o k)")))
            st.did(v.tensor_scalar(valid[par][:], rank_sb[:, bass.ds(w, 1), 2], 0.0, None, ALU.is_gt))
            st.wait()
            assert st.n == N_BEGIN

        def scores(st, par, n, col, el, landed, out_e):
            hot, eh, sc = hot9[:, 0:n], er_hot[:, 0:n], score[:, 0:n]
            st.did(v.tensor_tensor(hot, bc(typ_cur[par][:, col], 2, R1), bc(slot_id[:, 0:R1], 1, n), ALU.is_equal))
            st.wait()
            st.did(v.tensor_tensor(eh, bc(er9[par][:], 1, n), bc(hot, 2, H), ALU.mult))
            st.wait()
            st.did(v.tensor_reduce(sc, eh, AX_X, ALU.add))
            st.wait()
            landed()
            st.did(v.tensor_tensor(sc, sc, el, ALU.add))
            st.wait()
            st.did(v.scalar_tensor_tensor(out=out_e.rearrange("p h k -> p k h"), in0=sc, scalar=SLOPE, in1=sc,
                                          op0=ALU.mult, op1=ALU.max))
            st.wait()

        def front(w, par, half):
            st = Steps(dve, front_step, w * N_FRONT)

            def landed():
                for s in range(PAIRED - 1):
                    dve.wait_ge(row_landed[par][s], (half + 1) * (16 * SLOTS))
                dve.wait_ge(last_ready, w + 1)

            scores(st, par, NS, slice(0, NS), rows[par][:, :, AGG:ROW], landed, ebuf[:])
            st.did(v.tensor_reduce(m_win[par][:], ebuf[:], AX_X, ALU.max))
            st.wait()
            v.tensor_tensor(diff[:], ebuf[:], bc(m_win[par][:], 2, NS), ALU.subtract).then_inc(diff_ok, 1)
            dve.wait_ge(diff_ok, w + 1)
            alone(dve, dve_passed)
            assert st.n == N_FRONT

        def exps(w):
            st = Steps(dve, ex_step, w * N_EX)
            dve.wait_ge(den_ok, w + 1)
            st.did(v.reciprocal(rden[:], den[:]))
            st.wait()
            st.did(v.tensor_scalar(ex[:], rden[:], 2.0, -1.0, ALU.mult, ALU.add))
            st.wait()
            return st

        def weighted(par, s, skip=0):
            lo, hi = s * SLOTS + skip, (s + 1) * SLOTS
            r = rows[par][:, lo:hi, 0:AGG].rearrange("p k (h c) -> p k h c", h=H)
            return v.tensor_tensor(r, r, bc(ex[:, :, lo:hi].rearrange("p h k -> p k h"), 3, HC), ALU.mult)

        def fold(par, s, t):
            a, b = (rows[par][:, i * SLOTS:(i + 1) * SLOTS, 0:AGG] for i in (s, t))
            return v.tensor_tensor(a, a, b, ALU.add)

        def weigh_all(w, par, st, gate, between):
            st.did(weighted(par, 0))
            for _ in range(2):
                next(gate, None)
            st.did(weighted(par, 1))
            degree = dve.value_load(nb_row[0:1, bass.ds(w * 2 + 1, 1)], min_val=0, max_val=E)
            for _ in range(3):
                next(gate, None)
            st.wait()
            alone(dve, dve_passed)
            with dve.If(degree > PAIRED * SLOTS):
                weighted(par, PAIRED)
                dve.drain()
                fold(par, 0, PAIRED)
                dve.drain()
            fold(par, 0, 1).then_inc(folded, 1)
            for _ in gate:
                pass
            st.did(weighted(par, 2))
            st.did(weighted(par, 3, BY_ACT))
            st.wait()
            dve.wait_ge(act_weighed, w + 1)
            fold(par, 2, 3).then_inc(folded, 1)
            between()
            dve.wait_ge(folded, w * 3 + 2)
            fold(par, 0, 2).then_inc(folded, 1)
            assert st.n == N_EX

        def take(w):
            dve.wait_ge(agg_ok, w + 1)
            v.tensor_copy(acc[:], agg_ps[:, 0:AGG].rearrange("p (h c) -> p h c", h=H)).then_inc(acc_ok, 1)
            dve.wait_ge(acc_ok, w + 1)
            alone(dve, dve_passed)

        def further(j, par, col):
            st = Steps(dve, xfront_step, j * N_XFRONT + 1)
            st.wait()
            scores(st, par, SLOTS, col, xrows[:, :, AGG:ROW], lambda: dve.wait_ge(xrows_ready, j + 1),
                   xebuf[:, :, 0:SLOTS])
            st.did(v.tensor_reduce(m_new[:], xebuf[:], AX_X, ALU.max))
            st.wait()
            v.tensor_tensor(xdiff[:], xebuf[:], bc(m_new[:], 2, S1), ALU.subtract).then_inc(xdiff_ok, 1)
            dve.wait_ge(xdiff_ok, j + 1)
            st.did(v.tensor_copy(xebuf[:, :, SLOTS], m_new[:]))
            assert st.n == N_XFRONT
            st = Steps(dve, xex_step, j * N_XEX + 1)
            dve.wait_ge(xden_ok, j + 1)
            st.did(v.reciprocal(xrden[:], xden[:]))
            st.wait()
            st.did(v.tensor_scalar(xex[:], xrden[:], 2.0, -1.0, ALU.mult, ALU.add))
            st.wait()
            r = xrows[:, :, 0:AGG].rearrange("p k (h c) -> p k h c", h=H)
            st.did(v.tensor_tensor(r, r, bc(xex[:, :, 0:SLOTS].rearrange("p h k -> p k h"), 3, HC), ALU.mult))
            st.wait()
            st.did(v.tensor_tensor(acc[:], acc[:], bc(xex[:, :, SLOTS], 2, HC), ALU.mult))
            for n in (4, 2, 1):
                st.did(v.tensor_tensor(xrows[:, 0:n, 0:AGG], xrows[:, 0:n, 0:AGG], xrows[:, n:2 * n, 0:AGG], ALU.add))
                st.wait()
            assert st.n == N_XEX
            v.tensor_tensor(acc[:], acc[:], xrows[:, 0, 0:AGG].rearrange("p (h c) -> p h c", h=H), ALU.add
                            ).then_inc(xfolded, 1)
            dve.wait_ge(xfolded, j + 2)
            alone(dve, dve_passed)

        def post(w, par, half):
            st = Steps(dve, post_step, w * N_POST)
            st.did(v.reciprocal(r4[:], acc[:, :, HD]))
            st.wait()
            st.did(v.tensor_tensor(hn[:].rearrange("p (h d) -> p h d", h=H), acc[:, :, 0:HD], bc(r4[:], 2, HD),
                                   ALU.mult))
            st.wait()
            after(dve, out_done[par], half * 16)
            st.did(v.scalar_tensor_tensor(out=xo[par][:], in0=hn[:], scalar=valid[par][:, 0:1], in1=xres[par][:],
                                          op0=ALU.mult, op1=ALU.add))
            st.wait()
            st.did(v.bn_stats(st6[:], xo[par][:]))
            st.wait()
            alone(dve, dve_passed)
            st.did(v.bn_aggr(mv2[:], st6[:]))
            st.wait()
            st.did(v.tensor_scalar(varp[:], mv2[:, 1:2], EPS, None, ALU.add))
            st.wait()
            rsqrt_column_steps(nc, st, rstd2[:], varp[:], hcol[:], tmp1[:])
            assert st.n == N_POST, st.n
            v.tensor_scalar(z[:], xo[par][:], mv2[:, 0:1], rstd2[:, 0:1], ALU.subtract, ALU.mult).then_inc(z_ok, 1)

        def gate_in_steps(u):
            st = Steps(dve, gate_step, u * N_GATE)
            dve.wait_ge(logit_ok, u + 1)
            st.did(v.tensor_tensor(lg[:], gate_ps[:, 0:NE], gb[:], ALU.add))
            st.wait()
            alone(dve, dve_passed)
            st.did(v.max(mx8[:], lg[:]))
            st.wait()
            v.tensor_scalar(nm[:], mx8[:, 0:1], -0.5, None, ALU.mult).then_inc(gate_in, 1)
            alone(dve, dve_passed)
            st.did(v.max_index(ix8[:], mx8[:], lg[:]))
            st.wait()
            st.did(v.tensor_copy(ixf[:], ix8[:, 0:2]))
            return st

        def gate_out_steps(u, st):
            dve.wait_ge(gden_ok, u + 1)
            st.did(v.reciprocal(gp[:], gden[:]))
            yield
            st.wait()
            st.did(v.tensor_scalar(gp[:], gp[:], 2.0, -1.0, ALU.mult, ALU.add))
            yield
            st.wait()
            st.did(v.tensor_reduce(gsum[:], gp[:], AX_X, ALU.add))
            yield
            st.wait()
            st.did(v.reciprocal(gsum[:], gsum[:]))
            st.did(v.tensor_scalar(gmask[:], slot_id[:, 0:NE], ixf[:, 0:1], None, ALU.is_equal))
            yield
            st.wait()
            st.did(v.scalar_tensor_tensor(out=gmask[:], in0=slot_id[:, 0:NE], scalar=ixf[:, 1:2], in1=gmask[:],
                                          op0=ALU.is_equal, op1=ALU.add))
            yield
            st.wait()
            st.did(v.tensor_scalar(gp[:], gp[:], gsum[:, 0:1], None, ALU.mult))
            yield
            st.wait()
            assert st.n == N_GATE, st.n
            v.tensor_tensor(cw[:], gp[:], gmask[:], ALU.mult).then_inc(cw_ok, 1)

        def mix_start(u, par):
            st = Steps(dve, mix_step, u * N_MIX)
            dve.wait_ge(cw_ok, u + 1)
            dve.wait_ge(z_ok, u + 1)
            dve.wait_ge(b2_ok, u + 1)
            st.did(v.tensor_tensor(xo[par][:], xo[par][:], b2_ps, ALU.add))
            return st

        def mix(u, par, p, st, n=P):
            dve.wait_ge(w2_ok, u * NE + 2 * p + 2)
            for e in (2 * p, 2 * p + 1):
                st.wait()
                st.did(v.scalar_tensor_tensor(out=xo[par][0:n], in0=y_ps[p % 2][0:n, (e % 2) * D:(e % 2 + 1) * D],
                                              scalar=cw[0:n, e:e + 1], in1=xo[par][0:n], op0=ALU.mult, op1=ALU.add))

        def finish(u, par, st):
            assert st.n == N_MIX
            st.wait()
            v.tensor_copy(oid[par][:], rank_sb[:, bass.ds(u, 1), 0]).then_inc(out_ok, 1)

        def further_chunk(w, par):
            n = dve.snap(chunks, min_val=0)
            dve.reg_add(chunks, chunks, 1)
            st = Steps(dve, chunk_step, n * N_CHUNK)

            def go(ins):
                st.did(ins)
                st.wait()

            one = bass.ds(w, 1)
            go(v.tensor_scalar(coff[par][:], coff[par][:], float(CHUNK), None, ALU.add))
            go(v.tensor_tensor(xst[:], coff[par][:], rank_sb[:, one, 1], ALU.add))
            go(v.tensor_scalar(xst_i[:], xst[:], float(E), None, ALU.min))
            go(v.tensor_scalar(xblk[:].bitcast(I32), xst_i[:], 3, None, ALU.logical_shift_right))
            dve.sem_inc(xblk_ok, 1)
            for i, by in enumerate((4, 2, 1)):
                go(v.tensor_scalar(xbit_i[:, i:i + 1], xst_i[:], by, None, ALU.bitwise_and))
            go(v.tensor_copy(xbit[:, :, 0], xbit_i[:]))
            for i, by in enumerate((4, 2)):
                go(v.tensor_scalar(xbit[:, i, :], xbit[:, i, :], 1.0 / by, None, ALU.mult))
            dve.wait_ge(xblk_in, n * 16 + 16)
            shift_steps(nc, st, xidx_f[:], xraw[:], xby[:], xhalf[:], [xbit[:, i, :] for i in range(3)], CHUNK)
            go(v.tensor_copy(xidx[:], xidx_f[:, 0, :]))
            go(v.tensor_scalar(xlow[:], xidx[:].bitcast(I32), R - 1, None, ALU.bitwise_and))
            go(v.tensor_tensor(xdeg[:], rank_sb[:, one, 2], coff[par][:], ALU.subtract))
            go(v.tensor_scalar(xmask[:], slot_id[:], xdeg[:, 0:1], None, ALU.is_ge))
            go(v.scalar_tensor_tensor(out=typ_cur[par][:], in0=xmask[:], scalar=float(R), in1=xlow[:], op0=ALU.mult,
                                      op1=ALU.add))
            go(v.tensor_scalar(typ_cur[par][:], typ_cur[par][:], float(R), None, ALU.min))
            assert st.n == N_CHUNK, st.n
            dve.sem_inc(xidx_ok, 1)

        def window(w, par, half):
            u, upar = w - 1, 1 - par
            ffn = not isinstance(w, int) or w > 0
            if ffn:
                gate = gate_in_steps(u)
            st = exps(w)
            kept = {}

            def first_mix():
                kept["counts"] = bt.enter(w)
                if ffn:
                    kept["mix"] = mix_start(u, upar)
                    mix(u, upar, 0, kept["mix"])

            weigh_all(w, par, st, gate_out_steps(u, gate) if ffn else iter(()), first_mix)
            nb, g = kept["counts"]
            if ffn:
                xo_st = kept["mix"]
                mix(u, upar, 1, xo_st)
            next_window(dve, prepare, w, par, half)
            take(w)
            with dve.If(nb > STATIC):
                dve.drain()
                v.tensor_copy(xebuf[:, :, SLOTS], m_win[par][:])
                dve.drain()
                with dve.Fori(STATIC, nb) as i:
                    with dve.If(6 < (SLOTS - 1) - (i & (SLOTS - 1))):
                        further_chunk(w, par)
                    further(i - STATIC + g, par, bass.ds((i & (SLOTS - 1)) * SLOTS, SLOTS))
            post(w, par, half)
            if ffn:
                mix(u, upar, 2, xo_st)
                mix(u, upar, 3, xo_st)
                finish(u, upar, xo_st)
            bt.leave(w, nb, g)

        def prepare(w, par, half):
            begin(w, par, half)
            front(w, par, half)

        for s in (xfront_step, xex_step):
            dve.sem_inc(s, 1)
        dve.sem_inc(xfolded, 1)
        v.memset(rows[0][:, NS - 3 * HALF:NS, :], 0.0).then_inc(clear_step, 1)
        v.memset(rows[1][:, NS - 3 * HALF:NS, :], 0.0).then_inc(clear_step, 1)
        v.memset(xrows[:, HALF:SLOTS, :], 0.0).then_inc(clear_step, 1)
        dve.wait_ge(clear_step, 3)
        dve.sem_inc(cleared, 1)
        dve.wait_ge(const_ok, 2)
        dve.wait_ge(const_in, 64)
        prepare(0, 0, 0)
        windows(dve, window)
        u = W - 1
        for _ in gate_out_steps(u, gate_in_steps(u)):
            pass
        st = mix_start(u, 1)
        for p in range(PAIRS):
            mix(u, 1, p, st, LAST)
        finish(u, 1, st)

    @block.scalar
    def _(act):
        a = nc.scalar

        def stage(w, par):
            a.copy(idx_st[par][:, 0:NS], idx_all[:, bass.ds(w, 1), 0:NS].rearrange("p o k -> p (o k)")
                   ).then_inc(stage_step, 1)
            act.wait_ge(stage_step, w + 1)
            a.copy(idx_st[par][:, NS:NS + 1],
                   rank_sb[:, bass.ds(w, 1), 0]).then_inc(idx_staged, 1)

        def xstage(w, par):
            a.copy(idx_x[par][:], idx_all[:, bass.ds(w, 1), NS:CHUNK].rearrange("p o k -> p (o k)")
                   ).then_inc(xidx_staged, 1)

        stage(0, 0)
        stage(1, 1)
        xstage(0, 0)
        xstage(1, 1)
        act.dma_start(gw[:], gate_w.rearrange("(k p) e -> p k e", p=P)).then_inc(const_in, 16)
        act.dma_start(gb[:], gate_b.partition_broadcast(P)).then_inc(const_in, 16)
        act.dma_start(b2s[:], b2).then_inc(const_in, 16)
        act.dma_start(b1t[:], b1.rearrange("e (m p) -> p e m", p=P), allow_slow_non_contiguous=True).then_inc(const_in, 16)
        act.wait_ge(const_in, 64)
        bt = Batches(act, "act")

        def den_of(n, d, d_ok, t, t_ok, out, out_ok):
            act.wait_ge(d_ok, n + 1)
            a.activation(t[:], d[:], ACT.Tanh, scale=0.5).then_inc(t_ok, 1)
            act.wait_ge(t_ok, n + 1)
            a.activation(out[:], t[:], ACT.Copy, bias=1.0, scale=-1.0).then_inc(out_ok, 1)

        def den_of_window(w, par, half):
            den_of(w, diff, diff_ok, th, th_ok, den, den_ok)

        def z_in(u):
            act.wait_ge(ztr_ok, u + 1)
            a.copy(zT[:], zt_ps[:, 0:D].rearrange("p (k n) -> p k n", k=KD)).then_inc(zT_ok, 1)

        def gate_den(u):
            act.wait_ge(gate_in, u + 1)
            a.activation(gth[:], lg[:], ACT.Tanh, bias=nm[:, 0:1], scale=0.5).then_inc(gth_ok, 1)
            act.wait_ge(gth_ok, u + 1)
            a.activation(gden[:], gth[:], ACT.Copy, bias=1.0, scale=-1.0).then_inc(gden_ok, 1)

        def gelu(u, e, n=P):
            act.wait_ge(hid_ok, u * NE + e + 1)
            after(act, w2_ok, u * NE + e - 1)
            for m in range(KH):
                a.activation(hT[e % 2][:, m, 0:n], hid_ps[e % 2][:, m * P:m * P + n], ACT.Gelu,
                             bias=b1t[:, e, m:m + 1]).then_inc(gelu_ok, 1)

        def weigh(w, par, lo, hi):
            if lo == 0:
                act.wait_ge(ex_step, w * N_EX + 2)
            for k in range((PAIRED - 1) * SLOTS + lo, (PAIRED - 1) * SLOTS + hi):
                for h in range(H):
                    r = rows[par][:, k, h * HC:(h + 1) * HC]
                    last = a.activation(r, r, ACT.Copy, scale=ex[:, h, k:k + 1])
            if hi == BY_ACT:
                last.then_inc(act_weighed, 1)

        def cwt_in(u):
            act.wait_ge(cwt_ok, u + 1)
            a.copy(cwT[:], cwt_ps).then_inc(cwT_ok, 1)

        def window(w, par, half):
            ffn = not isinstance(w, int) or w > 0
            u = w - 1
            if ffn:
                z_in(u)
                gelu(u, 0)
                gate_den(u)
                gelu(u, 1)
                weigh(w, par, 0, 3)
                gelu(u, 2)
                weigh(w, par, 3, 5)
                gelu(u, 3)
                weigh(w, par, 5, BY_ACT)
                cwt_in(u)
                for e in range(4, 6):
                    gelu(u, e)
            else:
                weigh(w, par, 0, BY_ACT)
            nb, g = bt.enter(w)
            next_window(act, den_of_window, w, par, half)
            if isinstance(w, int):
                stage(w + 3, 1 - par)
            else:
                with act.If(w < W - 3):
                    stage(within(w + 3), 1 - par)
            with act.If(nb > STATIC):
                with act.Fori(STATIC, nb) as i:
                    den_of(i - STATIC + g, xdiff, xdiff_ok, xth, xth_ok, xden, xden_ok)
            if isinstance(w, int):
                xstage(w + 2, par)
            else:
                with act.If(w < W - 2):
                    xstage(within(w + 2), par)
            if ffn:
                for e in range(6, NE):
                    gelu(u, e)
            bt.leave(w, nb, g)

        den_of_window(0, 0, 0)
        stage(2, 0)
        windows(act, window)
        u = W - 1
        z_in(u)
        gelu(u, 0, LAST)
        gate_den(u)
        for e in range(1, NE):
            gelu(u, e, LAST)
            if e == 3:
                cwt_in(u)

    @block.tensor
    def _(pe):
        t = nc.tensor

        def z_turn(u):
            pe.wait_ge(z_ok, u + 1)
            for k in range(KD):
                last = t.transpose(zt_ps[:, k * P:(k + 1) * P], z[:, k * P:(k + 1) * P], ident[:])
            last.then_inc(ztr_ok, 1)
            pe.wait_ge(zT_ok, u + 1)
            for k in range(KD):
                last = t.matmul(gate_ps[:, 0:NE], zT[:, k, :], gw[:, k, :], start=(k == 0), stop=(k == KD - 1))
            last.then_inc(logit_ok, 1)

        def hidden(u, e, n=P):
            after(pe, gelu_ok, (u * NE + e - 1) * KH)
            for m in range(KH):
                for k in range(KD):
                    last = t.matmul(hid_ps[e % 2][:, m * P:m * P + n], w1[:, e, k, m * P:(m + 1) * P],
                                    zT[:, k, 0:n], start=(k == 0), stop=(k == KD - 1))
            last.then_inc(hid_ok, 1)

        def second(u, p, n=P):
            if p >= 2:
                pe.wait_ge(mix_step, u * N_MIX + 2 * p - 1)
            elif not isinstance(u, int) or u > 0:
                pe.wait_ge(mix_step, (u - 1) * N_MIX + 2 * p + 7)
            for e in (2 * p, 2 * p + 1):
                pe.wait_ge(gelu_ok, (u * NE + e + 1) * KH)
                for k in range(KH):
                    last = t.matmul(y_ps[p % 2][0:n, (e % 2) * D:(e % 2 + 1) * D], hT[e % 2][:, k, 0:n], w2[:, e, k, :],
                                    start=(k == 0), stop=(k == KH - 1))
                last.then_inc(w2_ok, 1)

        def cw_turn(u):
            pe.wait_ge(cw_ok, u + 1)
            t.transpose(cwt_ps, cw[:], ident[:]).then_inc(cwt_ok, 1)

        def b2_term(u):
            pe.wait_ge(cwT_ok, u + 1)
            t.matmul(b2_ps, cwT[:], b2s[:], start=True, stop=True).then_inc(b2_ok, 1)

        def sums(w, par):
            pe.wait_ge(folded, w * 3 + 3)
            for k in range(SLOTS):
                last = t.matmul(agg_ps[:, 0:AGG], ident[:], rows[par][:, k, 0:AGG], start=(k == 0),
                                stop=(k == SLOTS - 1))
            last.then_inc(agg_ok, 1)

        def window(w, par, half):
            ffn = not isinstance(w, int) or w > 0
            u = w - 1
            if ffn:
                z_turn(u)
                for p in range(2):
                    hidden(u, 2 * p)
                    hidden(u, 2 * p + 1)
                    second(u, p)
                cw_turn(u)
                hidden(u, 4)
                b2_term(u)
                hidden(u, 5)
                second(u, 2)
            sums(w, par)
            if ffn:
                hidden(u, 6)
                hidden(u, 7)
                second(u, 3)

        pe.wait_ge(const_in, 64)
        pe.wait_ge(w_in, 16 * NE)
        pe.wait_ge(w_in2, 16 * NE)
        windows(pe, window)
        u = W - 1
        z_turn(u)
        for p in range(PAIRS):
            hidden(u, 2 * p, LAST)
            hidden(u, 2 * p + 1, LAST)
            if p == 1:
                cw_turn(u)
            second(u, p, LAST)
            if p == 1:
                b2_term(u)


_INS = ['x', 'src', 'dst', 'edge_type_8', 'L0_gnn_conv_weights', 'L0_gnn_attn_l', 'L0_gnn_attn_r', 'L0_gnn_h_bias',
        'L0_ffn_gate_w', 'L0_ffn_gate_b', 'L0_ffn_W1', 'L0_ffn_b1', 'L0_ffn_W2', 'L0_ffn_b2']


def kernel(**inputs):
    import numpy as _np
    import concourse.bacc as _bacc
    from concourse import mybir as _mybir
    from concourse.bass_utils import run_bass_kernel_spmd as _run

    nc = _bacc.Bacc("TRN2", target_bir_lowering=False, num_devices=1)
    arrays, args = {}, []
    for name in _INS:
        a = _np.ascontiguousarray(inputs[name])
        arrays[f"in_{name}_dram"] = a
        args.append(nc.dram_tensor(f"in_{name}_dram", a.shape, _mybir.dt.from_np(a.dtype), kind="ExternalInput").ap())
    args.append(nc.dram_tensor("out_dram", (3750, 256), _mybir.dt.float32, kind="ExternalOutput").ap())
    build(nc, *args)
    r = _run(nc, [arrays], core_ids=[0])
    return r.results[0]["out_dram"]
```
